# Optimizing a Trainium2 kernel written in Bass

```python
import numpy as np
import jax
import jax.numpy as jnp

def _softmax(x, axis=-1):
    return jax.nn.softmax(x, axis=axis)

def _gelu(x):
    return jax.nn.gelu(x, approximate=True)

def _silu(x):
    return jax.nn.silu(x)

def _sigmoid(x):
    return jax.nn.sigmoid(x)

def _layernorm(x, axis=-1, eps=1e-05):
    m = jnp.mean(x, axis=axis, keepdims=True)
    v = jnp.var(x, axis=axis, keepdims=True)
    return (x - m) / jnp.sqrt(v + eps)

def _scatter_add(tgt, idx, src, axis=0):
    return tgt.at[idx].add(src)

def _segment_sum(src, seg, n):
    return jax.ops.segment_sum(src, seg, n)
kernel_name = 'mk_adj_preln_d4_adj_r2_84b8f7'

def setup_inputs(seed: int=0):
    np.random.seed(seed)
    _w = jnp.asarray

    def _rec_inputs():
        import jax
        import jax.numpy as jnp
        _gk = jax.random.key(seed)
        x = -0.0005207 + 1.001 * jax.random.normal(jax.random.fold_in(_gk, 1), (4096, 128), jnp.float32)
        _w = (1.0 + jnp.arange(4096, dtype=jnp.float32)) ** (-0.5)
        _w = _w / _w.mean()
        _pij = jnp.clip(0.000976562 * _w[:, None] * _w[None, :], 0.0, 1.0)
        _a = jax.random.uniform(jax.random.fold_in(_gk, 2), (4096, 4096)) < _pij
        _a = jnp.logical_or(_a, jnp.eye(4096, dtype=bool))
        _af = _a.astype(jnp.float32)
        _af = _af * jax.random.uniform(jax.random.fold_in(_gk, 3), (4096, 4096), jnp.float32, 0.05, 1)
        adj = _af
        return (x, adj)
    x, adj = _rec_inputs()

    def _L0_gnn_setup():
        import jax, jax.numpy as jnp
        import numpy as np
        N = 4096
        D = 128
        L = 3

        def _cxin_conv(x, a, eps, W, b):
            ax = a @ x
            h = ax + (1.0 + eps[0]) * ax
            for i in range(L):
                h = jax.nn.relu(h @ W[i].T + b[i])
            return h
        key = jax.random.key(seed)
        ks = jax.random.split(key, 8)
        s = 1.0 / np.sqrt(D)
        return {'x1': jax.random.normal(ks[0], (N, D), jnp.float32), 'x2': jax.random.normal(ks[1], (N, D), jnp.float32), 'G1': jax.random.uniform(ks[2], (N, N), jnp.float32), 'G2': jax.random.uniform(ks[3], (N, N), jnp.float32), 'eps1': jnp.zeros((1,), jnp.float32), 'eps2': jnp.zeros((1,), jnp.float32), 'W1': jax.random.normal(ks[4], (L, D, D), jnp.float32) * s, 'b1': jnp.zeros((L, D), jnp.float32), 'W2': jax.random.normal(ks[5], (L, D, D), jnp.float32) * s, 'b2': jnp.zeros((L, D), jnp.float32), 'Wm': jax.random.normal(ks[6], (D, 2 * D), jnp.float32) * (1.0 / np.sqrt(2 * D)), 'bm': jnp.zeros((D,), jnp.float32)}
    _L0_gnn_all = _L0_gnn_setup()
    _L0_gnn_in = {k: v for k, v in _L0_gnn_all.items() if k in ('x2', 'eps1', 'eps2', 'W1', 'b1', 'W2', 'b2', 'Wm', 'bm')}
    del _L0_gnn_all

    def _L1_gnn_setup():
        import jax, jax.numpy as jnp
        import numpy as np
        NEG_BIG = -9000000000000000.0
        ALPHA = 0.2
        key = jax.random.key(seed)
        k1, k2, k3, k4 = jax.random.split(key, 4)
        N, F_in, F_out = (4096, 128, 128)
        h = jax.random.normal(k1, (N, F_in), dtype=jnp.float32)
        adj = jax.random.randint(k2, (N, N), 0, 2).astype(jnp.float32)
        W = jax.random.normal(k3, (F_in, F_out), dtype=jnp.float32) * (1.414 / np.sqrt(F_in))
        a = jax.random.normal(k4, (2 * F_out, 1), dtype=jnp.float32) * (1.414 / np.sqrt(2 * F_out))
        return {'h': h, 'adj': adj, 'W': W, 'a': a}
    _L1_gnn_all = _L1_gnn_setup()
    _L1_gnn_in = {k: v for k, v in _L1_gnn_all.items() if k in ('W', 'a')}
    del _L1_gnn_all

    def _L2_gnn_setup():
        import jax, jax.numpy as jnp
        import numpy as np
        N, H, HEADS = (2048, 128, 3)
        ALPHA = 0.2
        NEG_INF = -9000000000000000.0

        def _sign_adj(key, n, density):
            k1, k2 = jax.random.split(key)
            mask = jax.random.uniform(k1, (n, n)) < density
            sign = jnp.where(jax.random.uniform(k2, (n, n)) < 0.5, -1.0, 1.0)
            adj = jnp.where(mask, sign, 0.0).astype(jnp.float32)
            idx = jnp.arange(n)
            return adj.at[idx, idx].set(1.0)

        def _gru_cell(x, hstate, Wih, Whh, bih, bhh):
            gi = x @ Wih.T + bih
            gh = hstate @ Whh.T + bhh
            ir, iz, inn = jnp.split(gi, 3, axis=1)
            hr, hz, hn = jnp.split(gh, 3, axis=1)
            r = jax.nn.sigmoid(ir + hr)
            z = jax.nn.sigmoid(iz + hz)
            n = jnp.tanh(inn + r * hn)
            return (1.0 - z) * n + z * hstate

        def _gat_head(h, node_adj, edge_adj, W, a):
            hW = h @ W
            hp = (node_adj > 0).astype(hW.dtype) @ hW
            hm = (node_adj < 0).astype(hW.dtype) @ hW
            e_plus = jax.nn.leaky_relu(jnp.concatenate([hp, hm], axis=1) @ a, ALPHA)[:, 0]
            e_minus = jax.nn.leaky_relu(jnp.concatenate([hm, hp], axis=1) @ a, ALPHA)[:, 0]
            att = jnp.where(edge_adj > 0, e_plus[None, :], NEG_INF)
            att = jnp.where(edge_adj < 0, e_minus[None, :], att)
            att = jax.nn.softmax(att, axis=1)
            return att * edge_adj @ hW
        key = jax.random.key(seed)
        ks = jax.random.split(key, 16)
        std = 0.01
        gain = 1.414
        return {'h': jax.random.normal(ks[0], (N, H), jnp.float32), 'node_adj': _sign_adj(ks[1], N, 0.005), 'edge_adj': _sign_adj(ks[2], N, 0.005), 'gat_W': jax.random.normal(ks[3], (HEADS, H, H), jnp.float32) * (gain / np.sqrt(H, dtype=np.float32)), 'gat_a': jax.random.normal(ks[4], (HEADS, 2 * H, 1), jnp.float32) * 0.1, 'edge_Wih': jax.random.normal(ks[5], (3 * H, H), jnp.float32) * std, 'edge_Whh': jax.random.normal(ks[6], (3 * H, H), jnp.float32) * std, 'edge_bih': jnp.zeros((3 * H,), jnp.float32), 'edge_bhh': jnp.zeros((3 * H,), jnp.float32), 'node_Wih': jax.random.normal(ks[7], (3 * H, H), jnp.float32) * std, 'node_Whh': jax.random.normal(ks[8], (3 * H, H), jnp.float32) * std, 'node_bih': jnp.zeros((3 * H,), jnp.float32), 'node_bhh': jnp.zeros((3 * H,), jnp.float32)}
    _L2_gnn_all = _L2_gnn_setup()
    _L2_gnn_in = {k: v for k, v in _L2_gnn_all.items() if k in ('gat_W', 'gat_a', 'edge_Wih', 'edge_Whh', 'edge_bih', 'edge_bhh', 'node_Wih', 'node_Whh', 'node_bih', 'node_bhh')}
    del _L2_gnn_all

    def _L3_gnn_setup():
        import jax, jax.numpy as jnp
        import numpy as np
        N = 3072
        HID = 128
        T = 350
        DENSITY = 0.05
        key = jax.random.key(seed)
        k1, k2, k3, k4, k5, k6 = jax.random.split(key, 6)
        h = jax.random.normal(k1, (N, HID), dtype=jnp.float32)
        a = jax.random.uniform(k2, (N, N), dtype=jnp.float32)
        mask = jax.random.uniform(k3, (N, N)) < DENSITY
        adj = jnp.where(mask, a, 0.0)
        simlar = jax.random.normal(k4, (N, N), dtype=jnp.float32)
        s = 1.0 / np.sqrt(HID)
        W_proj = jax.random.uniform(k5, (HID, HID), minval=-s, maxval=s, dtype=jnp.float32)
        b_proj = jnp.zeros((HID,), dtype=jnp.float32)
        W_gcn = jax.random.uniform(k6, (HID, HID), minval=-s, maxval=s, dtype=jnp.float32)
        b_gcn = jnp.zeros((HID,), dtype=jnp.float32)
        return {'h': h, 'adj': adj, 'simlar': simlar, 'W_proj': W_proj, 'b_proj': b_proj, 'W_gcn': W_gcn, 'b_gcn': b_gcn}
    _L3_gnn_all = _L3_gnn_setup()
    _L3_gnn_in = {k: v for k, v in _L3_gnn_all.items() if k in ('W_proj', 'b_proj', 'W_gcn', 'b_gcn')}
    del _L3_gnn_all
    return {'x': x, 'adj': adj, 'L0_gnn_x2': _L0_gnn_in['x2'], 'L0_gnn_eps1': _L0_gnn_in['eps1'], 'L0_gnn_eps2': _L0_gnn_in['eps2'], 'L0_gnn_W1': _L0_gnn_in['W1'], 'L0_gnn_b1': _L0_gnn_in['b1'], 'L0_gnn_W2': _L0_gnn_in['W2'], 'L0_gnn_b2': _L0_gnn_in['b2'], 'L0_gnn_Wm': _L0_gnn_in['Wm'], 'L0_gnn_bm': _L0_gnn_in['bm'], 'L1_gnn_W': _L1_gnn_in['W'], 'L1_gnn_a': _L1_gnn_in['a'], 'L2_gnn_gat_W': _L2_gnn_in['gat_W'], 'L2_gnn_gat_a': _L2_gnn_in['gat_a'], 'L2_gnn_edge_Wih': _L2_gnn_in['edge_Wih'], 'L2_gnn_edge_Whh': _L2_gnn_in['edge_Whh'], 'L2_gnn_edge_bih': _L2_gnn_in['edge_bih'], 'L2_gnn_edge_bhh': _L2_gnn_in['edge_bhh'], 'L2_gnn_node_Wih': _L2_gnn_in['node_Wih'], 'L2_gnn_node_Whh': _L2_gnn_in['node_Whh'], 'L2_gnn_node_bih': _L2_gnn_in['node_bih'], 'L2_gnn_node_bhh': _L2_gnn_in['node_bhh'], 'L3_gnn_W_proj': _L3_gnn_in['W_proj'], 'L3_gnn_b_proj': _L3_gnn_in['b_proj'], 'L3_gnn_W_gcn': _L3_gnn_in['W_gcn'], 'L3_gnn_b_gcn': _L3_gnn_in['b_gcn']}

def reference(x, adj, L0_gnn_x2, L0_gnn_eps1, L0_gnn_eps2, L0_gnn_W1, L0_gnn_b1, L0_gnn_W2, L0_gnn_b2, L0_gnn_Wm, L0_gnn_bm, L1_gnn_W, L1_gnn_a, L2_gnn_gat_W, L2_gnn_gat_a, L2_gnn_edge_Wih, L2_gnn_edge_Whh, L2_gnn_edge_bih, L2_gnn_edge_bhh, L2_gnn_node_Wih, L2_gnn_node_Whh, L2_gnn_node_bih, L2_gnn_node_bhh, L3_gnn_W_proj, L3_gnn_b_proj, L3_gnn_W_gcn, L3_gnn_b_gcn):
    import jax
    import jax.numpy as jnp

    def _L0_gnn_ref(x1, x2, G1, G2, eps1, eps2, W1, b1, W2, b2, Wm, bm):
        import jax, jax.numpy as jnp
        import numpy as np
        N = 4096
        D = 128
        L = 3

        def _cxin_conv(x, a, eps, W, b):
            ax = a @ x
            h = ax + (1.0 + eps[0]) * ax
            for i in range(L):
                h = jax.nn.relu(h @ W[i].T + b[i])
            return h
        out1 = _cxin_conv(x1, G1, eps1, W1, b1)
        out2 = _cxin_conv(x2, G2, eps2, W2, b2)
        merged = jnp.concatenate((out1, out2), axis=1)
        return merged @ Wm.T + bm

    def _L1_gnn_ref(h, adj, W, a):
        import jax, jax.numpy as jnp
        import numpy as np
        NEG_BIG = -9000000000000000.0
        ALPHA = 0.2
        F_out = W.shape[1]
        Wh = h @ W
        a1 = a[:F_out, 0]
        a2 = a[F_out:, 0]
        s1 = Wh @ a1
        s2 = Wh @ a2
        e = jax.nn.leaky_relu(s1[:, None] + s2[None, :], negative_slope=ALPHA)
        e = jnp.where(adj > 0, e, NEG_BIG)
        attention = jax.nn.softmax(e, axis=1)
        h_prime = attention @ Wh
        return jax.nn.elu(h_prime)

    def _L2_gnn_ref(h, node_adj, edge_adj, gat_W, gat_a, edge_Wih, edge_Whh, edge_bih, edge_bhh, node_Wih, node_Whh, node_bih, node_bhh):
        import jax, jax.numpy as jnp
        import numpy as np
        N, H, HEADS = (2048, 128, 3)
        ALPHA = 0.2
        NEG_INF = -9000000000000000.0

        def _sign_adj(key, n, density):
            k1, k2 = jax.random.split(key)
            mask = jax.random.uniform(k1, (n, n)) < density
            sign = jnp.where(jax.random.uniform(k2, (n, n)) < 0.5, -1.0, 1.0)
            adj = jnp.where(mask, sign, 0.0).astype(jnp.float32)
            idx = jnp.arange(n)
            return adj.at[idx, idx].set(1.0)

        def _gru_cell(x, hstate, Wih, Whh, bih, bhh):
            gi = x @ Wih.T + bih
            gh = hstate @ Whh.T + bhh
            ir, iz, inn = jnp.split(gi, 3, axis=1)
            hr, hz, hn = jnp.split(gh, 3, axis=1)
            r = jax.nn.sigmoid(ir + hr)
            z = jax.nn.sigmoid(iz + hz)
            n = jnp.tanh(inn + r * hn)
            return (1.0 - z) * n + z * hstate

        def _gat_head(h, node_adj, edge_adj, W, a):
            hW = h @ W
            hp = (node_adj > 0).astype(hW.dtype) @ hW
            hm = (node_adj < 0).astype(hW.dtype) @ hW
            e_plus = jax.nn.leaky_relu(jnp.concatenate([hp, hm], axis=1) @ a, ALPHA)[:, 0]
            e_minus = jax.nn.leaky_relu(jnp.concatenate([hm, hp], axis=1) @ a, ALPHA)[:, 0]
            att = jnp.where(edge_adj > 0, e_plus[None, :], NEG_INF)
            att = jnp.where(edge_adj < 0, e_minus[None, :], att)
            att = jax.nn.softmax(att, axis=1)
            return att * edge_adj @ hW
        dn = jnp.diag(node_adj)
        de = jnp.diag(edge_adj)
        idx = jnp.arange(node_adj.shape[0])
        node_adj_norm = node_adj.at[idx, idx].add(-dn)
        edge_adj_norm = edge_adj.at[idx, idx].add(-de)
        node_support = node_adj_norm @ h
        edge_output = _gru_cell(node_support, h, edge_Wih, edge_Whh, edge_bih, edge_bhh)
        edge_support = _gat_head(h, node_adj_norm, edge_adj_norm, gat_W[0], gat_a[0])
        for i in range(1, HEADS):
            edge_support = edge_support + _gat_head(h, node_adj_norm, edge_adj_norm, gat_W[i], gat_a[i])
        edge_support = edge_support / HEADS
        node_output = _gru_cell(edge_support, h, node_Wih, node_Whh, node_bih, node_bhh)
        return de[:, None] * edge_output + dn[:, None] * node_output

    def _L3_gnn_ref(h, adj, simlar, W_proj, b_proj, W_gcn, b_gcn):
        import jax, jax.numpy as jnp
        import numpy as np
        N = 3072
        HID = 128
        T = 350
        DENSITY = 0.05
        sim = jnp.tanh(adj * simlar)
        filt = sim * (adj > 0).astype(sim.dtype)
        vals, idx = jax.lax.top_k(filt, T)
        nnz = jnp.sum(filt != 0, axis=1)
        keep = jnp.arange(T)[None, :] < nnz[:, None]
        rows = jnp.arange(filt.shape[0])[:, None]
        new_adj = jnp.zeros_like(filt).at[rows, idx].set(jnp.where(keep, vals, 0.0))
        h2 = jnp.tanh(h @ W_proj + b_proj)
        feat = jax.nn.relu(new_adj @ (h2 @ W_gcn) + b_gcn)
        return feat
    h = jnp.maximum(_layernorm(x, axis=-1), 0.0)
    x = x + _L0_gnn_ref(h, L0_gnn_x2, adj, adj, L0_gnn_eps1, L0_gnn_eps2, L0_gnn_W1, L0_gnn_b1, L0_gnn_W2, L0_gnn_b2, L0_gnn_Wm, L0_gnn_bm)
    h = jnp.maximum(_layernorm(x, axis=-1), 0.0)
    x = x + _L1_gnn_ref(h, adj, L1_gnn_W, L1_gnn_a)
    h = jnp.maximum(_layernorm(x, axis=-1), 0.0)
    x = x + _L2_gnn_ref(h, adj, adj, L2_gnn_gat_W, L2_gnn_gat_a, L2_gnn_edge_Wih, L2_gnn_edge_Whh, L2_gnn_edge_bih, L2_gnn_edge_bhh, L2_gnn_node_Wih, L2_gnn_node_Whh, L2_gnn_node_bih, L2_gnn_node_bhh)
    h = jnp.maximum(_layernorm(x, axis=-1), 0.0)
    x = x + _L3_gnn_ref(h, adj, adj, L3_gnn_W_proj, L3_gnn_b_proj, L3_gnn_W_gcn, L3_gnn_b_gcn)
    return x

_drawn_inputs = setup_inputs


def setup_inputs(seed=0):
    import zlib

    import numpy as np

    out = dict(_drawn_inputs(seed))
    spreads = {'L0_gnn_b1': (0.0, 0.1),
     'L0_gnn_b2': (0.0, 0.1),
     'L0_gnn_bm': (0.0, 0.1),
     'L2_gnn_edge_bih': (0.0, 0.48),
     'L2_gnn_edge_bhh': (0.0, 0.8),
     'L2_gnn_node_bih': (0.0, 0.56),
     'L2_gnn_node_bhh': (0.0, 0.8),
     'L3_gnn_b_proj': (0.0, 0.1),
     'L3_gnn_b_gcn': (0.0, 0.1)}
    factors = {'L2_gnn_gat_W': 8.0,
     'L2_gnn_gat_a': 8.0,
     'L2_gnn_edge_Whh': 7.516,
     'L2_gnn_node_Wih': 8.0,
     'L2_gnn_node_Whh': 7.456}
    for name, (base, spread) in spreads.items():
        noise = np.random.default_rng([zlib.crc32(name.encode()), seed]).standard_normal(out[name].shape)
        drawn = base * np.exp(spread * noise) if base else spread * noise
        out[name] = jnp.asarray(drawn.astype(out[name].dtype))
    for name, factor in factors.items():
        out[name] = (out[name] * factor).astype(out[name].dtype)
    return out
```

```python
from contextlib import ExitStack, contextmanager

import concourse.bass as bass
from concourse import mybir

F32 = mybir.dt.float32
BF16 = mybir.dt.bfloat16
I32 = mybir.dt.int32
U32 = mybir.dt.uint32
ALU = mybir.AluOpType
ACT = mybir.ActivationFunctionType
AX = mybir.AxisListType

N = 4096
D = 128
P = 128
T = N // P
CLASSES = 8
QUARTERS = 4
SIDES = 2
JJ = N // CLASSES
PAIR = 2
TAKEN = PAIR * P // CLASSES
MAX_PAIRS = JJ // TAKEN
CAP = T * MAX_PAIRS
SETS = 4
HEADS = 3
GROUP = 4
GROUPS = T // GROUP
WIDE = GROUP * P
ALPHA = 0.2
EPS = 1e-5
BIG = 1e30
TOPK = 350
BLOCKS = N // P
STEPS, ROUNDS, NEGATIVES, CROWDED = range(4)


UV_END = D + 2 * HEADS + 1
SIGN_W = UV_END - D
SUPPORT_W = D + 2 * SIGN_W
HEAD_W = HEADS * (D + 1)


class Space:
    pass


class Stage(ExitStack):

    def __init__(self, nc):
        super().__init__()
        self.nc, self.sems = nc, []

    def sem(self, name):
        self.sems.append(self.nc.alloc_semaphore(name=name))
        return self.sems[-1]

    def __exit__(self, *exc):
        if exc[0] is None:
            self.nc.clear_and_free_semaphores(self.sems)
            self.nc.all_engine_barrier()
        return super().__exit__(*exc)


def runs(nc, eng, m):
    return eng.value_load(m.meta[0:1, STEPS:STEPS + 1], min_val=1, max_val=CAP // SETS)


@contextmanager
def where(eng, m, flag):
    if flag is None:
        yield
        return
    with eng.If(eng.value_load(m.meta[0:1, flag:flag + 1], min_val=0, max_val=1) > 0):
        yield
        eng.nop(nofuse=True)


def tiles_of_step(nc, eng, m, step):
    word = eng.value_load(m.tiles[0:1, bass.ds(step, 1)], min_val=0, max_val=(1 << 24) - 1)
    return [nc.s_assert_within(eng.snap((word >> (6 * s)) & 63), 0, T,
                               skip_runtime_bounds_check_because="the table holds 0 to T") for s in range(SETS)]


def stage_weights(nc, m, a):
    with Stage(nc) as ctx:
        loaded = ctx.sem("w_loaded")
        identity_step = ctx.sem("w_identity_step")
        folded = ctx.sem("w_folded")
        vec = ctx.sem("w_vector")
        copied = ctx.sem("w_copied")
        ps = ctx.enter_context(nc.psum_tensor("w_ps", [P, 8], F32))
        loads = [
            (m.x, a["x"].rearrange("(t p) d -> p t d", p=P)),
            (m.w0, a["L0_WT"].rearrange("b l i o -> i (b l) o")),
            (m.wm, a["L0_WmT"].rearrange("(b i) o -> i b o", b=2)),
            (m.b0, a["L0_bT"].rearrange("b l d -> d (b l)")),
            (m.bm, a["L0_gnn_bm"].rearrange("(a d) -> a d", a=1)),
            (m.eps[:, 0:1], a["L0_gnn_eps1"].rearrange("(a d) -> a d", a=1).broadcast_to([P, 1])),
            (m.eps[:, 1:2], a["L0_gnn_eps2"].rearrange("(a d) -> a d", a=1).broadcast_to([P, 1])),
            (m.w1[:, 0:D], a["L1_gnn_W"]),
            (m.w1t, a["L1_WT"]),
            (m.a1, a["L1_gnn_a"].rearrange("(s d) o -> d (s o)", s=2)),
            (m.w2, a["L2_gnn_gat_W"].rearrange("k i o -> i k o")),
            (m.w2t, a["L2_WT"].rearrange("k o i -> o k i")),
            (m.a2, a["L2_gnn_gat_a"].rearrange("k (s d) o -> d k (s o)", s=2)),
            (m.wih, a["L2_WihT"].rearrange("g i o -> i g o")),
            (m.whh, a["L2_WhhT"].rearrange("g i o -> i g o")),
            (m.bih, a["L2_bih"].rearrange("g (c d) -> d g c", d=D)),
            (m.bhh, a["L2_bhh"].rearrange("g (c d) -> d g c", d=D)),
            (m.wp, a["L3_gnn_W_proj"]),
            (m.bp, a["L3_gnn_b_proj"].rearrange("(d a) -> d a", a=1)),
            (m.wg, a["L3_gnn_W_gcn"]),
            (m.bg, a["L3_gnn_b_gcn"].rearrange("(a d) -> a d", a=1).broadcast_to([P, D])),
            (m.diagonal, a["adj_diagonal"]),
            (a["table0"][:, D:2 * D], a["L0_gnn_x2"]),
        ]
        with nc.Block() as block:
            @block.sync
            def _(sp):
                with nc.allow_non_contiguous_dma(reason="biases and the diagonal, once"):
                    for dst, src in loads:
                        sp.dma_start(dst if isinstance(dst, bass.AP) else dst[:], src).then_inc(loaded, 16)
                sp.wait_ge(loaded, 16 * len(loads))

            @block.gpsimd
            def _(pool):
                nc.gpsimd.memset(m.ident[:], 0.0).then_inc(identity_step, 1)
                pool.wait_ge(identity_step, 1)
                nc.gpsimd.affine_select(out=m.ident[:], in_=m.ident[:], compare_op=ALU.not_equal, fill=1.0,
                                        base=0, pattern=[[-1, P]], channel_multiplier=1).then_inc(identity_step, 1)
                nc.gpsimd.memset(m.identb[:], 0.0).then_inc(identity_step, 1)
                pool.wait_ge(identity_step, 3)
                nc.gpsimd.affine_select(out=m.identb[:], in_=m.identb[:], compare_op=ALU.not_equal, fill=1.0,
                                        base=0, pattern=[[-1, P]], channel_multiplier=1).then_inc(identity_step, 1)

            @block.tensor
            def _(pe):
                pe.wait_ge(loaded, 16 * len(loads))
                nc.tensor.matmul(ps[:, 0:2], m.w1t[:], m.a1[:], start=True, stop=True)
                for k in range(HEADS):
                    last = nc.tensor.matmul(ps[:, 2 + 2 * k:4 + 2 * k], m.w2t[:, k, :], m.a2[:, k, :],
                                            start=True, stop=True)
                last.then_inc(folded, 1)

            @block.vector
            def _(dve):
                nc.vector.memset(m.ones[:], 1.0).then_inc(vec, 1)
                dve.wait_ge(loaded, 16 * len(loads))
                dve.wait_ge(folded, 1)
                nc.vector.tensor_copy(m.w1[:, D:D + 1], ps[:, 1:2]).then_inc(vec, 1)
                nc.vector.tensor_copy(m.uv[:], ps[:, 2:8]).then_inc(vec, 1)
                nc.vector.tensor_copy(m.wa1[:], ps[:, 0:1]).then_inc(copied, 1)
                dve.wait_ge(vec, 3)
                dve.wait_ge(copied, 1)
                nc.vector.tensor_scalar(m.wa1_wide[:], m.ones[:], m.wa1[:, 0:1], None, ALU.mult).then_inc(vec, 1)
                nc.vector.tensor_scalar(m.eps[:], m.eps[:], 2.0, None, ALU.add).then_inc(vec, 1)
                nc.vector.tensor_tensor(m.bsum[:], m.bih[:], m.bhh[:], ALU.add).then_inc(vec, 1)


def stage_scan(nc, m, a):
    with Stage(nc) as ctx:
        ring = [m.acc[:, b * N:(b + 1) * N] for b in range(3)] + [m.shift2[:, 0:N]]
        loaded = [ctx.sem(f"scan_loaded{i}") for i in range(4)]
        reduced = [ctx.sem(f"scan_reduced{i}") for i in range(4)]
        src = a["adjT"].rearrange("(part p c) i -> c part p i", part=4, c=CLASSES)
        with nc.Block() as block:
            @block.sync
            def _(sp):
                with sp.Fori(0, CLASSES) as c:
                    for part in range(4):
                        sp.wait_ge(reduced[part], c)
                        sp.dma_start(ring[part], src[bass.ds(c, 1), part, :, :].rearrange("c p i -> p (c i)")
                                     ).then_inc(loaded[part], 16)

            @block.vector
            def _(dve):
                with dve.Fori(0, CLASSES) as c:
                    for part in range(4):
                        dve.wait_ge(loaded[part], 16 * c + 16)
                        nc.vector.tensor_reduce(
                            m.active[:, part, bass.ds(c, 1), :], ring[part].rearrange("p (t i) -> p t i", i=P),
                            AX.X, ALU.max, apply_absolute_value=True).then_inc(reduced[part], 1)


def stage_index(nc, m, a):
    with Stage(nc) as ctx:
        def sb(name, shape, dt=F32):
            return ctx.enter_context(nc.sbuf_tensor("ix_" + name, shape, dt))

        def sem(name):
            return ctx.sem("ix_" + name)

        flags = sb("flags", [P, 4, SIDES, P], BF16)
        ramp = sb("ramp", [P, SIDES, JJ])
        keys = sb("keys", [P, SIDES, JJ])
        step32 = sb("step32", [P, MAX_PAIRS])
        counts = sb("counts", [P, SIDES])
        most = sb("most", [P, 1])
        over = sb("over", [P, MAX_PAIRS])
        pairs_of_list = sb("pairs_of_list", [P, 1])
        pairs = sb("pairs", [1, T])
        ends = sb("ends", [1, 2, T])
        starts = sb("starts", [1, T])
        starts_i = sb("starts_i", [1, T], I32)
        step4 = sb("step4", [1, CAP // SETS])
        over4 = sb("over4", [1, CAP // SETS])
        meta_f = sb("meta_f", [1, 2])
        ends_col = sb("ends_col", [T, 1])
        pair_ramp = sb("pair_ramp", [T, CAP])
        passed = sb("passed", [T, CAP])
        packed = sb("packed", [1, CAP // SETS])
        taken = sb("taken", [P, PAIR, SIDES, TAKEN // PAIR])
        turned = sb("turned", [P, PAIR, SIDES * TAKEN // PAIR])
        lists = sb("lists", [P, MAX_PAIRS * PAIR, T])
        high = sb("high", [P, MAX_PAIRS * PAIR, T])
        tile_ramp = sb("tile_ramp", [P, MAX_PAIRS * PAIR, T])
        offset = sb("offset", [P, 1])
        ps_keys = ctx.enter_context(nc.psum_tensor("ix_ps_keys", [P, SIDES, JJ], F32))
        ps_small = ctx.enter_context(nc.psum_tensor("ix_ps_small", [P, 512], F32))
        ps_tiles = ctx.enter_context(nc.psum_tensor("ix_ps_tiles", [P, CAP], F32))
        pool_step, flagged, keyed, listed, row, col, col_done, tiled, dv = (
            sem(x) for x in ("pool_step", "flagged", "keyed", "listed", "row", "col", "col_done", "tiled", "dve_step"))
        took = sem("took")
        copied = sem("copied")

        with nc.Block() as block:
            @block.gpsimd
            def _(pool):
                nc.gpsimd.iota(ramp[:], pattern=[[0, SIDES], [-1, JJ]], base=JJ - 1, channel_multiplier=0,
                               allow_small_or_imprecise_dtypes=True).then_inc(pool_step, 1)
                nc.gpsimd.iota(step32[:], pattern=[[TAKEN, MAX_PAIRS]], base=0, channel_multiplier=0,
                               allow_small_or_imprecise_dtypes=True).then_inc(pool_step, 1)
                nc.gpsimd.iota(step4[:], pattern=[[SETS, CAP // SETS]], base=0, channel_multiplier=0,
                               allow_small_or_imprecise_dtypes=True).then_inc(pool_step, 1)
                nc.gpsimd.iota(pair_ramp[:], pattern=[[1, CAP]], base=0, channel_multiplier=0,
                               allow_small_or_imprecise_dtypes=True).then_inc(pool_step, 1)
                nc.gpsimd.iota(tile_ramp[:], pattern=[[0, MAX_PAIRS * PAIR], [1, T]], base=0, channel_multiplier=0,
                               allow_small_or_imprecise_dtypes=True).then_inc(pool_step, 1)
                nc.gpsimd.iota(m.row_ramp[:], pattern=[[1, P]], base=0, channel_multiplier=0,
                               allow_small_or_imprecise_dtypes=True).then_inc(pool_step, 1)
                nc.gpsimd.iota(m.class_of[:], pattern=[[0, 1]], base=0, channel_multiplier=1,
                               allow_small_or_imprecise_dtypes=True).then_inc(pool_step, 1)
                nc.gpsimd.iota(m.sixteens[:], pattern=[[16, CLASSES - 1]], base=16, channel_multiplier=0,
                               allow_small_or_imprecise_dtypes=True).then_inc(pool_step, 1)

            @block.tensor
            def _(pe):
                pe.wait_ge(flagged, 1)
                for side in range(SIDES):
                    for part in range(4):
                        last = nc.tensor.matmul(ps_keys[:, side, part * P:(part + 1) * P], flags[:, part, side, :],
                                                m.identb[:], start=True, stop=True)
                last.then_inc(keyed, 1)
                pe.wait_ge(listed, 1)
                nc.tensor.matmul(ps_small[0:1, 0:P], pairs_of_list[:], m.ident[:], start=True, stop=True).then_inc(row, 1)
                pe.wait_ge(col, 1)
                nc.tensor.matmul(ps_small[0:T, 128:129], ends[:, 1, :], m.ones[0:1, 0:1], start=True,
                                 stop=True).then_inc(col_done, 1)
                pe.wait_ge(tiled, 1)
                nc.tensor.matmul(ps_tiles[0:1, :], m.ones[0:T, 0:1], passed[:], start=True, stop=True).then_inc(tiled, 1)

            @block.vector
            def _(dve):
                steps = [0]

                def done(ins):
                    steps[0] += 1
                    ins.then_inc(dv, 1)
                    dve.wait_ge(dv, steps[0])

                dve.wait_ge(pool_step, 8)
                done(nc.vector.tensor_scalar(m.class_over[:], m.sixteens[:], m.class_of[:, 0:1], None, ALU.is_le))
                done(nc.vector.tensor_reduce(m.class_of[:], m.class_over[:], AX.X, ALU.add))
                by_side = m.active[:].rearrange("p a (q s) t -> p a s q t", s=SIDES)
                for side in range(SIDES):
                    last = nc.vector.tensor_scalar(
                        flags[:, :, side, :].rearrange("p a (q t) -> p a q t", q=QUARTERS), by_side[:, :, side, :, :],
                        0.0, None, ALU.is_gt)
                last.then_inc(flagged, 1)
                dve.wait_ge(keyed, 1)
                done(nc.vector.scalar_tensor_tensor(out=keys[:], in0=ps_keys[:], scalar=2.0 * JJ, in1=ramp[:],
                                                    op0=ALU.mult, op1=ALU.add))
                done(nc.vector.tensor_reduce(counts[:], ps_keys[:], AX.X, ALU.add))
                done(nc.vector.tensor_reduce(most[:], counts[:], AX.X, ALU.max))
                done(nc.vector.tensor_scalar(over[:], step32[:], most[:, 0:1], None, ALU.is_lt))
                nc.vector.tensor_reduce(pairs_of_list[:], over[:], AX.X, ALU.add).then_inc(listed, 1)
                dve.wait_ge(row, 1)
                done(nc.vector.tensor_reduce(pairs[:], ps_small[0:1, 0:P].rearrange("o (q t) -> o t q", q=QUARTERS),
                                             AX.X, ALU.max))
                done(nc.vector.tensor_scalar(pairs[:], pairs[:], 1.0, None, ALU.max))
                done(nc.vector.tensor_reduce(meta_f[:, 1:2], pairs[:], AX.X, ALU.max))
                done(nc.vector.tensor_copy(ends[:, 0, :], pairs[:]))
                src = 0
                for shift in (1, 2, 4, 8, 16):
                    dst = 1 - src
                    done(nc.vector.tensor_copy(ends[:, dst, 0:shift], ends[:, src, 0:shift]))
                    done(nc.vector.tensor_tensor(ends[:, dst, shift:T], ends[:, src, shift:T],
                                                 ends[:, src, 0:T - shift], ALU.add))
                    src = dst
                nc.vector.tensor_tensor(starts[:], ends[:, 1, :], pairs[:], ALU.subtract).then_inc(col, 1)
                dve.wait_ge(col, 1)
                done(nc.vector.tensor_copy(starts_i[:], starts[:]))
                done(nc.vector.tensor_scalar(over4[:], step4[:], ends[:, 1, T - 1:T], None, ALU.is_lt))
                done(nc.vector.tensor_reduce(meta_f[:, 0:1], over4[:], AX.X, ALU.add))
                done(nc.vector.tensor_copy(m.meta[:, 0:2], meta_f[:]))
                dve.wait_ge(col_done, 1)
                done(nc.vector.tensor_copy(ends_col[:], ps_small[0:T, 128:129]))
                nc.vector.tensor_scalar(passed[:], pair_ramp[:], ends_col[:, 0:1], None, ALU.is_ge).then_inc(tiled, 1)
                dve.wait_ge(tiled, 2)
                by_set = ps_tiles[0:1, :].rearrange("o (n s) -> o s n", s=SETS)
                done(nc.vector.tensor_copy(packed[:], by_set[:, 0, :]))
                for s in range(1, SETS):
                    done(nc.vector.scalar_tensor_tensor(out=packed[:], in0=by_set[:, s, :], scalar=float(64 ** s),
                                                        in1=packed[:], op0=ALU.mult, op1=ALU.add))
                done(nc.vector.tensor_copy(m.tiles[:], packed[:]))
                done(nc.vector.memset(lists[:], 0.0))
                half = TAKEN // PAIR
                rounds = dve.value_load(m.meta[0:1, ROUNDS:ROUNDS + 1], min_val=1, max_val=MAX_PAIRS)
                per_round = 2 * PAIR * SIDES * (half // 8) + 1
                with dve.Fori(0, rounds) as r:
                    k = 0
                    for part in range(TAKEN // 8):
                        h, e = divmod(part * 8, half)
                        for side in range(SIDES):
                            nc.vector.max(out=taken[:, h, side, e:e + 8], in_=keys[:, side, :]).then_inc(took, 1)
                        k += SIDES
                        dve.wait_ge(took, r * per_round + k)
                        dve.nop(nofuse=True)
                        for side in range(SIDES):
                            nc.vector.match_replace(out=keys[:, side, :], in_to_replace=taken[:, h, side, e:e + 8],
                                                    in_values=keys[:, side, :], imm_value=-1.0).then_inc(took, 1)
                        k += SIDES
                        dve.wait_ge(took, r * per_round + k)
                        dve.nop(nofuse=True)
                    for h in range(PAIR):
                        last = nc.vector.transpose(turned[:, h, :], taken[:, h, :, :].rearrange("p s e -> p (s e)"))
                    last.then_inc(took, 1)
                    dve.wait_ge(took, r * per_round + k + 1)
                    nc.vector.tensor_copy(lists[:, bass.ds(r * PAIR, PAIR), :], turned[:]).then_inc(copied, 1)
                    dve.wait_ge(copied, r + 1)
                flat = lists[:]
                done(nc.vector.tensor_scalar(high[:], flat, 2.0 * JJ, -2.0 * JJ, ALU.is_ge, ALU.mult))
                done(nc.vector.tensor_tensor(flat, flat, high[:], ALU.add))
                done(nc.vector.tensor_scalar(offset[:], m.class_of[:], float(CLASSES * (JJ - 1)), None, ALU.add))
                done(nc.vector.tensor_scalar(flat, flat, -float(CLASSES), offset[:, 0:1], ALU.mult, ALU.add))
                done(nc.vector.scalar_tensor_tensor(out=high[:], in0=flat, scalar=float(T), in1=tile_ramp[:],
                                                    op0=ALU.mult, op1=ALU.add))
                done(nc.vector.scalar_tensor_tensor(out=tile_ramp[:], in0=tile_ramp[:], scalar=-float(P), in1=flat,
                                                    op0=ALU.mult, op1=ALU.add))
                done(nc.vector.memset(m.index[:], 0))
                done(nc.vector.memset(m.relative[:], 0.0))
                base = steps[0]
                with dve.Fori(0, T) as t:
                    start = dve.value_load(starts_i[0:1, bass.ds(t, 1)], min_val=0, max_val=CAP - 1)
                    length = MAX_PAIRS * PAIR
                    for kind, what in ((0, high), (1, flat)):
                        nc.vector.tensor_copy(
                            m.index[:, bass.ds(start * PAIR, length), kind:kind + 1],
                            what[:, :, bass.ds(t, 1)]).then_inc(dv, 1)
                    nc.vector.tensor_copy(m.relative[:, bass.ds(start * PAIR, length)],
                                          tile_ramp[:, :, bass.ds(t, 1)].rearrange("p l o -> p (l o)")).then_inc(dv, 1)
                    dve.wait_ge(dv, t * 3 + (base + 3))


def stage_norm(nc, m, a, layer):
    with Stage(nc) as ctx:
        def sb(name, shape, dt=F32):
            return [ctx.enter_context(nc.sbuf_tensor(f"n{layer}_{name}{u}", shape, dt)) for u in range(2)]

        def sem(name):
            return [ctx.sem(f"n{layer}_{name}{u}") for u in range(2)]

        width = {0: D, 1: D + 2, 2: UV_END, 3: D}[layer]
        stats = sb("stats", [P, GROUP, nc.vector.BN_STATS_DIM])
        moments = sb("moments", [P, GROUP, nc.vector.BN_AGGR_DIM])
        root = sb("root", [P, GROUP])
        scale = sb("scale", [P, GROUP])
        shift = sb("shift", [P, GROUP])
        rows = sb("rows", [P, GROUP, width])
        hrow = sb("hrow", [P, GROUP, D]) if layer in (1, 3) else rows
        hT = sb("hT", [P, WIDE])
        h2T = sb("h2T", [P, WIDE]) if layer == 3 else None
        ps_t = [ctx.enter_context(nc.psum_tensor(f"n{layer}_ps_t{u}", [P, WIDE], F32)) for u in range(2)]
        ps_w = [ctx.enter_context(nc.psum_tensor(f"n{layer}_ps_w{u}", [P, GROUP, 256 if layer == 1 else 128], F32))
                for u in range(2)]
        ps_s = ([ctx.enter_context(nc.psum_tensor(f"n{layer}_ps_s{u}", [P, WIDE], F32)) for u in range(2)]
                if layer in (1, 3) else None)
        ones_set = ctx.sem(f"n{layer}_ones_set")
        dv, rooted, scaled, normed, turned, hT_ready, projected, rows_ready, stored, s_done, s_read, h2_ready = (
            sem(x) for x in ("dve", "rooted", "scaled", "normed", "turned", "hT_ready", "projected", "rows_ready",
                             "stored", "s_done", "s_read", "h2_ready"))
        table = {0: "table0", 1: "table1", 2: "table2", 3: "table3"}[layer]
        dst = a[table].rearrange("(t p) w -> p t w", p=P)
        steps = GROUPS // 2

        acc_clear = m.acc[:]

        def tiles(tensor, it, u):
            return tensor[:, bass.ds(it * (2 * GROUP) + u * GROUP, GROUP), :]

        with nc.Block() as block:
            @block.gpsimd
            def _(pool):
                nc.gpsimd.memset(acc_clear, 0.0)

            @block.vector
            def _(dve):
                if layer in (1, 2):
                    for u in range(2):
                        one = D if layer == 1 else UV_END - 1
                        nc.vector.memset(rows[u][:, :, one:one + 1], 1.0).then_inc(ones_set, 1)
                    dve.wait_ge(ones_set, 2)
                with dve.Fori(0, steps) as it:
                    def finish(u, it):
                        if layer == 0:
                            return
                        dve.wait_ge(projected[u], it + 1)
                        if layer in (1, 3):
                            dve.wait_ge(stored[u], 16 * it)
                        if layer == 1:
                            nc.vector.tensor_copy(rows[u][:, :, 0:D], ps_w[u][:, :, 0:D]).then_inc(rows_ready[u], 1)
                            nc.vector.tensor_copy(rows[u][:, :, D + 1:D + 2], ps_w[u][:, :, D:D + 1]).then_inc(
                                rows_ready[u], 1)
                            nc.vector.tensor_reduce(m.hsum[:, bass.ds(it * 2 + u, 1)], hT[u][:], AX.X, ALU.add
                                                    ).then_inc(rows_ready[u], 1)
                        elif layer == 2:
                            nc.vector.tensor_copy(rows[u][:, :, D:D + 2 * HEADS], ps_w[u][:, :, 0:2 * HEADS]).then_inc(
                                rows_ready[u], 1)
                        else:
                            nc.vector.tensor_copy(rows[u][:], ps_w[u][:]).then_inc(rows_ready[u], 1)

                    own = 4
                    for u in range(2):
                        dve.wait_ge(normed[u], it)
                        for i in range(GROUP):
                            last = nc.vector.bn_stats(stats[u][:, i, :], m.x[:, bass.ds(it * (2 * GROUP) + u * GROUP + i, 1), :]
                                                      .rearrange("p o d -> p (o d)"))
                        last.then_inc(dv[u], 1)
                        dve.wait_ge(dv[u], it * own + 1)
                        dve.nop(nofuse=True)
                        for i in range(GROUP):
                            last = nc.vector.bn_aggr(moments[u][:, i, :], stats[u][:, i, :])
                        last.then_inc(dv[u], 1)
                        dve.wait_ge(dv[u], it * own + 2)
                        nc.vector.tensor_scalar(scale[u][:], moments[u][:, :, 1], EPS, None, ALU.add).then_inc(dv[u], 1)
                        dve.wait_ge(rooted[u], it + 1)
                        nc.vector.reciprocal(scale[u][:], root[u][:]).then_inc(dv[u], 1)
                        dve.wait_ge(dv[u], it * own + 4)
                        nc.vector.scalar_tensor_tensor(out=shift[u][:], in0=moments[u][:, :, 0], scalar=-1.0,
                                                       in1=scale[u][:], op0=ALU.mult, op1=ALU.mult).then_inc(scaled[u], 1)
                        if u:
                            finish(0, it)
                    finish(1, it)

            @block.scalar
            def _(act):
                with act.Fori(0, steps) as it:
                    def root_of(u):
                        act.wait_ge(dv[u], it * 4 + 3)
                        nc.scalar.activation(root[u][:], scale[u][:], ACT.Sqrt).then_inc(rooted[u], 1)

                    def norm(u):
                        act.wait_ge(scaled[u], it + 1)
                        if layer in (0, 2):
                            act.wait_ge(stored[u], 16 * it)
                        if layer:
                            act.wait_ge(turned[u], it)
                        for i in range(GROUP):
                            last = nc.scalar.activation(
                                hrow[u][:, i, 0:D],
                                m.x[:, bass.ds(it * (2 * GROUP) + u * GROUP + i, 1), :].rearrange("p o d -> p (o d)"),
                                ACT.Relu, bias=shift[u][:, i:i + 1], scale=scale[u][:, i:i + 1])
                        last.then_inc(normed[u], 1)

                    def turn(u):
                        act.wait_ge(turned[u], it + 1)
                        if layer:
                            act.wait_ge(projected[u], it)
                        if layer == 1:
                            act.wait_ge(s_done[u], it)
                            act.wait_ge(rows_ready[u], 3 * it)
                        nc.scalar.copy(hT[u][:], ps_t[u][:]).then_inc(hT_ready[u], 1)
                        if layer == 2:
                            nc.scalar.copy(m.hT[:, bass.ds(it * (2 * WIDE) + u * WIDE, WIDE)], ps_t[u][:]).then_inc(
                                hT_ready[u], 1)
                        if layer == 1:
                            act.wait_ge(s_done[u], it + 1)
                            nc.scalar.copy(m.s1_wide[:, bass.ds(it * (2 * WIDE) + u * WIDE, WIDE)], ps_s[u][:]).then_inc(
                                s_read[u], 1)
                        if layer == 3:
                            act.wait_ge(s_done[u], it + 1)
                            nc.scalar.activation(h2T[u][:], ps_s[u][:], ACT.Tanh, bias=m.bp[:, 0:1]).then_inc(
                                h2_ready[u], 1)

                    root_of(0)
                    norm(0)
                    root_of(1)
                    norm(1)
                    if layer:
                        turn(0)
                        turn(1)

            @block.tensor
            def _(pe):
                if layer == 0:
                    return
                with pe.Fori(0, steps) as it:
                    for u in range(2):
                        pe.wait_ge(normed[u], it + 1)
                        pe.wait_ge(hT_ready[u], (2 if layer == 2 else 1) * it)
                        for i in range(GROUP):
                            last = nc.tensor.transpose(ps_t[u][:, i * P:(i + 1) * P], hrow[u][:, i, 0:D], m.ident[:])
                        last.then_inc(turned[u], 1)
                    for u in range(2):
                        pe.wait_ge(hT_ready[u], (2 if layer == 2 else 1) * it + 1)
                        if layer == 1:
                            pe.wait_ge(s_read[u], it)
                            nc.tensor.matmul(ps_s[u][:], m.wa1_wide[:], hT[u][:], start=True, stop=True).then_inc(
                                s_done[u], 1)
                            pe.wait_ge(rows_ready[u], 3 * it)
                            for i in range(GROUP):
                                last = nc.tensor.matmul(ps_w[u][:, i, 0:D + 1], hT[u][:, i * P:(i + 1) * P], m.w1[:],
                                                        start=True, stop=True)
                        elif layer == 2:
                            pe.wait_ge(rows_ready[u], it)
                            for i in range(GROUP):
                                last = nc.tensor.matmul(ps_w[u][:, i, 0:2 * HEADS], hT[u][:, i * P:(i + 1) * P],
                                                        m.uv[:], start=True, stop=True)
                        else:
                            pe.wait_ge(h2_ready[u], it)
                            nc.tensor.matmul(ps_s[u][:], m.wp[:], hT[u][:], start=True, stop=True).then_inc(
                                s_done[u], 1)
                            pe.wait_ge(h2_ready[u], it + 1)
                            pe.wait_ge(rows_ready[u], it)
                            for i in range(GROUP):
                                last = nc.tensor.matmul(ps_w[u][:, i, :], h2T[u][:, i * P:(i + 1) * P], m.wg[:],
                                                        start=True, stop=True)
                        last.then_inc(projected[u], 1)

            @block.sync
            def _(sp):
                with sp.Fori(0, steps) as it:
                    for u in range(2):
                        if layer == 0:
                            sp.wait_ge(normed[u], it + 1)
                        else:
                            sp.wait_ge(rows_ready[u], (it + 1) * (3 if layer == 1 else 1))
                        sp.dma_start(tiles(dst, it, u)[:, :, 0:width], rows[u][:]).then_inc(stored[u], 16)
                for u in range(2):
                    sp.wait_ge(stored[u], 16 * steps)


class Walk:

    def __init__(self, nc, m, a, name, ctx):
        self.nc, self.m, self.a, self.name, self.ctx = nc, m, a, name, ctx

    def sb(self, name, shape, dt=F32, sets=SETS):
        return [self.ctx.enter_context(self.nc.sbuf_tensor(f"{self.name}_{name}{s}", shape, dt)) for s in range(sets)]

    def ps(self, name, shape, sets=SETS):
        return [self.ctx.enter_context(self.nc.psum_tensor(f"{self.name}_{name}{s}", shape, F32)) for s in range(sets)]

    def sem(self, name, sets=SETS):
        return [self.ctx.sem(f"{self.name}_{name}{s}") for s in range(sets)]


def pair_of(tensor, it, s):
    return tensor[:, bass.ds(it * SETS + s, 1), :].rearrange("p o w -> p (o w)")


def stage_gin_pairs(nc, m, a):
    with Stage(nc) as ctx:
        w = Walk(nc, m, a, "g0", ctx)
        index = w.sb("index", [P, PAIR, 2], U32)
        adj = w.sb("adj", [P, PAIR, P])
        off = w.sb("off", [P, PAIR, P])
        feat = w.sb("feat", [P, PAIR, 2 * D])
        ps = w.ps("ps", [P, 512])
        index_ready, gathered, summed, off_ready, packed, off_packed, added = (
            w.sem(x) for x in ("index_ready", "gathered", "summed", "off_ready", "packed", "off_packed", "added"))
        gathers = 16 * 2 * PAIR
        adj_rows = a["adjT"].rearrange("j (t i) -> (j t) i", i=P)
        with nc.Block() as block:
            @block.scalar
            def _(act):
                n = runs(nc, act, m)
                with act.Fori(0, n) as it:
                    for s in range(SETS):
                        act.wait_ge(gathered[s], it * gathers)
                        nc.scalar.copy(index[s][:], m.index[:, bass.ds((it * SETS + s) * PAIR, PAIR), :]).then_inc(
                            index_ready[s], 1)

            @block.gpsimd
            def _(pool):
                n = runs(nc, pool, m)
                with pool.Fori(0, n) as it:
                    for s in range(SETS):
                        pool.wait_ge(index_ready[s], it + 1)
                        pool.wait_ge(summed[s], it)
                        pool.wait_ge(off_ready[s], it)
                        pool.wait_ge(packed[s], 16 * it)
                        pool.nop(nofuse=True)
                        for h in range(PAIR):
                            nc.gpsimd.indirect_dma_start(
                                out=adj[s][:, h, :], out_offset=None, in_=adj_rows,
                                in_offset=bass.IndirectOffsetOnAxis(ap=index[s][:, h, 0:1], axis=0)).then_inc(gathered[s], 16)
                            nc.gpsimd.indirect_dma_start(
                                out=feat[s][:, h, :], out_offset=None, in_=a["table0"],
                                in_offset=bass.IndirectOffsetOnAxis(ap=index[s][:, h, 1:2], axis=0)).then_inc(gathered[s], 16)

            @block.tensor
            def _(pe):
                n = runs(nc, pe, m)
                with pe.Fori(0, n) as it:
                    for s in range(SETS):
                        pe.wait_ge(gathered[s], (it + 1) * gathers)
                        pe.wait_ge(added[s], it)
                        for h in range(PAIR):
                            last = nc.tensor.matmul(ps[s][:, 0:2 * D], adj[s][:, h, :], feat[s][:, h, :],
                                                    start=h == 0, stop=h == PAIR - 1)
                        last.then_inc(summed[s], 1)

            @block.vector
            def _(dve):
                n = runs(nc, dve, m)
                with dve.Fori(0, n) as it:
                    tiles = tiles_of_step(nc, dve, m, it)
                    for s in range(SETS):
                        dve.wait_ge(gathered[s], (it + 1) * gathers)
                        dve.wait_ge(off_packed[s], 16 * it)
                        for h in range(PAIR):
                            last = nc.vector.scalar_tensor_tensor(
                                out=off[s][:, h, :], in0=m.row_ramp[:],
                                scalar=m.relative[:, bass.ds((it * SETS + s) * PAIR + h, 1)], in1=adj[s][:, h, :],
                                op0=ALU.not_equal, op1=ALU.mult)
                        last.then_inc(off_ready[s], 1)
                        dve.wait_ge(summed[s], it + 1)
                        dve.wait_ge(added[s - 1], it + (s > 0))
                        at = m.acc[:, bass.ds(tiles[s] * (2 * D), 2 * D)]
                        nc.vector.tensor_tensor(at, at, ps[s][:, 0:2 * D], ALU.add).then_inc(added[s], 1)

            @block.sync
            def _(sp):
                n = runs(nc, sp, m)
                with sp.Fori(0, n) as it:
                    for s in range(SETS):
                        sp.wait_ge(gathered[s], (it + 1) * gathers)
                        sp.dma_start(pair_of(a["adj_pack"], it, s), adj[s][:].rearrange("p h i -> p (h i)")).then_inc(
                            packed[s], 16)
                        sp.wait_ge(off_ready[s], it + 1)
                        sp.dma_start(pair_of(a["off_pack"], it, s), off[s][:].rearrange("p h i -> p (h i)")).then_inc(
                            off_packed[s], 16)
                for s in range(SETS):
                    sp.wait_ge(packed[s], 16 * n)
                    sp.wait_ge(off_packed[s], 16 * n)
                    sp.nop(nofuse=True)


def stage_gin_dense(nc, m, a):
    with Stage(nc) as ctx:
        def sb(name, shape):
            return [ctx.enter_context(nc.sbuf_tensor(f"d0_{name}{b}", shape, F32)) for b in range(2)]

        def ps(name):
            return [ctx.enter_context(nc.psum_tensor(f"d0_{name}{b}", [P, WIDE], F32)) for b in range(2)]

        def sem(name):
            return [ctx.sem(f"d0_{name}{b}") for b in range(2)]

        scaled = sb("scaled", [P, GROUP, D])
        act_in = [sb(f"layer{l}_", [P, WIDE]) for l in range(4)]
        ps_t = ps("ps_t")
        ps_l = ps("ps_l")
        ps_o = ps("ps_o")
        scaled_ready, turned, multiplied, activated, merged, added = (
            sem(x) for x in ("scaled_ready", "turned", "multiplied", "activated", "merged", "added"))
        acc = m.acc[:, 0:T * 2 * D].rearrange("p (t b d) -> p t b d", b=2, d=D)
        with nc.Block() as block:
            @block.vector
            def _(dve):
                def add(u, it):
                    dve.wait_ge(merged[u], it + 1)
                    at = m.x[:, bass.ds(it * (2 * GROUP) + u * GROUP, GROUP), :]
                    nc.vector.tensor_tensor(at, at, ps_o[u][:].rearrange("p (g d) -> p g d", d=D), ALU.add).then_inc(
                        added[u], 1)

                with dve.Fori(0, GROUPS // 2) as it:
                    for u in range(2):
                        for b in range(2):
                            dve.wait_ge(turned[b], it * 2 + u)
                            nc.vector.tensor_scalar(
                                scaled[b][:], acc[:, bass.ds(it * (2 * GROUP) + u * GROUP, GROUP), b, :],
                                m.eps[:, b:b + 1], None, ALU.mult).then_inc(scaled_ready[b], 1)
                    add(0, it)
                    add(1, it)

            @block.tensor
            def _(pe):
                with pe.Fori(0, GROUPS // 2) as it:
                    for u in range(2):
                        g = it * 2 + u
                        for b in range(2):
                            pe.wait_ge(scaled_ready[b], g + 1)
                            pe.wait_ge(activated[b], g * 4)
                            for i in range(GROUP):
                                last = nc.tensor.transpose(ps_t[b][:, i * P:(i + 1) * P], scaled[b][:, i, :], m.ident[:])
                            last.then_inc(turned[b], 1)
                        for l in range(3):
                            for b in range(2):
                                pe.wait_ge(activated[b], g * 4 + (l + 1))
                                nc.tensor.matmul(ps_l[b][:], m.w0[:, b * 3 + l, :], act_in[l][b][:], start=True,
                                                 stop=True).then_inc(multiplied[b], 1)
                        for b in range(2):
                            pe.wait_ge(activated[b], g * 4 + 4)
                        pe.wait_ge(added[u], it)
                        for i in range(GROUP):
                            out = ps_o[u][:, i * P:(i + 1) * P]
                            for b in range(2):
                                nc.tensor.matmul(out, act_in[3][b][:, i * P:(i + 1) * P], m.wm[:, b, :],
                                                 start=b == 0, stop=False)
                            last = nc.tensor.matmul(out, m.ones[0:1, :], m.bm[:], start=False, stop=True)
                        last.then_inc(merged[u], 1)

            @block.scalar
            def _(act):
                with act.Fori(0, GROUPS // 2) as it:
                    for u in range(2):
                        g = it * 2 + u
                        for b in range(2):
                            act.wait_ge(turned[b], g + 1)
                            if u:
                                act.wait_ge(merged[0], it + 1)
                            else:
                                act.wait_ge(merged[1], it)
                            nc.scalar.copy(act_in[0][b][:], ps_t[b][:]).then_inc(activated[b], 1)
                        for l in range(3):
                            for b in range(2):
                                act.wait_ge(multiplied[b], g * 3 + (l + 1))
                                nc.scalar.activation(act_in[l + 1][b][:], ps_l[b][:], ACT.Relu,
                                                     bias=m.b0[:, b * 3 + l:b * 3 + l + 1]).then_inc(activated[b], 1)


def stage_gat_max(nc, m, a):
    with Stage(nc) as ctx:
        w = Walk(nc, m, a, "g1", ctx)
        width = D + 2
        index = w.sb("index", [P, PAIR, 2], U32)
        adj = w.sb("adj", [P, PAIR, P])
        feat = w.sb("feat", [P, PAIR, width])
        bias = w.sb("bias", [P, PAIR, P])
        masked = w.sb("masked", [P, PAIR, P])
        best = w.sb("best", [P, 1])
        ps = w.ps("ps", [P, 512])
        index_ready, gathered, adj_loaded, packed, biased, masked_ready, turned, reduced, kept = (
            w.sem(x) for x in ("index_ready", "gathered", "adj_loaded", "packed", "biased", "masked_ready", "turned",
                               "reduced", "kept"))
        with nc.Block() as block:
            @block.gpsimd
            def _(pool):
                n = runs(nc, pool, m)
                with pool.Fori(0, n) as it:
                    for s in range(SETS):
                        pool.wait_ge(index_ready[s], it + 1)
                        pool.wait_ge(packed[s], 16 * it)
                        pool.wait_ge(masked_ready[s], it)
                        pool.nop(nofuse=True)
                        for h in range(PAIR):
                            nc.gpsimd.indirect_dma_start(
                                out=feat[s][:, h, :], out_offset=None, in_=a["table1"],
                                in_offset=bass.IndirectOffsetOnAxis(ap=index[s][:, h, 1:2], axis=0)).then_inc(gathered[s], 16)

            @block.sync
            def _(sp):
                n = runs(nc, sp, m)
                with sp.Fori(0, n) as it:
                    for s in range(SETS):
                        sp.wait_ge(biased[s], it)
                        sp.dma_start(adj[s][:].rearrange("p h i -> p (h i)"), pair_of(a["adj_pack"], it, s)).then_inc(
                            adj_loaded[s], 16)
                    for s in range(SETS):
                        sp.wait_ge(gathered[s], (it + 1) * (16 * PAIR))
                        sp.dma_start(pair_of(a["wh_pack"], it, s), feat[s][:].rearrange("p h w -> p (h w)")).then_inc(
                            packed[s], 16)
                for s in range(SETS):
                    sp.wait_ge(packed[s], 16 * n)
                    sp.nop(nofuse=True)

            @block.scalar
            def _(act):
                n = runs(nc, act, m)
                with act.Fori(0, n) as it:
                    for s in range(SETS):
                        act.wait_ge(gathered[s], it * (16 * PAIR))
                        nc.scalar.copy(index[s][:], m.index[:, bass.ds((it * SETS + s) * PAIR, PAIR), :]).then_inc(
                            index_ready[s], 1)
                    for s in range(SETS):
                        act.wait_ge(gathered[s], (it + 1) * (16 * PAIR))
                        act.wait_ge(biased[s], it + 1)
                        act.wait_ge(turned[s], it)
                        for h in range(PAIR):
                            last = nc.scalar.activation(masked[s][:, h, :], bias[s][:, h, :], ACT.Identity,
                                                        bias=feat[s][:, h, D + 1:D + 2])
                        last.then_inc(masked_ready[s], 1)

            @block.tensor
            def _(pe):
                n = runs(nc, pe, m)
                with pe.Fori(0, n) as it:
                    for s in range(SETS):
                        pe.wait_ge(masked_ready[s], it + 1)
                        pe.wait_ge(reduced[s], it)
                        for h in range(PAIR):
                            last = nc.tensor.transpose(ps[s][:, h * P:(h + 1) * P], masked[s][:, h, :], m.ident[:])
                        last.then_inc(turned[s], 1)

            @block.vector
            def _(dve):
                n = runs(nc, dve, m)
                with dve.Fori(0, n) as it:
                    for s in range(SETS):
                        dve.wait_ge(adj_loaded[s], it * 16 + 16)
                        dve.wait_ge(masked_ready[s], it)
                        nc.vector.tensor_scalar(bias[s][:], adj[s][:], 0.0, -BIG, ALU.is_le, ALU.mult).then_inc(
                            biased[s], 1)
                    tiles = tiles_of_step(nc, dve, m, it)
                    for s in range(SETS):
                        dve.wait_ge(turned[s], it + 1)
                        nc.vector.tensor_reduce(best[s][:], ps[s][:, 0:PAIR * P], AX.X, ALU.max).then_inc(reduced[s], 1)
                        dve.wait_ge(reduced[s], it + 1)
                        dve.wait_ge(kept[s - 1], it + (s > 0))
                        at = m.best1[:, bass.ds(tiles[s], 1)]
                        nc.vector.tensor_tensor(at, at, best[s][:], ALU.max).then_inc(kept[s], 1)


def spread_rows(nc, m, a, name, value, wide, scratch, columns, before=None):
    with Stage(nc) as ctx:
        turned, copied, stored, loaded = (
            ctx.sem(f"{name}_{x}") for x in ("turned", "copied", "stored", "loaded"))
        ps = ctx.enter_context(nc.psum_tensor(f"{name}_ps", [P, P], F32))
        rows = ctx.enter_context(nc.sbuf_tensor(f"{name}_rows", [P, P], F32))
        ready = ctx.sem(f"{name}_ready")
        with nc.Block() as block:
            @block.vector
            def _(dve):
                before(dve, ready)
                dve.wait_ge(turned, 1)
                nc.vector.tensor_copy(rows[0:columns, :], ps[0:columns, :]).then_inc(copied, 1)

            @block.tensor
            def _(pe):
                pe.wait_ge(ready, 1)
                nc.tensor.transpose(ps[0:columns, :], value, m.ident[:]).then_inc(turned, 1)

            @block.sync
            def _(sp):
                sp.wait_ge(copied, 1)
                sp.dma_start(scratch.rearrange("(c i) -> c i", i=P), rows[0:columns, :]).then_inc(stored, 16)
                sp.wait_ge(stored, 16)
                sp.dma_start(wide, scratch.rearrange("(a n) -> a n", a=1).broadcast_to([P, columns * P])).then_inc(
                    loaded, 16)
                sp.wait_ge(loaded, 16)


def stage_gat_shift(nc, m, a):
    with Stage(nc) as ctx:
        def sb(name, shape):
            return ctx.enter_context(nc.sbuf_tensor("sh_" + name, shape, F32))

        best_wide = sb("best_wide", [P, N])
        tenth = sb("tenth", [P, 1024])
        step = ctx.sem("sh_step")

        def before(dve, ready):
            nc.vector.tensor_copy(m.best1c[:], m.best1[:, 0:T]).then_inc(ready, 1)

        spread_rows(nc, m, a, "sh1", m.best1c[:], best_wide[:], a["row_scratch"][0:N], T, before)
        with nc.Block() as block:
            @block.vector
            def _(dve):
                k = 0
                for c in range(4):
                    part = slice(c * 1024, (c + 1) * 1024)
                    nc.vector.tensor_tensor(best_wide[:, part], best_wide[:, part], m.s1_wide[:, part], ALU.add
                                            ).then_inc(step, 1)
                    k += 1
                    dve.wait_ge(step, k)
                    nc.vector.tensor_scalar(tenth[:], best_wide[:, part], ALPHA, None, ALU.mult).then_inc(step, 1)
                    k += 1
                    dve.wait_ge(step, k)
                    nc.vector.tensor_tensor(m.shift1[:, part], best_wide[:, part], tenth[:], ALU.max).then_inc(step, 1)
                    k += 1
                    dve.wait_ge(step, k)


def stage_gat_pairs(nc, m, a):
    with Stage(nc) as ctx:
        w = Walk(nc, m, a, "g2", ctx)
        width = D + 2
        adj = w.sb("adj", [P, PAIR, P])
        feat = w.sb("feat", [P, PAIR, width])
        bias = w.sb("bias", [P, PAIR, P])
        leaky = w.sb("leaky", [P, PAIR, P])
        prob = w.sb("prob", [P, PAIR, P])
        ps = w.ps("ps", [P, 512])
        adj_loaded, feat_loaded, biased, leaky_ready, chain, shifted, exped, summed, added = (
            w.sem(x) for x in ("adj_loaded", "feat_loaded", "biased", "leaky_ready", "chain", "shifted", "exped",
                               "summed", "added"))
        with nc.Block() as block:
            @block.sync
            def _(sp):
                n = runs(nc, sp, m)
                with sp.Fori(0, n) as it:
                    for s in range(SETS):
                        sp.wait_ge(biased[s], it)
                        sp.dma_start(adj[s][:].rearrange("p h i -> p (h i)"), pair_of(a["adj_pack"], it, s)).then_inc(
                            adj_loaded[s], 16)
                        sp.wait_ge(summed[s], it)
                        sp.dma_start(feat[s][:].rearrange("p h w -> p (h w)"), pair_of(a["wh_pack"], it, s)).then_inc(
                            feat_loaded[s], 16)

            @block.scalar
            def _(act):
                n = runs(nc, act, m)
                with act.Fori(0, n) as it:
                    tiles = tiles_of_step(nc, act, m, it)
                    for s in range(SETS):
                        act.wait_ge(feat_loaded[s], it * 16 + 16)
                        act.wait_ge(shifted[s], it)
                        for h in range(PAIR):
                            last = nc.scalar.activation(leaky[s][:, h, :], m.s1_wide[:, bass.ds(tiles[s] * P, P)],
                                                        ACT.Identity, bias=feat[s][:, h, D + 1:D + 2])
                        last.then_inc(leaky_ready[s], 1)
                    for s in range(SETS):
                        act.wait_ge(shifted[s], it + 1)
                        act.wait_ge(summed[s], it)
                        nc.scalar.activation(prob[s][:], bias[s][:], ACT.Exp).then_inc(exped[s], 1)

            @block.tensor
            def _(pe):
                n = runs(nc, pe, m)
                with pe.Fori(0, n) as it:
                    for s in range(SETS):
                        pe.wait_ge(exped[s], it + 1)
                        pe.wait_ge(added[s], it)
                        for h in range(PAIR):
                            last = nc.tensor.matmul(ps[s][:, 0:D + 1], prob[s][:, h, :], feat[s][:, h, 0:D + 1],
                                                    start=h == 0, stop=h == PAIR - 1)
                        last.then_inc(summed[s], 1)

            @block.vector
            def _(dve):
                n = runs(nc, dve, m)
                with dve.Fori(0, n) as it:
                    tiles = tiles_of_step(nc, dve, m, it)
                    for s in range(SETS):
                        dve.wait_ge(adj_loaded[s], it * 16 + 16)
                        dve.wait_ge(exped[s], it)
                        nc.vector.tensor_scalar(bias[s][:], adj[s][:], 0.0, -BIG, ALU.is_le, ALU.mult).then_inc(
                            biased[s], 1)
                    for s in range(SETS):
                        dve.wait_ge(leaky_ready[s], it + 1)
                        nc.vector.scalar_tensor_tensor(out=leaky[s][:], in0=leaky[s][:], scalar=ALPHA, in1=leaky[s][:],
                                                       op0=ALU.mult, op1=ALU.max).then_inc(chain[s], 1)
                    for s in range(SETS):
                        dve.wait_ge(chain[s], it * 2 + 1)
                        shift = m.shift1[:, bass.ds(tiles[s] * P, P)].rearrange("p (o i) -> p o i", o=1)
                        nc.vector.tensor_tensor(leaky[s][:], leaky[s][:], shift.broadcast_to([P, PAIR, P]),
                                                ALU.subtract).then_inc(chain[s], 1)
                    for s in range(SETS):
                        dve.wait_ge(chain[s], it * 2 + 2)
                        dve.wait_ge(biased[s], it + 1)
                        nc.vector.tensor_tensor(bias[s][:], bias[s][:], leaky[s][:], ALU.add).then_inc(shifted[s], 1)
                    for s in range(SETS):
                        dve.wait_ge(summed[s], it + 1)
                        dve.wait_ge(added[s - 1], it + (s > 0))
                        at = m.acc[:, bass.ds(tiles[s] * (D + 1), D + 1)]
                        nc.vector.tensor_tensor(at, at, ps[s][:, 0:D + 1], ALU.add).then_inc(added[s], 1)


def stage_gat_dense(nc, m, a):
    with Stage(nc) as ctx:
        def sb(name, shape):
            return ctx.enter_context(nc.sbuf_tensor("d1_" + name, shape, F32))

        alone = sb("alone", [P, T])
        denom = sb("denom", [P, T])
        hsum = sb("hsum", [P, 1])
        hsum_wide = sb("hsum_wide", [P, P])
        mean = sb("mean", [P, D])
        out = [sb(f"out{u}", [P, D]) for u in range(2)]
        low = [sb(f"low{u}", [P, D]) for u in range(2)]
        ps = ctx.enter_context(nc.psum_tensor("d1_ps", [P, 512], F32))
        step, meaned = (ctx.sem("d1_" + x) for x in ("step", "meaned"))
        lowered, exped, chain = ([ctx.sem(f"d1_{x}{u}") for u in range(2)]
                                 for x in ("lowered", "exped", "chain"))
        acc = m.acc[:, 0:T * (D + 1)].rearrange("p (t d) -> p t d", d=D + 1)
        with nc.Block() as block:
            @block.tensor
            def _(pe):
                pe.wait_ge(step, 3)
                nc.tensor.matmul(ps[:, 0:D], hsum_wide[:], m.w1[:, 0:D], start=True, stop=True).then_inc(meaned, 1)

            @block.vector
            def _(dve):
                nc.vector.tensor_scalar(alone[:], m.best1[:, 0:T], -0.5 * BIG, None, ALU.is_lt).then_inc(step, 1)
                nc.vector.tensor_reduce(hsum[:], m.hsum[:], AX.X, ALU.add).then_inc(step, 1)
                dve.wait_ge(step, 2)
                nc.vector.tensor_scalar(hsum_wide[:], m.ones[:], hsum[:, 0:1], 1.0 / N, ALU.mult, ALU.mult).then_inc(step, 1)
                nc.vector.tensor_tensor(denom[:], acc[:, :, D], alone[:], ALU.add).then_inc(step, 1)
                dve.wait_ge(step, 4)
                nc.vector.reciprocal(denom[:], denom[:]).then_inc(step, 1)
                dve.wait_ge(meaned, 1)
                nc.vector.tensor_copy(mean[:], ps[:, 0:D]).then_inc(step, 1)
                dve.wait_ge(step, 6)
                with dve.Fori(0, T // 2) as it:
                    for u in range(2):
                        t = it * 2 + u
                        dve.wait_ge(chain[u], it * 4)
                        nc.vector.tensor_scalar(out[u][:], acc[:, bass.ds(t, 1), 0:D].rearrange("p o d -> p (o d)"),
                                                denom[:, bass.ds(t, 1)], None, ALU.mult).then_inc(chain[u], 1)
                        dve.wait_ge(chain[u], it * 4 + 1)
                        nc.vector.scalar_tensor_tensor(out=out[u][:], in0=mean[:], scalar=alone[:, bass.ds(t, 1)],
                                                       in1=out[u][:], op0=ALU.mult, op1=ALU.add).then_inc(chain[u], 1)
                        dve.wait_ge(chain[u], it * 4 + 2)
                        nc.vector.tensor_scalar(low[u][:], out[u][:], 0.0, None, ALU.min).then_inc(lowered[u], 1)
                    for u in range(2):
                        t = it * 2 + u
                        dve.wait_ge(exped[u], it + 1)
                        nc.vector.scalar_tensor_tensor(out=out[u][:], in0=out[u][:], scalar=0.0, in1=low[u][:],
                                                       op0=ALU.max, op1=ALU.add).then_inc(chain[u], 1)
                        dve.wait_ge(chain[u], it * 4 + 3)
                        at = m.x[:, bass.ds(t, 1), :].rearrange("p o d -> p (o d)")
                        nc.vector.scalar_tensor_tensor(out=at, in0=out[u][:], scalar=-1.0, in1=at, op0=ALU.add,
                                                       op1=ALU.add).then_inc(chain[u], 1)

            @block.scalar
            def _(act):
                with act.Fori(0, T // 2) as it:
                    for u in range(2):
                        act.wait_ge(lowered[u], it + 1)
                        nc.scalar.activation(low[u][:], low[u][:], ACT.Exp).then_inc(exped[u], 1)




def stage_signed_sums(nc, m, a):
    with Stage(nc) as ctx:
        w = Walk(nc, m, a, "g3", ctx)
        width = UV_END
        index = w.sb("index", [P, PAIR, 2], U32)
        adj = w.sb("adj", [P, PAIR, P])
        above = w.sb("above", [P, PAIR, P])
        below = w.sb("below", [P, PAIR, P])
        feat = w.sb("feat", [P, PAIR, width])
        ps = w.ps("ps", [P, 512])
        index_ready, gathered, adj_loaded, packed, compared, summed, added = (
            w.sem(x) for x in ("index_ready", "gathered", "adj_loaded", "packed", "compared", "summed", "added"))
        with nc.Block() as block:
            @block.gpsimd
            def _(pool):
                n = runs(nc, pool, m)
                with pool.Fori(0, n) as it:
                    for s in range(SETS):
                        pool.wait_ge(index_ready[s], it + 1)
                        pool.wait_ge(packed[s], 16 * it)
                        pool.wait_ge(summed[s], it)
                        pool.nop(nofuse=True)
                        for h in range(PAIR):
                            nc.gpsimd.indirect_dma_start(
                                out=feat[s][:, h, :], out_offset=None, in_=a["table2"],
                                in_offset=bass.IndirectOffsetOnAxis(ap=index[s][:, h, 1:2], axis=0)).then_inc(gathered[s], 16)

            @block.sync
            def _(sp):
                n = runs(nc, sp, m)
                with sp.Fori(0, n) as it:
                    for s in range(SETS):
                        sp.wait_ge(summed[s], it)
                        sp.dma_start(adj[s][:].rearrange("p h i -> p (h i)"), pair_of(a["off_pack"], it, s)).then_inc(
                            adj_loaded[s], 16)
                    for s in range(SETS):
                        sp.wait_ge(gathered[s], (it + 1) * (16 * PAIR))
                        sp.dma_start(pair_of(a["h_pack"], it, s), feat[s][:].rearrange("p h w -> p (h w)")).then_inc(
                            packed[s], 16)
                for s in range(SETS):
                    sp.wait_ge(packed[s], 16 * n)
                    sp.nop(nofuse=True)

            @block.scalar
            def _(act):
                n = runs(nc, act, m)
                with act.Fori(0, n) as it:
                    for s in range(SETS):
                        act.wait_ge(gathered[s], it * (16 * PAIR))
                        nc.scalar.copy(index[s][:], m.index[:, bass.ds((it * SETS + s) * PAIR, PAIR), :]).then_inc(
                            index_ready[s], 1)

            @block.tensor
            def _(pe):
                n = runs(nc, pe, m)
                with pe.Fori(0, n) as it:
                    for s in range(SETS):
                        pe.wait_ge(gathered[s], (it + 1) * (16 * PAIR))
                        pe.wait_ge(compared[s], it + 1)
                        pe.wait_ge(adj_loaded[s], it * 16 + 16)
                        pe.wait_ge(added[s], it)
                        for left, at, cols in ((adj, slice(0, D), slice(0, D)),
                                               (above, slice(D, D + SIGN_W), slice(D, width)),
                                               (below, slice(D + SIGN_W, SUPPORT_W), slice(D, width))):
                            for h in range(PAIR):
                                last = nc.tensor.matmul(ps[s][:, at], left[s][:, h, :], feat[s][:, h, cols],
                                                        start=h == 0, stop=h == PAIR - 1)
                        last.then_inc(summed[s], 1)

            @block.vector
            def _(dve):
                n = runs(nc, dve, m)
                with dve.Fori(0, n) as it:
                    for s in range(SETS):
                        dve.wait_ge(adj_loaded[s], it * 16 + 16)
                        dve.wait_ge(summed[s], it)
                        nc.vector.tensor_scalar(above[s][:], adj[s][:], 0.0, None, ALU.is_gt)
                        nc.vector.tensor_scalar(below[s][:], adj[s][:], 0.0, None, ALU.is_lt).then_inc(compared[s], 1)
                    tiles = tiles_of_step(nc, dve, m, it)
                    for s in range(SETS):
                        dve.wait_ge(summed[s], it + 1)
                        dve.wait_ge(added[s - 1], it + (s > 0))
                        at = m.acc[:, bass.ds(tiles[s] * SUPPORT_W, SUPPORT_W)]
                        nc.vector.tensor_tensor(at, at, ps[s][:, 0:SUPPORT_W], ALU.add).then_inc(added[s], 1)


def stage_signed_scores(nc, m, a):
    with Stage(nc) as ctx:
        scores = [ctx.enter_context(nc.sbuf_tensor(f"sc_scores{g}", [P, T, 4], F32)) for g in range(2)]
        tenth = [ctx.enter_context(nc.sbuf_tensor(f"sc_tenth{g}", [P, T, 4], F32)) for g in range(2)]
        most = ctx.enter_context(nc.sbuf_tensor("sc_most", [P, 2], F32))
        flags = ctx.enter_context(nc.sbuf_tensor("sc_flags", [1, 2], F32))
        ps = ctx.enter_context(nc.psum_tensor("sc_ps", [P, 2 * P], F32))
        step, stored, counted, turned, flagged = (
            ctx.sem("sc_" + x) for x in ("step", "stored", "counted", "turned", "flagged"))
        acc = m.acc[:, 0:T * SUPPORT_W].rearrange("p (t w) -> p t w", w=SUPPORT_W)
        above = acc[:, :, D:D + 2 * HEADS].rearrange("p t (k o) -> p t k o", o=2)
        below = acc[:, :, D + SIGN_W:D + SIGN_W + 2 * HEADS].rearrange("p t (k o) -> p t k o", o=2)
        with nc.Block() as block:
            @block.vector
            def _(dve):
                for g, (first, second) in enumerate(((above, below), (below, above))):
                    nc.vector.memset(scores[g][:], 0.0).then_inc(step, 1)
                    dve.wait_ge(step, 4 * g + 1)
                    nc.vector.tensor_tensor(scores[g][:, :, 0:HEADS], first[:, :, :, 0], second[:, :, :, 1], ALU.add
                                            ).then_inc(step, 1)
                    dve.wait_ge(step, 4 * g + 2)
                    nc.vector.tensor_scalar(tenth[g][:], scores[g][:], ALPHA, None, ALU.mult).then_inc(step, 1)
                    dve.wait_ge(step, 4 * g + 3)
                    nc.vector.tensor_tensor(scores[g][:], scores[g][:], tenth[g][:], ALU.max).then_inc(step, 1)
                for c, count in enumerate((SUPPORT_W - 1, UV_END - 1)):
                    nc.vector.tensor_reduce(most[:, c:c + 1], acc[:, :, count], AX.X, ALU.max).then_inc(counted, 1)
                dve.wait_ge(turned, 1)
                for c in range(2):
                    nc.vector.tensor_reduce(flags[:, c:c + 1], ps[0:1, c * P:(c + 1) * P], AX.X, ALU.max).then_inc(
                        flagged, 1)
                dve.wait_ge(flagged, 2)
                nc.vector.tensor_scalar(m.meta[:, NEGATIVES:NEGATIVES + 1], flags[:, 0:1], 0.5, None, ALU.is_gt)
                nc.vector.tensor_scalar(m.meta[:, CROWDED:CROWDED + 1], flags[:, 1:2], TOPK - 0.5, None, ALU.is_gt)

            @block.tensor
            def _(pe):
                pe.wait_ge(counted, 2)
                for c in range(2):
                    last = nc.tensor.matmul(ps[0:1, c * P:(c + 1) * P], most[:, c:c + 1], m.ident[:], start=True,
                                            stop=True)
                last.then_inc(turned, 1)

            @block.sync
            def _(sp):
                for g in range(2):
                    sp.wait_ge(step, 4 * g + 4)
                    sp.dma_start(a["score_table"][g * N:(g + 1) * N, :].rearrange("(t p) k -> p t k", p=P),
                                 scores[g][:]).then_inc(stored, 16)
                sp.wait_ge(stored, 32)


def stage_signed_max(nc, m, a, sign):
    flag = None if sign > 0 else NEGATIVES
    with Stage(nc) as ctx:
        w = Walk(nc, m, a, f"g4{sign > 0:d}", ctx)
        index = w.sb("index", [P, PAIR], U32)
        adj = w.sb("adj", [P, PAIR, P])
        score = w.sb("score", [P, PAIR, 4])
        bias = w.sb("bias", [P, PAIR, P])
        masked = w.sb("masked", [P, HEADS, PAIR, P], sets=2)
        best = w.sb("best", [P, HEADS], sets=2)
        ps = w.ps("ps", [P, 1024], sets=2)
        index_ready, gathered, adj_loaded, packed, biased, masked_ready, turned, reduced, kept = (
            w.sem(x) for x in ("index_ready", "gathered", "adj_loaded", "packed", "biased", "masked_ready", "turned",
                               "reduced", "kept"))

        def two_before(eng, semaphore, s, it):
            eng.wait_ge(semaphore[(s + 2) % SETS], it + (s >= 2))

        with nc.Block() as block:
            @block.gpsimd
            def _(pool):
                with where(pool, m, flag):
                    n = runs(nc, pool, m)
                    with pool.Fori(0, n) as it:
                        for s in range(SETS):
                            pool.wait_ge(index_ready[s], it + 1)
                            pool.wait_ge(packed[s], 16 * it)
                            pool.wait_ge(masked_ready[s], it)
                            pool.nop(nofuse=True)
                            for h in range(PAIR):
                                nc.gpsimd.indirect_dma_start(
                                    out=score[s][:, h, :], out_offset=None, in_=a["score_table"],
                                    in_offset=bass.IndirectOffsetOnAxis(ap=index[s][:, h:h + 1], axis=0)).then_inc(gathered[s], 16)

            @block.sync
            def _(sp):
                with where(sp, m, flag):
                    n = runs(nc, sp, m)
                    pack = a["score_pack1" if sign > 0 else "score_pack0"]
                    with sp.Fori(0, n) as it:
                        for s in range(SETS):
                            sp.wait_ge(biased[s], it)
                            sp.dma_start(adj[s][:].rearrange("p h i -> p (h i)"), pair_of(a["off_pack"], it, s)).then_inc(
                                adj_loaded[s], 16)
                        for s in range(SETS):
                            sp.wait_ge(gathered[s], (it + 1) * (16 * PAIR))
                            sp.dma_start(pair_of(pack, it, s), score[s][:].rearrange("p h w -> p (h w)")).then_inc(
                                packed[s], 16)
                    for s in range(SETS):
                        sp.wait_ge(packed[s], 16 * n)
                        sp.nop(nofuse=True)

            @block.scalar
            def _(act):
                with where(act, m, flag):
                    n = runs(nc, act, m)
                    with act.Fori(0, n) as it:
                        for s in range(SETS):
                            act.wait_ge(gathered[s], it * (16 * PAIR))
                            nc.scalar.activation(index[s][:], m.index[:, bass.ds((it * SETS + s) * PAIR, PAIR), 1],
                                                 ACT.Copy, bias=0.0 if sign > 0 else float(N)).then_inc(index_ready[s], 1)
                        for s in range(SETS):
                            u = s % 2
                            act.wait_ge(gathered[s], (it + 1) * (16 * PAIR))
                            act.wait_ge(biased[s], it + 1)
                            two_before(act, turned, s, it)
                            for k in range(HEADS):
                                for h in range(PAIR):
                                    last = nc.scalar.activation(masked[u][:, k, h, :], bias[s][:, h, :], ACT.Identity,
                                                                bias=score[s][:, h, k:k + 1])
                            last.then_inc(masked_ready[s], 1)

            @block.tensor
            def _(pe):
                with where(pe, m, flag):
                    n = runs(nc, pe, m)
                    with pe.Fori(0, n) as it:
                        for s in range(SETS):
                            u = s % 2
                            pe.wait_ge(masked_ready[s], it + 1)
                            two_before(pe, reduced, s, it)
                            for k in range(HEADS):
                                for h in range(PAIR):
                                    c = (k * PAIR + h) * P
                                    last = nc.tensor.transpose(ps[u][:, c:c + P], masked[u][:, k, h, :], m.ident[:])
                            last.then_inc(turned[s], 1)

            @block.vector
            def _(dve):
                with where(dve, m, flag):
                    n = runs(nc, dve, m)
                    with dve.Fori(0, n) as it:
                        for s in range(SETS):
                            dve.wait_ge(adj_loaded[s], it * 16 + 16)
                            dve.wait_ge(masked_ready[s], it)
                            nc.vector.tensor_scalar(bias[s][:], adj[s][:], 0.0, -BIG, ALU.is_le if sign > 0 else ALU.is_ge,
                                                    ALU.mult).then_inc(biased[s], 1)
                        tiles = tiles_of_step(nc, dve, m, it)
                        for s in range(SETS):
                            u = s % 2
                            dve.wait_ge(turned[s], it + 1)
                            nc.vector.tensor_reduce(best[u][:], ps[u][:, 0:HEADS * PAIR * P].rearrange(
                                "p (k s) -> p k s", k=HEADS), AX.X, ALU.max).then_inc(reduced[s], 1)
                            dve.wait_ge(reduced[s], it + 1)
                            dve.wait_ge(kept[s - 1], it + (s > 0))
                            at = m.best2[:, bass.ds(tiles[s], 1), :].rearrange("p o k -> p (o k)")
                            nc.vector.tensor_tensor(at, at, best[u][:], ALU.max).then_inc(kept[s], 1)


def stage_signed_pairs(nc, m, a, sign):
    flag = None if sign > 0 else NEGATIVES
    with Stage(nc) as ctx:
        w = Walk(nc, m, a, f"g5{sign > 0:d}", ctx)
        adj = w.sb("adj", [P, PAIR, P])
        feat = w.sb("feat", [P, PAIR, UV_END])
        score = w.sb("score", [P, PAIR, 4])
        bias = w.sb("bias", [P, PAIR, P])
        expo = w.sb("expo", [P, HEADS, PAIR, P], sets=2)
        prob = w.sb("prob", [P, HEADS, PAIR, P], sets=2)
        ps = w.ps("ps", [P, 512])
        loaded, biased, shifted, exped, weighted, summed, added = (
            w.sem(x) for x in ("loaded", "biased", "shifted", "exped", "weighted", "summed", "added"))

        def two_before(eng, semaphore, s, it):
            eng.wait_ge(semaphore[(s + 2) % SETS], it + (s >= 2))

        with nc.Block() as block:
            @block.sync
            def _(sp):
                with where(sp, m, flag):
                    n = runs(nc, sp, m)
                    pack = a["score_pack1" if sign > 0 else "score_pack0"]
                    with sp.Fori(0, n) as it:
                        for s in range(SETS):
                            sp.wait_ge(summed[s], it)
                            for dst, src in ((adj, a["off_pack"]), (score, pack), (feat, a["h_pack"])):
                                sp.dma_start(dst[s][:].rearrange("p h i -> p (h i)"), pair_of(src, it, s)).then_inc(
                                    loaded[s], 16)

            @block.vector
            def _(dve):
                with where(dve, m, flag):
                    n = runs(nc, dve, m)
                    with dve.Fori(0, n) as it:
                        tiles = tiles_of_step(nc, dve, m, it)

                        def front(s):
                            u = s % 2
                            dve.wait_ge(loaded[s], it * 48 + 48)
                            nc.vector.tensor_scalar(bias[s][:], adj[s][:], 0.0, -BIG, ALU.is_le if sign > 0 else ALU.is_ge,
                                                    ALU.mult).then_inc(biased[s], 1)
                            dve.wait_ge(biased[s], it + 1)
                            two_before(dve, summed, s, it)
                            shift = m.shift2[:, bass.ds(tiles[s] * (HEADS * P), HEADS * P)].rearrange(
                                "p (k o i) -> p k o i", k=HEADS, o=1)
                            nc.vector.tensor_tensor(
                                expo[u][:], bias[s][:].rearrange("p (o h) i -> p o h i", o=1).broadcast_to(
                                    [P, HEADS, PAIR, P]),
                                shift.broadcast_to([P, HEADS, PAIR, P]), ALU.subtract).then_inc(shifted[s], 1)

                        def back(s):
                            u = s % 2
                            dve.wait_ge(exped[s], it + 1)
                            nc.vector.tensor_tensor(
                                prob[u][:], expo[u][:], adj[s][:].rearrange("p (o h) i -> p o h i", o=1).broadcast_to(
                                    [P, HEADS, PAIR, P]), ALU.mult).then_inc(weighted[s], 1)

                        def add(s):
                            dve.wait_ge(summed[s], it + 1)
                            dve.wait_ge(added[s - 1], it + (s > 0))
                            at = m.acc[:, bass.ds(tiles[s] * HEAD_W, HEAD_W)]
                            nc.vector.tensor_tensor(at, at, ps[s][:, 0:HEAD_W], ALU.add).then_inc(added[s], 1)

                        front(0)
                        front(1)
                        back(0)
                        front(2)
                        back(1)
                        add(0)
                        front(3)
                        back(2)
                        add(1)
                        back(3)
                        add(2)
                        add(3)

            @block.scalar
            def _(act):
                with where(act, m, flag):
                    n = runs(nc, act, m)
                    with act.Fori(0, n) as it:
                        for s in range(SETS):
                            u = s % 2
                            act.wait_ge(shifted[s], it + 1)
                            act.wait_ge(loaded[s], it * 48 + 48)
                            for k in range(HEADS):
                                for h in range(PAIR):
                                    last = nc.scalar.activation(expo[u][:, k, h, :], expo[u][:, k, h, :], ACT.Exp,
                                                                bias=score[s][:, h, k:k + 1])
                            last.then_inc(exped[s], 1)

            @block.tensor
            def _(pe):
                with where(pe, m, flag):
                    n = runs(nc, pe, m)
                    with pe.Fori(0, n) as it:
                        for s in range(SETS):
                            u = s % 2
                            pe.wait_ge(exped[s], it + 1)
                            pe.wait_ge(weighted[s], it + 1)
                            pe.wait_ge(loaded[s], it * 48 + 48)
                            pe.wait_ge(added[s], it)
                            for k in range(HEADS):
                                c = k * (D + 1)
                                for h in range(PAIR):
                                    nc.tensor.matmul(ps[s][:, c:c + D], prob[u][:, k, h, :], feat[s][:, h, 0:D],
                                                     start=h == 0, stop=h == PAIR - 1)
                                for h in range(PAIR):
                                    last = nc.tensor.matmul(ps[s][:, c + D:c + D + 1], expo[u][:, k, h, :],
                                                            m.ones[:, 0:1], start=h == 0, stop=h == PAIR - 1)
                            last.then_inc(summed[s], 1)


def stage_gru(nc, m, a, which):
    heads = HEADS if which else 1
    with Stage(nc) as ctx:
        def sb(name, shape):
            return ctx.enter_context(nc.sbuf_tensor(f"r{which}_{name}", shape, F32))

        def sem(name):
            return ctx.sem(f"r{which}_{name}")

        rden = sb("rden", [P, GROUP, HEADS])
        part = sb("part", [P, heads, GROUP, D])
        partT = sb("partT", [P, heads, WIDE])
        sT = sb("sT", [P, WIDE])
        r = sb("r", [P, WIDE])
        z = sb("z", [P, WIDE])
        hn = sb("hn", [P, WIDE])
        cand = sb("cand", [P, WIDE])
        new = sb("new", [P, WIDE])
        scaled = sb("scaled", [P, GROUP, D])
        ps_t = [ctx.enter_context(nc.psum_tensor(f"r{which}_ps_t{k}", [P, WIDE], F32)) for k in range(heads)]
        ps_e = ctx.enter_context(nc.psum_tensor(f"r{which}_ps_e", [P, WIDE], F32))
        ps_g = [ctx.enter_context(nc.psum_tensor(f"r{which}_ps_g{k}", [P, WIDE], F32)) for k in range(4)]
        parted, turned, copied, mixed, mixed_copied, gated, gates_read, dv, tanhed, newed, back, added = (
            sem(x) for x in ("parted", "turned", "copied", "mixed", "mixed_copied", "gated", "gates_read", "dve",
                             "tanhed", "newed", "back", "added"))
        acts = sem("acts")

        def group(tensor, it):
            return tensor[:, bass.ds(it * GROUP, GROUP), :]

        with nc.Block() as block:
            @block.vector
            def _(dve):
                own = 5 if which else 3
                with dve.Fori(0, GROUPS) as it:
                    dve.wait_ge(turned, it)
                    if which:
                        acc = m.acc[:, 0:T * HEAD_W].rearrange("p (t k w) -> p t k w", k=HEADS, w=D + 1)
                        rows = acc[:, bass.ds(it * GROUP, GROUP), :, :]
                        nc.vector.tensor_scalar(rden[:], rows[:, :, :, D], 1.0 / BIG, None, ALU.max).then_inc(dv, 1)
                        dve.wait_ge(dv, it * 5 + 1)
                        nc.vector.reciprocal(rden[:], rden[:]).then_inc(dv, 1)
                        dve.wait_ge(dv, it * 5 + 2)
                        for k in range(HEADS):
                            last = nc.vector.tensor_tensor(part[:, k, :, :], rows[:, :, k, 0:D],
                                                           rden[:, :, k:k + 1].broadcast_to([P, GROUP, D]), ALU.mult)
                        last.then_inc(parted, 1)
                    else:
                        acc = m.acc[:, 0:T * SUPPORT_W].rearrange("p (t w) -> p t w", w=SUPPORT_W)
                        nc.vector.tensor_copy(part[:, 0, :, :], group(acc, it)[:, :, 0:D]).then_inc(parted, 1)
                    dve.wait_ge(acts, it + 1)
                    nc.vector.tensor_tensor(r[:], r[:], hn[:], ALU.mult).then_inc(dv, 1)
                    dve.wait_ge(dv, it * own + (own - 2))
                    nc.vector.tensor_tensor(cand[:], ps_g[2][:], r[:], ALU.add).then_inc(gates_read, 1)
                    dve.wait_ge(tanhed, it + 1)
                    nc.vector.tensor_tensor(new[:], m.hT[:, bass.ds(it * WIDE, WIDE)], cand[:], ALU.subtract).then_inc(dv, 1)
                    dve.wait_ge(dv, it * own + (own - 1))
                    nc.vector.tensor_tensor(new[:], new[:], z[:], ALU.mult).then_inc(dv, 1)
                    dve.wait_ge(dv, it * own + own)
                    nc.vector.tensor_tensor(new[:], new[:], cand[:], ALU.add).then_inc(newed, 1)
                    dve.wait_ge(back, it + 1)
                    dia = m.diagonal[:, bass.ds(it * GROUP, GROUP)].rearrange("p (g o) -> p g o", o=1)
                    nc.vector.tensor_tensor(scaled[:], ps_t[0][:].rearrange("p (g d) -> p g d", d=D),
                                            dia.broadcast_to([P, GROUP, D]), ALU.mult).then_inc(added, 1)
                    dve.wait_ge(added, it * 2 + 1)
                    nc.vector.tensor_tensor(group(m.x, it), group(m.x, it), scaled[:], ALU.add).then_inc(added, 1)

            @block.tensor
            def _(pe):
                with pe.Fori(0, GROUPS) as it:
                    pe.wait_ge(parted, it + 1)
                    pe.wait_ge(added, it * 2)
                    for k in range(heads):
                        for g in range(GROUP):
                            last = nc.tensor.transpose(ps_t[k][:, g * P:(g + 1) * P], part[:, k, g, :], m.ident[:])
                    last.then_inc(turned, 1)
                    pe.wait_ge(copied, it + 1)
                    if which:
                        for k in range(HEADS):
                            last = nc.tensor.matmul(ps_e[:], m.w2[:, k, :], partT[:, k, :], start=k == 0,
                                                    stop=k == HEADS - 1)
                        last.then_inc(mixed, 1)
                        pe.wait_ge(mixed_copied, it + 1)
                    support = sT[:] if which else partT[:, 0, :]
                    h = m.hT[:, bass.ds(it * WIDE, WIDE)]
                    for k in range(2):
                        c = slice(k * D, (k + 1) * D)
                        nc.tensor.matmul(ps_g[k][:], m.wih[:, which, c], support, start=True, stop=False)
                        nc.tensor.matmul(ps_g[k][:], m.whh[:, which, c], h, start=False, stop=True)
                    nc.tensor.matmul(ps_g[2][:], m.wih[:, which, 2 * D:3 * D], support, start=True, stop=True)
                    nc.tensor.matmul(ps_g[3][:], m.whh[:, which, 2 * D:3 * D], h, start=True, stop=True).then_inc(gated, 1)
                    pe.wait_ge(newed, it + 1)
                    for g in range(GROUP):
                        last = nc.tensor.transpose(ps_t[0][:, g * P:(g + 1) * P], new[:, g * P:(g + 1) * P], m.ident[:])
                    last.then_inc(back, 1)

            @block.scalar
            def _(act):
                with act.Fori(0, GROUPS) as it:
                    act.wait_ge(turned, it + 1)
                    for k in range(heads):
                        last = nc.scalar.copy(partT[:, k, :], ps_t[k][:])
                    last.then_inc(copied, 1)
                    if which:
                        act.wait_ge(mixed, it + 1)
                        nc.scalar.mul(sT[:], ps_e[:], 1.0 / HEADS).then_inc(mixed_copied, 1)
                    act.wait_ge(gated, it + 1)
                    nc.scalar.activation(r[:], ps_g[0][:], ACT.Sigmoid, bias=m.bsum[:, which, 0:1])
                    nc.scalar.activation(z[:], ps_g[1][:], ACT.Sigmoid, bias=m.bsum[:, which, 1:2])
                    nc.scalar.activation(hn[:], ps_g[3][:], ACT.Identity, bias=m.bhh[:, which, 2:3]).then_inc(acts, 1)
                    act.wait_ge(gates_read, it + 1)
                    nc.scalar.activation(cand[:], cand[:], ACT.Tanh, bias=m.bih[:, which, 2:3]).then_inc(tanhed, 1)


def stage_select(nc, m, a):
    rounds = -(-TOPK // 8)
    with Stage(nc) as ctx:
        adj, filtered, left = (m.shift2[:, i * N:(i + 1) * N] for i in range(3))
        top = ctx.enter_context(nc.sbuf_tensor("tk_top", [P, 8], F32))
        turned = ctx.enter_context(nc.sbuf_tensor("tk_turned", [P, 4, P], F32))
        ps = ctx.enter_context(nc.psum_tensor("tk_ps", [P, 4, P], F32))
        loaded, squared, tanhed, dv, chosen, turns, copies, stores = (
            ctx.sem("tk_" + x) for x in ("loaded", "squared", "tanhed", "dve", "chosen", "turns", "copies", "stores"))
        blocks = T // 4
        dst = a["selected"].rearrange("(q b j) i -> j q b i", b=4, j=P)
        own = 2 * rounds + 3
        with nc.Block() as block:
            @block.sync
            def _(sp):
                with where(sp, m, CROWDED):
                    with sp.Fori(0, T) as t:
                        sp.wait_ge(turns, t * blocks)
                        sp.nop(nofuse=True)
                        sp.dma_start(adj, a["adj"][bass.ds(t * P, P), :]).then_inc(loaded, 16)
                        for q in range(blocks):
                            sp.wait_ge(copies, t * blocks + (q + 1))
                            sp.nop(nofuse=True)
                            sp.dma_start(dst[:, q:q + 1, :, bass.ds(t * P, P)].rearrange("j o b i -> j (o b) i"),
                                         turned[:]).then_inc(stores, 16)
                    sp.wait_ge(stores, 16 * T * blocks)

            @block.scalar
            def _(act):
                with where(act, m, CROWDED):
                    with act.Fori(0, T) as t:
                        act.wait_ge(squared, t + 1)
                        nc.scalar.activation(filtered, filtered, ACT.Tanh).then_inc(tanhed, 1)
                        for q in range(blocks):
                            act.wait_ge(turns, t * blocks + (q + 1))
                            act.wait_ge(stores, t * (blocks * 16) + q * 16)
                            nc.scalar.copy(turned[:], ps[:]).then_inc(copies, 1)

            @block.tensor
            def _(pe):
                with where(pe, m, CROWDED):
                    with pe.Fori(0, T) as t:
                        pe.wait_ge(chosen, t + 1)
                        for q in range(blocks):
                            pe.wait_ge(copies, t * blocks + q)
                            for b in range(4):
                                last = nc.tensor.transpose(ps[:, b, :], adj[:, (q * 4 + b) * P:(q * 4 + b + 1) * P], m.ident[:])
                            last.then_inc(turns, 1)

            @block.vector
            def _(dve):
                with where(dve, m, CROWDED):
                    with dve.Fori(0, T) as t:
                        dve.wait_ge(loaded, t * 16 + 16)
                        dve.wait_ge(chosen, t)
                        nc.vector.scalar_tensor_tensor(out=filtered, in0=adj, scalar=0.0, in1=adj, op0=ALU.max,
                                                       op1=ALU.mult).then_inc(squared, 1)
                        dve.wait_ge(tanhed, t + 1)
                        nc.vector.tensor_copy(left, filtered).then_inc(dv, 1)
                        dve.wait_ge(dv, t * own + 1)
                        dve.nop(nofuse=True)
                        with dve.Fori(0, rounds - 1) as r:
                            nc.vector.max(out=top[:], in_=left).then_inc(dv, 1)
                            dve.wait_ge(dv, t * own + r * 2 + 2)
                            dve.nop(nofuse=True)
                            nc.vector.match_replace(out=left, in_to_replace=top[:], in_values=left,
                                                    imm_value=-1.0).then_inc(dv, 1)
                            dve.wait_ge(dv, t * own + r * 2 + 3)
                            dve.nop(nofuse=True)
                        nc.vector.max(out=top[:], in_=left).then_inc(dv, 1)
                        dve.wait_ge(dv, t * own + 2 * rounds)
                        nc.vector.memset(top[:, 8 - (8 * rounds - TOPK):8], -2.0).then_inc(dv, 1)
                        dve.wait_ge(dv, t * own + (2 * rounds + 1))
                        dve.nop(nofuse=True)
                        nc.vector.match_replace(out=left, in_to_replace=top[:], in_values=left,
                                                imm_value=-1.0).then_inc(dv, 1)
                        dve.wait_ge(dv, t * own + (2 * rounds + 2))
                        nc.vector.tensor_scalar(left, left, 0.0, None, ALU.is_lt).then_inc(dv, 1)
                        dve.wait_ge(dv, t * own + (2 * rounds + 3))
                        nc.vector.tensor_tensor(adj, adj, left, ALU.mult).then_inc(chosen, 1)


def stage_repack(nc, m, a):
    with Stage(nc) as ctx:
        index = ctx.enter_context(nc.sbuf_tensor("rp_index", [P, PAIR], U32))
        adj = ctx.enter_context(nc.sbuf_tensor("rp_adj", [P, PAIR, P], F32))
        index_ready, gathered, packed = (ctx.sem("rp_" + x) for x in ("index_ready", "gathered", "packed"))
        rows = a["selected"].rearrange("j (t i) -> (j t) i", i=P)
        with nc.Block() as block:
            @block.scalar
            def _(act):
                with where(act, m, CROWDED):
                    n = runs(nc, act, m)
                    with act.Fori(0, n * SETS) as g:
                        act.wait_ge(gathered, g * (16 * PAIR))
                        nc.scalar.copy(index[:], m.index[:, bass.ds(g * PAIR, PAIR), 0]).then_inc(index_ready, 1)

            @block.gpsimd
            def _(pool):
                with where(pool, m, CROWDED):
                    n = runs(nc, pool, m)
                    with pool.Fori(0, n * SETS) as g:
                        pool.wait_ge(index_ready, g + 1)
                        pool.wait_ge(packed, g * 16)
                        pool.nop(nofuse=True)
                        for h in range(PAIR):
                            nc.gpsimd.indirect_dma_start(
                                out=adj[:, h, :], out_offset=None, in_=rows,
                                in_offset=bass.IndirectOffsetOnAxis(ap=index[:, h:h + 1], axis=0)).then_inc(gathered, 16)

            @block.sync
            def _(sp):
                with where(sp, m, CROWDED):
                    n = runs(nc, sp, m)
                    with sp.Fori(0, n * SETS) as g:
                        sp.wait_ge(gathered, (g + 1) * (16 * PAIR))
                        sp.dma_start(a["adj_pack"][:, bass.ds(g, 1), :].rearrange("p o w -> p (o w)"),
                                     adj[:].rearrange("p h i -> p (h i)")).then_inc(packed, 16)
                    sp.wait_ge(packed, n * (SETS * 16))
                    sp.nop(nofuse=True)


def stage_filter_pairs(nc, m, a):
    with Stage(nc) as ctx:
        w = Walk(nc, m, a, "g6", ctx)
        index = w.sb("index", [P, PAIR, 2], U32)
        adj = w.sb("adj", [P, PAIR, P])
        square = w.sb("square", [P, PAIR, P])
        feat = w.sb("feat", [P, PAIR, D])
        ps = w.ps("ps", [P, 512])
        index_ready, gathered, adj_loaded, squared, filtered, summed, added = (
            w.sem(x) for x in ("index_ready", "gathered", "adj_loaded", "squared", "filtered", "summed", "added"))
        with nc.Block() as block:
            @block.gpsimd
            def _(pool):
                n = runs(nc, pool, m)
                with pool.Fori(0, n) as it:
                    for s in range(SETS):
                        pool.wait_ge(index_ready[s], it + 1)
                        pool.wait_ge(summed[s], it)
                        pool.nop(nofuse=True)
                        for h in range(PAIR):
                            nc.gpsimd.indirect_dma_start(
                                out=feat[s][:, h, :], out_offset=None, in_=a["table3"],
                                in_offset=bass.IndirectOffsetOnAxis(ap=index[s][:, h, 1:2], axis=0)).then_inc(gathered[s], 16)

            @block.sync
            def _(sp):
                n = runs(nc, sp, m)
                with sp.Fori(0, n) as it:
                    for s in range(SETS):
                        sp.wait_ge(squared[s], it)
                        sp.dma_start(adj[s][:].rearrange("p h i -> p (h i)"), pair_of(a["adj_pack"], it, s)).then_inc(
                            adj_loaded[s], 16)

            @block.scalar
            def _(act):
                n = runs(nc, act, m)
                with act.Fori(0, n) as it:
                    for s in range(SETS):
                        act.wait_ge(gathered[s], it * (16 * PAIR))
                        nc.scalar.copy(index[s][:], m.index[:, bass.ds((it * SETS + s) * PAIR, PAIR), :]).then_inc(
                            index_ready[s], 1)
                    for s in range(SETS):
                        act.wait_ge(squared[s], it + 1)
                        nc.scalar.activation(square[s][:], square[s][:], ACT.Tanh).then_inc(filtered[s], 1)

            @block.tensor
            def _(pe):
                n = runs(nc, pe, m)
                with pe.Fori(0, n) as it:
                    for s in range(SETS):
                        pe.wait_ge(gathered[s], (it + 1) * (16 * PAIR))
                        pe.wait_ge(filtered[s], it + 1)
                        pe.wait_ge(added[s], it)
                        for h in range(PAIR):
                            last = nc.tensor.matmul(ps[s][:, 0:D], square[s][:, h, :], feat[s][:, h, :],
                                                    start=h == 0, stop=h == PAIR - 1)
                        last.then_inc(summed[s], 1)

            @block.vector
            def _(dve):
                n = runs(nc, dve, m)
                with dve.Fori(0, n) as it:
                    for s in range(SETS):
                        dve.wait_ge(adj_loaded[s], it * 16 + 16)
                        dve.wait_ge(summed[s], it)
                        nc.vector.scalar_tensor_tensor(out=square[s][:], in0=adj[s][:], scalar=0.0, in1=adj[s][:],
                                                       op0=ALU.max, op1=ALU.mult).then_inc(squared[s], 1)
                    tiles = tiles_of_step(nc, dve, m, it)
                    for s in range(SETS):
                        dve.wait_ge(summed[s], it + 1)
                        dve.wait_ge(added[s - 1], it + (s > 0))
                        at = m.acc[:, bass.ds(tiles[s] * D, D)]
                        nc.vector.tensor_tensor(at, at, ps[s][:, 0:D], ALU.add).then_inc(added[s], 1)


def stage_output(nc, m, a):
    with Stage(nc) as ctx:
        step, stored = (ctx.sem("out_" + x) for x in ("step", "stored"))
        parts = 4
        size = T // parts
        out = a["out"].rearrange("(t p) d -> p t d", p=P)
        acc = m.acc[:, 0:T * D].rearrange("p (t d) -> p t d", d=D)
        with nc.Block() as block:
            @block.vector
            def _(dve):
                for c in range(parts):
                    at = slice(c * size, (c + 1) * size)
                    bias = m.bg[:].rearrange("p (o d) -> p o d", o=1).broadcast_to([P, size, D])
                    nc.vector.tensor_tensor(acc[:, at, :], acc[:, at, :], bias, ALU.add).then_inc(step, 1)
                    dve.wait_ge(step, 2 * c + 1)
                    nc.vector.scalar_tensor_tensor(
                        out=m.x[:, at, :].rearrange("p t d -> p (t d)"), in0=acc[:, at, :].rearrange("p t d -> p (t d)"),
                        scalar=0.0, in1=m.x[:, at, :].rearrange("p t d -> p (t d)"), op0=ALU.max,
                        op1=ALU.add).then_inc(step, 1)

            @block.sync
            def _(sp):
                for c in range(parts):
                    at = slice(c * size, (c + 1) * size)
                    sp.wait_ge(step, 2 * c + 2)
                    sp.dma_start(out[:, at, :], m.x[:, at, :]).then_inc(stored, 16)
                sp.wait_ge(stored, 16 * parts)


def stage_clear(nc, m, a, what):
    with Stage(nc) as ctx:
        done = ctx.sem(f"clear_{what}")
        with nc.Block() as block:
            @block.vector
            def _(dve):
                if what == "best":
                    nc.vector.memset(m.best1[:], -BIG).then_inc(done, 1)
                    nc.vector.memset(m.best2[:], -BIG).then_inc(done, 1)
                    nc.vector.memset(m.s1_wide[:, N:N + P], 0.0).then_inc(done, 1)
                    nc.vector.memset(m.shift1[:, N:N + P], BIG).then_inc(done, 1)
                    nc.vector.memset(m.shift2[:, T * HEADS * P:], BIG).then_inc(done, 1)
                else:
                    nc.vector.memset(m.acc[:], 0.0).then_inc(done, 1)


SCRATCH = {
    "selected": (N, N), "table0": (N, 2 * D), "table1": (N, D + 2), "table2": (N, UV_END), "table3": (N, D),
    "score_table": (2 * N, 4), "row_scratch": (T * HEADS * P,),
    "adj_pack": (P, CAP, PAIR * P), "off_pack": (P, CAP, PAIR * P), "wh_pack": (P, CAP, PAIR * (D + 2)),
    "h_pack": (P, CAP, PAIR * UV_END), "score_pack0": (P, CAP, PAIR * 4), "score_pack1": (P, CAP, PAIR * 4),
}


def build(nc, a):
    for name, shape in SCRATCH.items():
        a[name] = nc.dram_tensor("scratch_" + name, shape, F32, kind="Internal").ap()
    with ExitStack() as ctx:
        def sb(name, shape, dt=F32):
            return ctx.enter_context(nc.sbuf_tensor("m_" + name, shape, dt))

        m = Space()
        m.x = sb("x", [P, T, D])
        m.acc = sb("acc", [P, (T + 1) * HEAD_W])
        m.hT = sb("hT", [P, N])
        m.shift2 = sb("shift2", [P, T * HEADS * P + HEADS * P])
        m.s1_wide = m.shift2[:, 0:N + P]
        m.shift1 = m.shift2[:, N + P:2 * (N + P)]
        m.index = sb("index", [P, CAP * PAIR + MAX_PAIRS * PAIR, 2], U32)
        m.relative = sb("relative", [P, CAP * PAIR + MAX_PAIRS * PAIR])
        m.active = sb("active", [P, 4, CLASSES, T])
        m.meta = sb("meta", [1, 4], I32)
        m.tiles = sb("tiles", [1, CAP // SETS], I32)
        m.best1 = sb("best1", [P, T + 1])
        m.best1c = sb("best1c", [P, T])
        m.best2 = sb("best2", [P, T + 1, HEADS])
        m.hsum = sb("hsum", [P, GROUPS])
        m.ident = sb("ident", [P, P])
        m.identb = sb("identb", [P, P], BF16)
        m.ones = sb("ones", [P, P])
        m.row_ramp = sb("row_ramp", [P, P])
        m.class_of = sb("class_of", [P, 1])
        m.class_over = sb("class_over", [P, CLASSES - 1])
        m.sixteens = sb("sixteens", [P, CLASSES - 1])
        m.w0 = sb("w0", [P, 6, D])
        m.wm = sb("wm", [P, 2, D])
        m.b0 = sb("b0", [P, 6])
        m.bm = sb("bm", [1, D])
        m.eps = sb("eps", [P, 2])
        m.w1 = sb("w1", [P, D + 1])
        m.w1t = sb("w1t", [P, D])
        m.a1 = sb("a1", [P, 2])
        m.wa1 = sb("wa1", [P, 1])
        m.wa1_wide = sb("wa1_wide", [P, P])
        m.w2 = sb("w2", [P, HEADS, D])
        m.w2t = sb("w2t", [P, HEADS, D])
        m.a2 = sb("a2", [P, HEADS, 2])
        m.uv = sb("uv", [P, 2 * HEADS])
        m.wih = sb("wih", [P, 2, 3 * D])
        m.whh = sb("whh", [P, 2, 3 * D])
        m.bih = sb("bih", [P, 2, 3])
        m.bhh = sb("bhh", [P, 2, 3])
        m.bsum = sb("bsum", [P, 2, 3])
        m.wp = sb("wp", [P, D])
        m.bp = sb("bp", [P, 1])
        m.wg = sb("wg", [P, D])
        m.bg = sb("bg", [P, D])
        m.diagonal = sb("diagonal", [P, T])

        stage_weights(nc, m, a)
        stage_scan(nc, m, a)
        stage_clear(nc, m, a, "best")
        stage_index(nc, m, a)
        stage_norm(nc, m, a, 0)
        stage_gin_pairs(nc, m, a)
        stage_gin_dense(nc, m, a)
        stage_norm(nc, m, a, 1)
        stage_gat_max(nc, m, a)
        stage_gat_shift(nc, m, a)
        stage_gat_pairs(nc, m, a)
        stage_gat_dense(nc, m, a)
        stage_norm(nc, m, a, 2)
        stage_signed_sums(nc, m, a)
        stage_signed_scores(nc, m, a)
        stage_gru(nc, m, a, 0)
        stage_clear(nc, m, a, "sums")
        stage_signed_max(nc, m, a, 1)
        stage_signed_max(nc, m, a, -1)

        def before(dve, ready):
            nc.vector.tensor_scalar(m.best2c[:], m.best2[:, 0:T, :].rearrange("p t k -> p (t k)"), -0.1 * BIG, None,
                                    ALU.max).then_inc(ready, 1)

        m.best2c = sb("best2c", [P, T * HEADS])
        spread_rows(nc, m, a, "sh2", m.best2c[:], m.shift2[:, 0:T * HEADS * P], a["row_scratch"], T * HEADS, before)
        stage_signed_pairs(nc, m, a, 1)
        stage_signed_pairs(nc, m, a, -1)
        stage_gru(nc, m, a, 1)
        stage_norm(nc, m, a, 3)
        stage_select(nc, m, a)
        stage_repack(nc, m, a)
        stage_filter_pairs(nc, m, a)
        stage_output(nc, m, a)


_AS_THEY_ARE = ["x", "L0_gnn_x2", "L0_gnn_eps1", "L0_gnn_eps2", "L0_gnn_bm", "L1_gnn_W", "L1_gnn_a", "L2_gnn_gat_W",
                "L2_gnn_gat_a", "L3_gnn_W_proj", "L3_gnn_b_proj", "L3_gnn_W_gcn", "L3_gnn_b_gcn"]


def layout(inputs):
    import numpy as _np

    i = {k: _np.asarray(v) for k, v in inputs.items()}
    c = _np.ascontiguousarray
    arrays = {k: c(i[k]) for k in _AS_THEY_ARE}
    arrays["adj"] = c(i["adj"])
    arrays["adjT"] = c(i["adj"].T)
    arrays["adj_diagonal"] = c(_np.diagonal(i["adj"]).reshape(T, P).T)
    arrays["L0_WT"] = c(_np.stack([i["L0_gnn_W1"], i["L0_gnn_W2"]]).transpose(0, 1, 3, 2))
    arrays["L0_bT"] = c(_np.stack([i["L0_gnn_b1"], i["L0_gnn_b2"]]))
    arrays["L0_WmT"] = c(i["L0_gnn_Wm"].T)
    arrays["L1_WT"] = c(i["L1_gnn_W"].T)
    arrays["L2_WT"] = c(i["L2_gnn_gat_W"].transpose(0, 2, 1))
    arrays["L2_WihT"] = c(_np.stack([i["L2_gnn_edge_Wih"].T, i["L2_gnn_node_Wih"].T]))
    arrays["L2_WhhT"] = c(_np.stack([i["L2_gnn_edge_Whh"].T, i["L2_gnn_node_Whh"].T]))
    arrays["L2_bih"] = c(_np.stack([i["L2_gnn_edge_bih"], i["L2_gnn_node_bih"]]))
    arrays["L2_bhh"] = c(_np.stack([i["L2_gnn_edge_bhh"], i["L2_gnn_node_bhh"]]))
    return arrays


def kernel(**inputs):
    import concourse.bacc as _bacc
    from concourse import mybir as _mybir
    from concourse.bass_utils import run_bass_kernel_spmd as _run

    nc = _bacc.Bacc("TRN2", target_bir_lowering=False, num_devices=1)
    arrays = {f"in_{k}_dram": v for k, v in layout(inputs).items()}
    args = {k[3:-5]: nc.dram_tensor(k, v.shape, _mybir.dt.from_np(v.dtype), kind="ExternalInput").ap()
            for k, v in arrays.items()}
    args["out"] = nc.dram_tensor("out_0_dram", (N, D), F32, kind="ExternalOutput").ap()
    build(nc, args)
    r = _run(nc, [arrays], core_ids=[0])
    return r.results[0]["out_0_dram"]
```

```python
from contextlib import ExitStack, contextmanager

import concourse.bass as bass
from concourse import mybir

F32 = mybir.dt.float32
BF16 = mybir.dt.bfloat16
I32 = mybir.dt.int32
U32 = mybir.dt.uint32
ALU = mybir.AluOpType
ACT = mybir.ActivationFunctionType
AX = mybir.AxisListType

N = 4096
D = 128
P = 128
T = N // P
CLASSES = 8
QUARTERS = 4
SIDES = 2
JJ = N // CLASSES
PAIR = 2
TAKEN = PAIR * P // CLASSES
MAX_PAIRS = JJ // TAKEN
CAP = T * MAX_PAIRS
SETS = 4
HEADS = 3
GROUP = 4
GROUPS = T // GROUP
WIDE = GROUP * P
ALPHA = 0.2
EPS = 1e-5
BIG = 1e30
TOPK = 350
BLOCKS = N // P
STEPS, ROUNDS, NEGATIVES, CROWDED, LAST = range(5)


UV_END = D + 2 * HEADS + 1
SIGN_W = UV_END - D
SUPPORT_W = D + 2 * SIGN_W
HEAD_W = HEADS * (D + 1)


class Space:
    pass


class Stage(ExitStack):

    def __init__(self, nc):
        super().__init__()
        self.nc, self.sems = nc, []

    def sem(self, name):
        self.sems.append(self.nc.alloc_semaphore(name=name))
        return self.sems[-1]

    def __exit__(self, *exc):
        if exc[0] is None:
            self.nc.clear_and_free_semaphores(self.sems)
            self.nc.all_engine_barrier()
        return super().__exit__(*exc)


def runs(nc, eng, m):
    return eng.value_load(m.meta[0:1, STEPS:STEPS + 1], min_val=1, max_val=CAP // SETS)


def last_run(nc, eng, m):
    return eng.value_load(m.meta[0:1, LAST:LAST + 1], min_val=T // SETS - 1, max_val=CAP // SETS - 1)


@contextmanager
def where(eng, m, flag):
    if flag is None:
        yield
        return
    with eng.If(eng.value_load(m.meta[0:1, flag:flag + 1], min_val=0, max_val=1) > 0):
        yield
        eng.nop(nofuse=True)


def tiles_of_step(nc, eng, m, step):
    word = eng.value_load(m.tiles[0:1, bass.ds(step, 1)], min_val=0, max_val=(1 << 24) - 1)
    return [nc.s_assert_within(eng.snap((word >> (6 * s)) & 63), 0, T,
                               skip_runtime_bounds_check_because="the table holds 0 to T") for s in range(SETS)]


def stage_weights(nc, m, a):
    with Stage(nc) as ctx:
        loaded = ctx.sem("w_loaded")
        identity_step = ctx.sem("w_identity_step")
        folded = ctx.sem("w_folded")
        vec = ctx.sem("w_vector")
        copied = ctx.sem("w_copied")
        ps = ctx.enter_context(nc.psum_tensor("w_ps", [P, 8], F32))
        loads = [
            (m.x, a["x"].rearrange("(t p) d -> p t d", p=P)),
            (m.w0, a["L0_WT"].rearrange("b l i o -> i (b l) o")),
            (m.wm, a["L0_WmT"].rearrange("(b i) o -> i b o", b=2)),
            (m.b0, a["L0_bT"].rearrange("b l d -> d (b l)")),
            (m.bm, a["L0_gnn_bm"].rearrange("(a d) -> a d", a=1)),
            (m.eps[:, 0:1], a["L0_gnn_eps1"].rearrange("(a d) -> a d", a=1).broadcast_to([P, 1])),
            (m.eps[:, 1:2], a["L0_gnn_eps2"].rearrange("(a d) -> a d", a=1).broadcast_to([P, 1])),
            (m.w1[:, 0:D], a["L1_gnn_W"]),
            (m.w1t, a["L1_WT"]),
            (m.a1, a["L1_gnn_a"].rearrange("(s d) o -> d (s o)", s=2)),
            (m.w2, a["L2_gnn_gat_W"].rearrange("k i o -> i k o")),
            (m.w2t, a["L2_WT"].rearrange("k o i -> o k i")),
            (m.a2, a["L2_gnn_gat_a"].rearrange("k (s d) o -> d k (s o)", s=2)),
            (m.wih, a["L2_WihT"].rearrange("g i o -> i g o")),
            (m.whh, a["L2_WhhT"].rearrange("g i o -> i g o")),
            (m.bih, a["L2_bih"].rearrange("g (c d) -> d g c", d=D)),
            (m.bhh, a["L2_bhh"].rearrange("g (c d) -> d g c", d=D)),
            (m.wp, a["L3_gnn_W_proj"]),
            (m.bp, a["L3_gnn_b_proj"].rearrange("(d a) -> d a", a=1)),
            (m.wg, a["L3_gnn_W_gcn"]),
            (m.bg, a["L3_gnn_b_gcn"].rearrange("(a d) -> a d", a=1).broadcast_to([P, D])),
            (m.diagonal, a["adj_diagonal"]),
            (a["table0"][:, D:2 * D], a["L0_gnn_x2"]),
        ]
        with nc.Block() as block:
            @block.sync
            def _(sp):
                with nc.allow_non_contiguous_dma(reason="biases and the diagonal, once"):
                    for dst, src in loads:
                        sp.dma_start(dst if isinstance(dst, bass.AP) else dst[:], src).then_inc(loaded, 16)
                sp.wait_ge(loaded, 16 * len(loads))

            @block.gpsimd
            def _(pool):
                nc.gpsimd.memset(m.ident[:], 0.0).then_inc(identity_step, 1)
                pool.wait_ge(identity_step, 1)
                nc.gpsimd.affine_select(out=m.ident[:], in_=m.ident[:], compare_op=ALU.not_equal, fill=1.0,
                                        base=0, pattern=[[-1, P]], channel_multiplier=1).then_inc(identity_step, 1)
                nc.gpsimd.memset(m.identb[:], 0.0).then_inc(identity_step, 1)
                pool.wait_ge(identity_step, 3)
                nc.gpsimd.affine_select(out=m.identb[:], in_=m.identb[:], compare_op=ALU.not_equal, fill=1.0,
                                        base=0, pattern=[[-1, P]], channel_multiplier=1).then_inc(identity_step, 1)

            @block.tensor
            def _(pe):
                pe.wait_ge(loaded, 16 * len(loads))
                nc.tensor.matmul(ps[:, 0:2], m.w1t[:], m.a1[:], start=True, stop=True)
                for k in range(HEADS):
                    last = nc.tensor.matmul(ps[:, 2 + 2 * k:4 + 2 * k], m.w2t[:, k, :], m.a2[:, k, :],
                                            start=True, stop=True)
                last.then_inc(folded, 1)

            @block.vector
            def _(dve):
                nc.vector.memset(m.ones[:], 1.0).then_inc(vec, 1)
                dve.wait_ge(loaded, 16 * len(loads))
                dve.wait_ge(folded, 1)
                nc.vector.tensor_copy(m.w1[:, D:D + 1], ps[:, 1:2]).then_inc(vec, 1)
                nc.vector.tensor_copy(m.uv[:], ps[:, 2:8]).then_inc(vec, 1)
                nc.vector.tensor_copy(m.wa1[:], ps[:, 0:1]).then_inc(copied, 1)
                dve.wait_ge(vec, 3)
                dve.wait_ge(copied, 1)
                nc.vector.tensor_scalar(m.wa1_wide[:], m.ones[:], m.wa1[:, 0:1], None, ALU.mult).then_inc(vec, 1)
                nc.vector.tensor_scalar(m.eps[:], m.eps[:], 2.0, None, ALU.add).then_inc(vec, 1)
                nc.vector.tensor_tensor(m.bsum[:], m.bih[:], m.bhh[:], ALU.add).then_inc(vec, 1)


def stage_scan(nc, m, a):
    with Stage(nc) as ctx:
        ring = [m.acc[:, b * N:(b + 1) * N] for b in range(3)] + [m.shift2[:, 0:N]]
        loaded = [ctx.sem(f"scan_loaded{i}") for i in range(4)]
        reduced = [ctx.sem(f"scan_reduced{i}") for i in range(4)]
        src = a["adjT"].rearrange("(part p c) i -> c part p i", part=4, c=CLASSES)
        with nc.Block() as block:
            @block.sync
            def _(sp):
                with sp.Fori(0, CLASSES) as c:
                    for part in range(4):
                        sp.wait_ge(reduced[part], c)
                        sp.dma_start(ring[part], src[bass.ds(c, 1), part, :, :].rearrange("c p i -> p (c i)")
                                     ).then_inc(loaded[part], 16)

            @block.vector
            def _(dve):
                with dve.Fori(0, CLASSES) as c:
                    for part in range(4):
                        dve.wait_ge(loaded[part], 16 * c + 16)
                        nc.vector.tensor_reduce(
                            m.active[:, part, bass.ds(c, 1), :], ring[part].rearrange("p (t i) -> p t i", i=P),
                            AX.X, ALU.max, apply_absolute_value=True).then_inc(reduced[part], 1)


def stage_index(nc, m, a):
    with Stage(nc) as ctx:
        def sb(name, shape, dt=F32):
            return ctx.enter_context(nc.sbuf_tensor("ix_" + name, shape, dt))

        def sem(name):
            return ctx.sem("ix_" + name)

        flags = sb("flags", [P, 4, SIDES, P], BF16)
        ramp = sb("ramp", [P, SIDES, JJ])
        keys = sb("keys", [P, SIDES, JJ])
        step32 = sb("step32", [P, MAX_PAIRS])
        counts = sb("counts", [P, SIDES])
        most = sb("most", [P, 1])
        over = sb("over", [P, MAX_PAIRS])
        pairs_of_list = sb("pairs_of_list", [P, 1])
        pairs = sb("pairs", [1, T])
        ends = sb("ends", [1, 2, T])
        starts = sb("starts", [1, T])
        starts_i = sb("starts_i", [1, T], I32)
        step4 = sb("step4", [1, CAP // SETS])
        over4 = sb("over4", [1, CAP // SETS])
        meta_f = sb("meta_f", [1, 2])
        ends_col = sb("ends_col", [T, 1])
        pair_ramp = sb("pair_ramp", [T, CAP])
        passed = sb("passed", [T, CAP])
        packed = sb("packed", [1, CAP // SETS])
        taken = sb("taken", [P, PAIR, SIDES, TAKEN // PAIR])
        turned = sb("turned", [P, PAIR, SIDES * TAKEN // PAIR])
        lists = sb("lists", [P, MAX_PAIRS * PAIR, T])
        high = sb("high", [P, MAX_PAIRS * PAIR, T])
        tile_ramp = sb("tile_ramp", [P, MAX_PAIRS * PAIR, T])
        offset = sb("offset", [P, 1])
        ps_keys = ctx.enter_context(nc.psum_tensor("ix_ps_keys", [P, SIDES, JJ], F32))
        ps_small = ctx.enter_context(nc.psum_tensor("ix_ps_small", [P, 512], F32))
        ps_tiles = ctx.enter_context(nc.psum_tensor("ix_ps_tiles", [P, CAP], F32))
        pool_step, flagged, keyed, listed, row, col, col_done, tiled, dv = (
            sem(x) for x in ("pool_step", "flagged", "keyed", "listed", "row", "col", "col_done", "tiled", "dve_step"))
        took = sem("took")
        copied = sem("copied")

        with nc.Block() as block:
            @block.gpsimd
            def _(pool):
                nc.gpsimd.iota(ramp[:], pattern=[[0, SIDES], [-1, JJ]], base=JJ - 1, channel_multiplier=0,
                               allow_small_or_imprecise_dtypes=True).then_inc(pool_step, 1)
                nc.gpsimd.iota(step32[:], pattern=[[TAKEN, MAX_PAIRS]], base=0, channel_multiplier=0,
                               allow_small_or_imprecise_dtypes=True).then_inc(pool_step, 1)
                nc.gpsimd.iota(step4[:], pattern=[[SETS, CAP // SETS]], base=0, channel_multiplier=0,
                               allow_small_or_imprecise_dtypes=True).then_inc(pool_step, 1)
                nc.gpsimd.iota(pair_ramp[:], pattern=[[1, CAP]], base=0, channel_multiplier=0,
                               allow_small_or_imprecise_dtypes=True).then_inc(pool_step, 1)
                nc.gpsimd.iota(tile_ramp[:], pattern=[[0, MAX_PAIRS * PAIR], [1, T]], base=0, channel_multiplier=0,
                               allow_small_or_imprecise_dtypes=True).then_inc(pool_step, 1)
                nc.gpsimd.iota(m.row_ramp[:], pattern=[[1, P]], base=0, channel_multiplier=0,
                               allow_small_or_imprecise_dtypes=True).then_inc(pool_step, 1)
                nc.gpsimd.iota(m.class_of[:], pattern=[[0, 1]], base=0, channel_multiplier=1,
                               allow_small_or_imprecise_dtypes=True).then_inc(pool_step, 1)
                nc.gpsimd.iota(m.sixteens[:], pattern=[[16, CLASSES - 1]], base=16, channel_multiplier=0,
                               allow_small_or_imprecise_dtypes=True).then_inc(pool_step, 1)

            @block.tensor
            def _(pe):
                pe.wait_ge(flagged, 1)
                for side in range(SIDES):
                    for part in range(4):
                        last = nc.tensor.matmul(ps_keys[:, side, part * P:(part + 1) * P], flags[:, part, side, :],
                                                m.identb[:], start=True, stop=True)
                last.then_inc(keyed, 1)
                pe.wait_ge(listed, 1)
                nc.tensor.matmul(ps_small[0:1, 0:P], pairs_of_list[:], m.ident[:], start=True, stop=True).then_inc(row, 1)
                pe.wait_ge(col, 1)
                nc.tensor.matmul(ps_small[0:T, 128:129], ends[:, 1, :], m.ones[0:1, 0:1], start=True,
                                 stop=True).then_inc(col_done, 1)
                pe.wait_ge(tiled, 1)
                nc.tensor.matmul(ps_tiles[0:1, :], m.ones[0:T, 0:1], passed[:], start=True, stop=True).then_inc(tiled, 1)

            @block.vector
            def _(dve):
                steps = [0]

                def done(ins):
                    steps[0] += 1
                    ins.then_inc(dv, 1)
                    dve.wait_ge(dv, steps[0])

                dve.wait_ge(pool_step, 8)
                done(nc.vector.tensor_scalar(m.class_over[:], m.sixteens[:], m.class_of[:, 0:1], None, ALU.is_le))
                done(nc.vector.tensor_reduce(m.class_of[:], m.class_over[:], AX.X, ALU.add))
                by_side = m.active[:].rearrange("p a (q s) t -> p a s q t", s=SIDES)
                for side in range(SIDES):
                    last = nc.vector.tensor_scalar(
                        flags[:, :, side, :].rearrange("p a (q t) -> p a q t", q=QUARTERS), by_side[:, :, side, :, :],
                        0.0, None, ALU.is_gt)
                last.then_inc(flagged, 1)
                dve.wait_ge(keyed, 1)
                done(nc.vector.scalar_tensor_tensor(out=keys[:], in0=ps_keys[:], scalar=2.0 * JJ, in1=ramp[:],
                                                    op0=ALU.mult, op1=ALU.add))
                done(nc.vector.tensor_reduce(counts[:], ps_keys[:], AX.X, ALU.add))
                done(nc.vector.tensor_reduce(most[:], counts[:], AX.X, ALU.max))
                done(nc.vector.tensor_scalar(over[:], step32[:], most[:, 0:1], None, ALU.is_lt))
                nc.vector.tensor_reduce(pairs_of_list[:], over[:], AX.X, ALU.add).then_inc(listed, 1)
                dve.wait_ge(row, 1)
                done(nc.vector.tensor_reduce(pairs[:], ps_small[0:1, 0:P].rearrange("o (q t) -> o t q", q=QUARTERS),
                                             AX.X, ALU.max))
                done(nc.vector.tensor_scalar(pairs[:], pairs[:], 1.0, None, ALU.max))
                done(nc.vector.tensor_reduce(meta_f[:, 1:2], pairs[:], AX.X, ALU.max))
                done(nc.vector.tensor_copy(ends[:, 0, :], pairs[:]))
                src = 0
                for shift in (1, 2, 4, 8, 16):
                    dst = 1 - src
                    done(nc.vector.tensor_copy(ends[:, dst, 0:shift], ends[:, src, 0:shift]))
                    done(nc.vector.tensor_tensor(ends[:, dst, shift:T], ends[:, src, shift:T],
                                                 ends[:, src, 0:T - shift], ALU.add))
                    src = dst
                nc.vector.tensor_tensor(starts[:], ends[:, 1, :], pairs[:], ALU.subtract).then_inc(col, 1)
                dve.wait_ge(col, 1)
                done(nc.vector.tensor_copy(starts_i[:], starts[:]))
                done(nc.vector.tensor_scalar(over4[:], step4[:], ends[:, 1, T - 1:T], None, ALU.is_lt))
                done(nc.vector.tensor_reduce(meta_f[:, 0:1], over4[:], AX.X, ALU.add))
                done(nc.vector.tensor_copy(m.meta[:, 0:2], meta_f[:]))
                done(nc.vector.tensor_scalar(m.meta[:, LAST:LAST + 1], meta_f[:, 0:1], -1.0, None, ALU.add))
                dve.wait_ge(col_done, 1)
                done(nc.vector.tensor_copy(ends_col[:], ps_small[0:T, 128:129]))
                nc.vector.tensor_scalar(passed[:], pair_ramp[:], ends_col[:, 0:1], None, ALU.is_ge).then_inc(tiled, 1)
                dve.wait_ge(tiled, 2)
                by_set = ps_tiles[0:1, :].rearrange("o (n s) -> o s n", s=SETS)
                done(nc.vector.tensor_copy(packed[:], by_set[:, 0, :]))
                for s in range(1, SETS):
                    done(nc.vector.scalar_tensor_tensor(out=packed[:], in0=by_set[:, s, :], scalar=float(64 ** s),
                                                        in1=packed[:], op0=ALU.mult, op1=ALU.add))
                done(nc.vector.tensor_copy(m.tiles[:], packed[:]))
                done(nc.vector.memset(lists[:], 0.0))
                half = TAKEN // PAIR
                rounds = dve.value_load(m.meta[0:1, ROUNDS:ROUNDS + 1], min_val=1, max_val=MAX_PAIRS)
                per_round = 2 * PAIR * SIDES * (half // 8) + 1
                with dve.Fori(0, rounds) as r:
                    k = 0
                    for part in range(TAKEN // 8):
                        h, e = divmod(part * 8, half)
                        for side in range(SIDES):
                            nc.vector.max(out=taken[:, h, side, e:e + 8], in_=keys[:, side, :]).then_inc(took, 1)
                        k += SIDES
                        dve.wait_ge(took, r * per_round + k)
                        dve.nop(nofuse=True)
                        for side in range(SIDES):
                            nc.vector.match_replace(out=keys[:, side, :], in_to_replace=taken[:, h, side, e:e + 8],
                                                    in_values=keys[:, side, :], imm_value=-1.0).then_inc(took, 1)
                        k += SIDES
                        dve.wait_ge(took, r * per_round + k)
                        dve.nop(nofuse=True)
                    for h in range(PAIR):
                        last = nc.vector.transpose(turned[:, h, :], taken[:, h, :, :].rearrange("p s e -> p (s e)"))
                    last.then_inc(took, 1)
                    dve.wait_ge(took, r * per_round + k + 1)
                    nc.vector.tensor_copy(lists[:, bass.ds(r * PAIR, PAIR), :], turned[:]).then_inc(copied, 1)
                    dve.wait_ge(copied, r + 1)
                flat = lists[:]
                done(nc.vector.tensor_scalar(high[:], flat, 2.0 * JJ, -2.0 * JJ, ALU.is_ge, ALU.mult))
                done(nc.vector.tensor_tensor(flat, flat, high[:], ALU.add))
                done(nc.vector.tensor_scalar(offset[:], m.class_of[:], float(CLASSES * (JJ - 1)), None, ALU.add))
                done(nc.vector.tensor_scalar(flat, flat, -float(CLASSES), offset[:, 0:1], ALU.mult, ALU.add))
                done(nc.vector.scalar_tensor_tensor(out=high[:], in0=flat, scalar=float(T), in1=tile_ramp[:],
                                                    op0=ALU.mult, op1=ALU.add))
                done(nc.vector.scalar_tensor_tensor(out=tile_ramp[:], in0=tile_ramp[:], scalar=-float(P), in1=flat,
                                                    op0=ALU.mult, op1=ALU.add))
                done(nc.vector.memset(m.index[:], 0))
                done(nc.vector.memset(m.relative[:], 0.0))
                base = steps[0]
                with dve.Fori(0, T) as t:
                    start = dve.value_load(starts_i[0:1, bass.ds(t, 1)], min_val=0, max_val=CAP - 1)
                    length = MAX_PAIRS * PAIR
                    for kind, what in ((0, high), (1, flat)):
                        nc.vector.tensor_copy(
                            m.index[:, bass.ds(start * PAIR, length), kind:kind + 1],
                            what[:, :, bass.ds(t, 1)]).then_inc(dv, 1)
                    nc.vector.tensor_copy(m.relative[:, bass.ds(start * PAIR, length)],
                                          tile_ramp[:, :, bass.ds(t, 1)].rearrange("p l o -> p (l o)")).then_inc(dv, 1)
                    dve.wait_ge(dv, t * 3 + (base + 3))


def stage_norm(nc, m, a, layer):
    with Stage(nc) as ctx:
        def sb(name, shape, dt=F32):
            return [ctx.enter_context(nc.sbuf_tensor(f"n{layer}_{name}{u}", shape, dt)) for u in range(2)]

        def sem(name):
            return [ctx.sem(f"n{layer}_{name}{u}") for u in range(2)]

        width = {0: D, 1: D + 2, 2: UV_END, 3: D}[layer]
        stats = sb("stats", [P, GROUP, nc.vector.BN_STATS_DIM])
        moments = sb("moments", [P, GROUP, nc.vector.BN_AGGR_DIM])
        root = sb("root", [P, GROUP])
        scale = sb("scale", [P, GROUP])
        shift = sb("shift", [P, GROUP])
        rows = sb("rows", [P, GROUP, width])
        hrow = sb("hrow", [P, GROUP, D]) if layer in (1, 3) else rows
        hT = sb("hT", [P, WIDE])
        h2T = sb("h2T", [P, WIDE]) if layer == 3 else None
        ps_t = [ctx.enter_context(nc.psum_tensor(f"n{layer}_ps_t{u}", [P, WIDE], F32)) for u in range(2)]
        ps_w = [ctx.enter_context(nc.psum_tensor(f"n{layer}_ps_w{u}", [P, GROUP, 256 if layer == 1 else 128], F32))
                for u in range(2)]
        ps_s = ([ctx.enter_context(nc.psum_tensor(f"n{layer}_ps_s{u}", [P, WIDE], F32)) for u in range(2)]
                if layer in (1, 3) else None)
        ones_set = ctx.sem(f"n{layer}_ones_set")
        dv, rooted, scaled, normed, turned, hT_ready, projected, rows_ready, stored, s_done, s_read, h2_ready = (
            sem(x) for x in ("dve", "rooted", "scaled", "normed", "turned", "hT_ready", "projected", "rows_ready",
                             "stored", "s_done", "s_read", "h2_ready"))
        table = {0: "table0", 1: "table1", 2: "table2", 3: "table3"}[layer]
        dst = a[table].rearrange("(t p) w -> p t w", p=P)
        steps = GROUPS // 2

        acc_clear = m.acc[:]

        def tiles(tensor, it, u):
            return tensor[:, bass.ds(it * (2 * GROUP) + u * GROUP, GROUP), :]

        with nc.Block() as block:
            @block.gpsimd
            def _(pool):
                nc.gpsimd.memset(acc_clear, 0.0)

            @block.vector
            def _(dve):
                if layer in (1, 2):
                    for u in range(2):
                        one = D if layer == 1 else UV_END - 1
                        nc.vector.memset(rows[u][:, :, one:one + 1], 1.0).then_inc(ones_set, 1)
                    dve.wait_ge(ones_set, 2)
                with dve.Fori(0, steps) as it:
                    def finish(u, it):
                        if layer == 0:
                            return
                        dve.wait_ge(projected[u], it + 1)
                        if layer in (1, 3):
                            dve.wait_ge(stored[u], 16 * it)
                        if layer == 1:
                            nc.vector.tensor_copy(rows[u][:, :, 0:D], ps_w[u][:, :, 0:D]).then_inc(rows_ready[u], 1)
                            nc.vector.tensor_copy(rows[u][:, :, D + 1:D + 2], ps_w[u][:, :, D:D + 1]).then_inc(
                                rows_ready[u], 1)
                            nc.vector.tensor_reduce(m.hsum[:, bass.ds(it * 2 + u, 1)], hT[u][:], AX.X, ALU.add
                                                    ).then_inc(rows_ready[u], 1)
                        elif layer == 2:
                            nc.vector.tensor_copy(rows[u][:, :, D:D + 2 * HEADS], ps_w[u][:, :, 0:2 * HEADS]).then_inc(
                                rows_ready[u], 1)
                        else:
                            nc.vector.tensor_copy(rows[u][:], ps_w[u][:]).then_inc(rows_ready[u], 1)

                    own = 4
                    for u in range(2):
                        dve.wait_ge(normed[u], it)
                        for i in range(GROUP):
                            last = nc.vector.bn_stats(stats[u][:, i, :], m.x[:, bass.ds(it * (2 * GROUP) + u * GROUP + i, 1), :]
                                                      .rearrange("p o d -> p (o d)"))
                        last.then_inc(dv[u], 1)
                        dve.wait_ge(dv[u], it * own + 1)
                        dve.nop(nofuse=True)
                        for i in range(GROUP):
                            last = nc.vector.bn_aggr(moments[u][:, i, :], stats[u][:, i, :])
                        last.then_inc(dv[u], 1)
                        dve.wait_ge(dv[u], it * own + 2)
                        nc.vector.tensor_scalar(scale[u][:], moments[u][:, :, 1], EPS, None, ALU.add).then_inc(dv[u], 1)
                        dve.wait_ge(rooted[u], it + 1)
                        nc.vector.reciprocal(scale[u][:], root[u][:]).then_inc(dv[u], 1)
                        dve.wait_ge(dv[u], it * own + 4)
                        nc.vector.scalar_tensor_tensor(out=shift[u][:], in0=moments[u][:, :, 0], scalar=-1.0,
                                                       in1=scale[u][:], op0=ALU.mult, op1=ALU.mult).then_inc(scaled[u], 1)
                        if u:
                            finish(0, it)
                    finish(1, it)

            @block.scalar
            def _(act):
                with act.Fori(0, steps) as it:
                    def root_of(u):
                        act.wait_ge(dv[u], it * 4 + 3)
                        nc.scalar.activation(root[u][:], scale[u][:], ACT.Sqrt).then_inc(rooted[u], 1)

                    def norm(u):
                        act.wait_ge(scaled[u], it + 1)
                        if layer in (0, 2):
                            act.wait_ge(stored[u], 16 * it)
                        if layer:
                            act.wait_ge(turned[u], it)
                        for i in range(GROUP):
                            last = nc.scalar.activation(
                                hrow[u][:, i, 0:D],
                                m.x[:, bass.ds(it * (2 * GROUP) + u * GROUP + i, 1), :].rearrange("p o d -> p (o d)"),
                                ACT.Relu, bias=shift[u][:, i:i + 1], scale=scale[u][:, i:i + 1])
                        last.then_inc(normed[u], 1)

                    def turn(u):
                        act.wait_ge(turned[u], it + 1)
                        if layer:
                            act.wait_ge(projected[u], it)
                        if layer == 1:
                            act.wait_ge(s_done[u], it)
                            act.wait_ge(rows_ready[u], 3 * it)
                        nc.scalar.copy(hT[u][:], ps_t[u][:]).then_inc(hT_ready[u], 1)
                        if layer == 2:
                            nc.scalar.copy(m.hT[:, bass.ds(it * (2 * WIDE) + u * WIDE, WIDE)], ps_t[u][:]).then_inc(
                                hT_ready[u], 1)
                        if layer == 1:
                            act.wait_ge(s_done[u], it + 1)
                            nc.scalar.copy(m.s1_wide[:, bass.ds(it * (2 * WIDE) + u * WIDE, WIDE)], ps_s[u][:]).then_inc(
                                s_read[u], 1)
                        if layer == 3:
                            act.wait_ge(s_done[u], it + 1)
                            nc.scalar.activation(h2T[u][:], ps_s[u][:], ACT.Tanh, bias=m.bp[:, 0:1]).then_inc(
                                h2_ready[u], 1)

                    root_of(0)
                    norm(0)
                    root_of(1)
                    norm(1)
                    if layer:
                        turn(0)
                        turn(1)

            @block.tensor
            def _(pe):
                if layer == 0:
                    return
                with pe.Fori(0, steps) as it:
                    for u in range(2):
                        pe.wait_ge(normed[u], it + 1)
                        pe.wait_ge(hT_ready[u], (2 if layer == 2 else 1) * it)
                        for i in range(GROUP):
                            last = nc.tensor.transpose(ps_t[u][:, i * P:(i + 1) * P], hrow[u][:, i, 0:D], m.ident[:])
                        last.then_inc(turned[u], 1)
                    for u in range(2):
                        pe.wait_ge(hT_ready[u], (2 if layer == 2 else 1) * it + 1)
                        if layer == 1:
                            pe.wait_ge(s_read[u], it)
                            nc.tensor.matmul(ps_s[u][:], m.wa1_wide[:], hT[u][:], start=True, stop=True).then_inc(
                                s_done[u], 1)
                            pe.wait_ge(rows_ready[u], 3 * it)
                            for i in range(GROUP):
                                last = nc.tensor.matmul(ps_w[u][:, i, 0:D + 1], hT[u][:, i * P:(i + 1) * P], m.w1[:],
                                                        start=True, stop=True)
                        elif layer == 2:
                            pe.wait_ge(rows_ready[u], it)
                            for i in range(GROUP):
                                last = nc.tensor.matmul(ps_w[u][:, i, 0:2 * HEADS], hT[u][:, i * P:(i + 1) * P],
                                                        m.uv[:], start=True, stop=True)
                        else:
                            pe.wait_ge(h2_ready[u], it)
                            nc.tensor.matmul(ps_s[u][:], m.wp[:], hT[u][:], start=True, stop=True).then_inc(
                                s_done[u], 1)
                            pe.wait_ge(h2_ready[u], it + 1)
                            pe.wait_ge(rows_ready[u], it)
                            for i in range(GROUP):
                                last = nc.tensor.matmul(ps_w[u][:, i, :], h2T[u][:, i * P:(i + 1) * P], m.wg[:],
                                                        start=True, stop=True)
                        last.then_inc(projected[u], 1)

            @block.sync
            def _(sp):
                with sp.Fori(0, steps) as it:
                    for u in range(2):
                        if layer == 0:
                            sp.wait_ge(normed[u], it + 1)
                        else:
                            sp.wait_ge(rows_ready[u], (it + 1) * (3 if layer == 1 else 1))
                        sp.dma_start(tiles(dst, it, u)[:, :, 0:width], rows[u][:]).then_inc(stored[u], 16)
                for u in range(2):
                    sp.wait_ge(stored[u], 16 * steps)


class Walk:

    def __init__(self, nc, m, a, name, ctx):
        self.nc, self.m, self.a, self.name, self.ctx = nc, m, a, name, ctx

    def sb(self, name, shape, dt=F32, sets=SETS):
        return [self.ctx.enter_context(self.nc.sbuf_tensor(f"{self.name}_{name}{s}", shape, dt)) for s in range(sets)]

    def halves(self, name, shape, dt=F32):
        return self.ctx.enter_context(self.nc.sbuf_tensor(f"{self.name}_{name}", [P, 2] + shape, dt))

    def ps(self, name, shape, sets=SETS):
        return [self.ctx.enter_context(self.nc.psum_tensor(f"{self.name}_{name}{s}", shape, F32)) for s in range(sets)]

    def sem(self, name, sets=SETS):
        return [self.ctx.sem(f"{self.name}_{name}{s}") for s in range(sets)]


def pair_of(tensor, it, s):
    return tensor[:, bass.ds(it * SETS + s, 1), :].rearrange("p o w -> p (o w)")


def step_of(tensor, it):
    return tensor[:, bass.ds(it * SETS, SETS), :].rearrange("p s w -> p (s w)")


def half_of(buffer, it):
    return buffer[:, bass.ds(it & 1, 1), :, :, :].rearrange("p o s h w -> p (o s h w)")


def pair_in(buffer, it, s):
    return buffer[:, bass.ds(it & 1, 1), s:s + 1, :, :].rearrange("p a b h w -> p (a b h) w")


def stage_gin_pairs(nc, m, a):
    with Stage(nc) as ctx:
        w = Walk(nc, m, a, "g0", ctx)
        index = w.sb("index", [P, PAIR, 2], U32)
        adj = w.sb("adj", [P, PAIR, P])
        off = w.sb("off", [P, PAIR, P])
        feat = w.sb("feat", [P, PAIR, 2 * D])
        ps = w.ps("ps", [P, 512])
        index_ready, gathered, summed, off_ready, packed, off_packed, added = (
            w.sem(x) for x in ("index_ready", "gathered", "summed", "off_ready", "packed", "off_packed", "added"))
        gathers = 16 * 2 * PAIR
        adj_rows = a["adjT"].rearrange("j (t i) -> (j t) i", i=P)
        with nc.Block() as block:
            @block.scalar
            def _(act):
                n = runs(nc, act, m)
                with act.Fori(0, n) as it:
                    for s in range(SETS):
                        act.wait_ge(gathered[s], it * gathers)
                        nc.scalar.copy(index[s][:], m.index[:, bass.ds((it * SETS + s) * PAIR, PAIR), :]).then_inc(
                            index_ready[s], 1)

            @block.gpsimd
            def _(pool):
                n = runs(nc, pool, m)
                with pool.Fori(0, n) as it:
                    for s in range(SETS):
                        pool.wait_ge(index_ready[s], it + 1)
                        pool.wait_ge(summed[s], it)
                        pool.wait_ge(off_ready[s], it)
                        pool.wait_ge(packed[s], 16 * it)
                        pool.nop(nofuse=True)
                        for h in range(PAIR):
                            nc.gpsimd.indirect_dma_start(
                                out=adj[s][:, h, :], out_offset=None, in_=adj_rows,
                                in_offset=bass.IndirectOffsetOnAxis(ap=index[s][:, h, 0:1], axis=0)).then_inc(gathered[s], 16)
                            nc.gpsimd.indirect_dma_start(
                                out=feat[s][:, h, :], out_offset=None, in_=a["table0"],
                                in_offset=bass.IndirectOffsetOnAxis(ap=index[s][:, h, 1:2], axis=0)).then_inc(gathered[s], 16)

            @block.tensor
            def _(pe):
                n = runs(nc, pe, m)
                with pe.Fori(0, n) as it:
                    for s in range(SETS):
                        pe.wait_ge(gathered[s], (it + 1) * gathers)
                        pe.wait_ge(added[s], it)
                        for h in range(PAIR):
                            last = nc.tensor.matmul(ps[s][:, 0:2 * D], adj[s][:, h, :], feat[s][:, h, :],
                                                    start=h == 0, stop=h == PAIR - 1)
                        last.then_inc(summed[s], 1)

            @block.vector
            def _(dve):
                n = runs(nc, dve, m)
                with dve.Fori(0, n) as it:
                    tiles = tiles_of_step(nc, dve, m, it)
                    for s in range(SETS):
                        dve.wait_ge(gathered[s], (it + 1) * gathers)
                        dve.wait_ge(off_packed[s], 16 * it)
                        for h in range(PAIR):
                            last = nc.vector.scalar_tensor_tensor(
                                out=off[s][:, h, :], in0=m.row_ramp[:],
                                scalar=m.relative[:, bass.ds((it * SETS + s) * PAIR + h, 1)], in1=adj[s][:, h, :],
                                op0=ALU.not_equal, op1=ALU.mult)
                        last.then_inc(off_ready[s], 1)
                        dve.wait_ge(summed[s], it + 1)
                        dve.wait_ge(added[s - 1], it + (s > 0))
                        at = m.acc[:, bass.ds(tiles[s] * (2 * D), 2 * D)]
                        nc.vector.tensor_tensor(at, at, ps[s][:, 0:2 * D], ALU.add).then_inc(added[s], 1)

            @block.sync
            def _(sp):
                n = runs(nc, sp, m)
                with sp.Fori(0, n) as it:
                    for s in range(SETS):
                        sp.wait_ge(gathered[s], (it + 1) * gathers)
                        sp.dma_start(pair_of(a["adj_pack"], it, s), adj[s][:].rearrange("p h i -> p (h i)")).then_inc(
                            packed[s], 16)
                        sp.wait_ge(off_ready[s], it + 1)
                        sp.dma_start(pair_of(a["off_pack"], it, s), off[s][:].rearrange("p h i -> p (h i)")).then_inc(
                            off_packed[s], 16)
                for s in range(SETS):
                    sp.wait_ge(packed[s], 16 * n)
                    sp.wait_ge(off_packed[s], 16 * n)
                    sp.nop(nofuse=True)


def stage_gin_dense(nc, m, a):
    with Stage(nc) as ctx:
        def sb(name, shape):
            return [ctx.enter_context(nc.sbuf_tensor(f"d0_{name}{b}", shape, F32)) for b in range(2)]

        def ps(name):
            return [ctx.enter_context(nc.psum_tensor(f"d0_{name}{b}", [P, WIDE], F32)) for b in range(2)]

        def sem(name):
            return [ctx.sem(f"d0_{name}{b}") for b in range(2)]

        scaled = sb("scaled", [P, GROUP, D])
        act_in = [sb(f"layer{l}_", [P, WIDE]) for l in range(4)]
        ps_t = ps("ps_t")
        ps_l = ps("ps_l")
        ps_o = ps("ps_o")
        scaled_ready, turned, multiplied, activated, merged, added = (
            sem(x) for x in ("scaled_ready", "turned", "multiplied", "activated", "merged", "added"))
        acc = m.acc[:, 0:T * 2 * D].rearrange("p (t b d) -> p t b d", b=2, d=D)
        with nc.Block() as block:
            @block.vector
            def _(dve):
                def add(u, it):
                    dve.wait_ge(merged[u], it + 1)
                    at = m.x[:, bass.ds(it * (2 * GROUP) + u * GROUP, GROUP), :]
                    nc.vector.tensor_tensor(at, at, ps_o[u][:].rearrange("p (g d) -> p g d", d=D), ALU.add).then_inc(
                        added[u], 1)

                with dve.Fori(0, GROUPS // 2) as it:
                    for u in range(2):
                        for b in range(2):
                            dve.wait_ge(turned[b], it * 2 + u)
                            nc.vector.tensor_scalar(
                                scaled[b][:], acc[:, bass.ds(it * (2 * GROUP) + u * GROUP, GROUP), b, :],
                                m.eps[:, b:b + 1], None, ALU.mult).then_inc(scaled_ready[b], 1)
                    add(0, it)
                    add(1, it)

            @block.tensor
            def _(pe):
                with pe.Fori(0, GROUPS // 2) as it:
                    for u in range(2):
                        g = it * 2 + u
                        for b in range(2):
                            pe.wait_ge(scaled_ready[b], g + 1)
                            pe.wait_ge(activated[b], g * 4)
                            for i in range(GROUP):
                                last = nc.tensor.transpose(ps_t[b][:, i * P:(i + 1) * P], scaled[b][:, i, :], m.ident[:])
                            last.then_inc(turned[b], 1)
                        for l in range(3):
                            for b in range(2):
                                pe.wait_ge(activated[b], g * 4 + (l + 1))
                                nc.tensor.matmul(ps_l[b][:], m.w0[:, b * 3 + l, :], act_in[l][b][:], start=True,
                                                 stop=True).then_inc(multiplied[b], 1)
                        for b in range(2):
                            pe.wait_ge(activated[b], g * 4 + 4)
                        pe.wait_ge(added[u], it)
                        for i in range(GROUP):
                            out = ps_o[u][:, i * P:(i + 1) * P]
                            for b in range(2):
                                nc.tensor.matmul(out, act_in[3][b][:, i * P:(i + 1) * P], m.wm[:, b, :],
                                                 start=b == 0, stop=False)
                            last = nc.tensor.matmul(out, m.ones[0:1, :], m.bm[:], start=False, stop=True)
                        last.then_inc(merged[u], 1)

            @block.scalar
            def _(act):
                with act.Fori(0, GROUPS // 2) as it:
                    for u in range(2):
                        g = it * 2 + u
                        for b in range(2):
                            act.wait_ge(turned[b], g + 1)
                            if u:
                                act.wait_ge(merged[0], it + 1)
                            else:
                                act.wait_ge(merged[1], it)
                            nc.scalar.copy(act_in[0][b][:], ps_t[b][:]).then_inc(activated[b], 1)
                        for l in range(3):
                            for b in range(2):
                                act.wait_ge(multiplied[b], g * 3 + (l + 1))
                                nc.scalar.activation(act_in[l + 1][b][:], ps_l[b][:], ACT.Relu,
                                                     bias=m.b0[:, b * 3 + l:b * 3 + l + 1]).then_inc(activated[b], 1)


def stage_gat_max(nc, m, a):
    with Stage(nc) as ctx:
        w = Walk(nc, m, a, "g1", ctx)
        width = D + 2
        index = w.sb("index", [P, PAIR, 2], U32)
        adj = w.halves("adj", [SETS, PAIR, P])
        feat = w.sb("feat", [P, PAIR, width])
        bias = w.sb("bias", [P, PAIR, P])
        masked = w.sb("masked", [P, PAIR, P])
        best = w.sb("best", [P, 1])
        ps = w.ps("ps", [P, 512])
        loaded = ctx.sem("g1_loaded")
        index_ready, gathered, packed, biased, masked_ready, turned, reduced, kept = (
            w.sem(x) for x in ("index_ready", "gathered", "packed", "biased", "masked_ready", "turned", "reduced",
                               "kept"))
        with nc.Block() as block:
            @block.gpsimd
            def _(pool):
                n = runs(nc, pool, m)
                with pool.Fori(0, n) as it:
                    for s in range(SETS):
                        pool.wait_ge(index_ready[s], it + 1)
                        pool.wait_ge(packed[s], 16 * it)
                        pool.wait_ge(masked_ready[s], it)
                        pool.nop(nofuse=True)
                        for h in range(PAIR):
                            nc.gpsimd.indirect_dma_start(
                                out=feat[s][:, h, :], out_offset=None, in_=a["table1"],
                                in_offset=bass.IndirectOffsetOnAxis(ap=index[s][:, h, 1:2], axis=0)).then_inc(gathered[s], 16)

            @block.sync
            def _(sp):
                n = runs(nc, sp, m)
                sp.dma_start(half_of(adj, 0), step_of(a["adj_pack"], 0)).then_inc(loaded, 16)
                sp.wait_ge(loaded, 16)
                sp.dma_start(half_of(adj, 1), step_of(a["adj_pack"], 1)).then_inc(loaded, 16)
                with sp.Fori(2, n) as it:
                    sp.wait_ge(loaded, it * 16)
                    sp.nop(nofuse=True)
                    sp.wait_ge(biased[SETS - 1], it - 1)
                    sp.nop(nofuse=True)
                    sp.dma_start(half_of(adj, it), step_of(a["adj_pack"], it)).then_inc(loaded, 16)

            @block.scalar
            def _(act):
                n = runs(nc, act, m)
                for s in range(SETS):
                    nc.scalar.copy(index[s][:], m.index[:, s * PAIR:(s + 1) * PAIR, :]).then_inc(index_ready[s], 1)
                with act.Fori(0, n) as it:
                    for s in range(SETS):
                        act.wait_ge(gathered[s], (it + 1) * (16 * PAIR))
                        nc.scalar.dma_start(pair_of(a["wh_pack"], it, s), feat[s][:].rearrange("p h w -> p (h w)")
                                            ).then_inc(packed[s], 16)
                        nc.scalar.copy(index[s][:], m.index[:, bass.ds((it * SETS + SETS + s) * PAIR, PAIR), :]
                                       ).then_inc(index_ready[s], 1)
                        act.wait_ge(biased[s], it + 1)
                        act.wait_ge(turned[s], it)
                        for h in range(PAIR):
                            last = nc.scalar.activation(masked[s][:, h, :], bias[s][:, h, :], ACT.Identity,
                                                        bias=feat[s][:, h, D + 1:D + 2])
                        last.then_inc(masked_ready[s], 1)
                for s in range(SETS):
                    act.wait_ge(packed[s], 16 * n)
                act.nop(nofuse=True)

            @block.tensor
            def _(pe):
                n = runs(nc, pe, m)
                with pe.Fori(0, n) as it:
                    for s in range(SETS):
                        pe.wait_ge(masked_ready[s], it + 1)
                        pe.wait_ge(reduced[s], it)
                        for h in range(PAIR):
                            last = nc.tensor.transpose(ps[s][:, h * P:(h + 1) * P], masked[s][:, h, :], m.ident[:])
                        last.then_inc(turned[s], 1)

            @block.vector
            def _(dve):
                last = last_run(nc, dve, m)

                def mask(it, s):
                    dve.wait_ge(loaded, it * 16 + 16)
                    dve.wait_ge(masked_ready[s], it)
                    nc.vector.tensor_scalar(bias[s][:], pair_in(adj, it, s), 0.0, -BIG, ALU.is_le, ALU.mult).then_inc(
                        biased[s], 1)

                def reduce(it, s):
                    dve.wait_ge(turned[s], it + 1)
                    nc.vector.tensor_reduce(best[s][:], ps[s][:, 0:PAIR * P], AX.X, ALU.max).then_inc(reduced[s], 1)

                def keep(it, s, tile):
                    dve.wait_ge(reduced[s], it + 1)
                    dve.wait_ge(kept[s - 1], it + (s > 0))
                    at = m.best1[:, bass.ds(tile, 1)]
                    nc.vector.tensor_tensor(at, at, best[s][:], ALU.max).then_inc(kept[s], 1)

                for s in range(SETS):
                    mask(0, s)
                with dve.Fori(0, last) as it:
                    tiles = tiles_of_step(nc, dve, m, it)
                    for s in range(SETS):
                        reduce(it, s)
                        mask(it + 1, s)
                        keep(it, s, tiles[s])
                tiles = tiles_of_step(nc, dve, m, last)
                for s in range(SETS):
                    reduce(last, s)
                    keep(last, s, tiles[s])


def spread_rows(nc, m, a, name, value, wide, scratch, columns, before=None):
    with Stage(nc) as ctx:
        turned, copied, stored, loaded = (
            ctx.sem(f"{name}_{x}") for x in ("turned", "copied", "stored", "loaded"))
        ps = ctx.enter_context(nc.psum_tensor(f"{name}_ps", [P, P], F32))
        rows = ctx.enter_context(nc.sbuf_tensor(f"{name}_rows", [P, P], F32))
        ready = ctx.sem(f"{name}_ready")
        with nc.Block() as block:
            @block.vector
            def _(dve):
                before(dve, ready)
                dve.wait_ge(turned, 1)
                nc.vector.tensor_copy(rows[0:columns, :], ps[0:columns, :]).then_inc(copied, 1)

            @block.tensor
            def _(pe):
                pe.wait_ge(ready, 1)
                nc.tensor.transpose(ps[0:columns, :], value, m.ident[:]).then_inc(turned, 1)

            @block.sync
            def _(sp):
                sp.wait_ge(copied, 1)
                sp.dma_start(scratch.rearrange("(c i) -> c i", i=P), rows[0:columns, :]).then_inc(stored, 16)
                sp.wait_ge(stored, 16)
                sp.dma_start(wide, scratch.rearrange("(a n) -> a n", a=1).broadcast_to([P, columns * P])).then_inc(
                    loaded, 16)
                sp.wait_ge(loaded, 16)


def stage_gat_shift(nc, m, a):
    with Stage(nc) as ctx:
        def sb(name, shape):
            return ctx.enter_context(nc.sbuf_tensor("sh_" + name, shape, F32))

        best_wide = sb("best_wide", [P, N])
        tenth = sb("tenth", [P, 1024])
        step = ctx.sem("sh_step")

        def before(dve, ready):
            nc.vector.tensor_copy(m.best1c[:], m.best1[:, 0:T]).then_inc(ready, 1)

        spread_rows(nc, m, a, "sh1", m.best1c[:], best_wide[:], a["row_scratch"][0:N], T, before)
        with nc.Block() as block:
            @block.vector
            def _(dve):
                k = 0
                for c in range(4):
                    part = slice(c * 1024, (c + 1) * 1024)
                    nc.vector.tensor_tensor(best_wide[:, part], best_wide[:, part], m.s1_wide[:, part], ALU.add
                                            ).then_inc(step, 1)
                    k += 1
                    dve.wait_ge(step, k)
                    nc.vector.tensor_scalar(tenth[:], best_wide[:, part], ALPHA, None, ALU.mult).then_inc(step, 1)
                    k += 1
                    dve.wait_ge(step, k)
                    nc.vector.tensor_tensor(m.shift1[:, part], best_wide[:, part], tenth[:], ALU.max).then_inc(step, 1)
                    k += 1
                    dve.wait_ge(step, k)


def stage_gat_pairs(nc, m, a):
    with Stage(nc) as ctx:
        w = Walk(nc, m, a, "g2", ctx)
        adj = w.halves("adj", [SETS, PAIR, P])
        feat = w.halves("feat", [SETS, PAIR, D + 2])
        bias = w.sb("bias", [P, PAIR, P])
        leaky = w.sb("leaky", [P, PAIR, P])
        below = w.sb("below", [P, PAIR, P])
        prob = w.sb("prob", [P, PAIR, P])
        ps = w.ps("ps", [P, 512])
        touch = ctx.enter_context(nc.sbuf_tensor("g2_touch", [1, 1], F32))
        loaded, touched = (ctx.sem("g2" + x) for x in ("_loaded", "_touched"))
        biased, placed, leaked, moved, shifted, exped, summed, added = (
            w.sem(x) for x in ("biased", "placed", "leaked", "moved", "shifted", "exped", "summed", "added"))
        loads = ((adj, a["adj_pack"]), (feat, a["wh_pack"]))
        with nc.Block() as block:
            @block.sync
            def _(sp):
                n = runs(nc, sp, m)

                def load(it):
                    for dst, pack in loads:
                        sp.dma_start(half_of(dst, it), step_of(pack, it)).then_inc(loaded, 16)

                load(0)
                sp.wait_ge(loaded, 32)
                load(1)
                with sp.Fori(2, n) as it:
                    sp.wait_ge(loaded, it * 32)
                    sp.nop(nofuse=True)
                    sp.wait_ge(summed[SETS - 1], it - 1)
                    sp.nop(nofuse=True)
                    load(it)

            @block.gpsimd
            def _(pool):
                n = runs(nc, pool, m)
                with pool.Fori(0, n) as it:
                    for s in range(SETS):
                        pool.wait_ge(moved[s], it + 1)
                        pool.wait_ge(biased[s], it + 1)
                        pool.wait_ge(exped[s], it)
                        nc.gpsimd.tensor_tensor(below[s][:], bias[s][:], leaky[s][:], ALU.add).then_inc(shifted[s], 1)

            @block.scalar
            def _(act):
                n = runs(nc, act, m)
                with act.Fori(0, n) as it:
                    act.wait_ge(touched, it)
                    nc.scalar.activation(touch[:], m.ones[0:1, 0:1], ACT.Exp).then_inc(touched, 1)
                    tiles = tiles_of_step(nc, act, m, it)

                    def place(s):
                        act.wait_ge(loaded, it * 32 + 32)
                        act.wait_ge(shifted[s], it)
                        for h in range(PAIR):
                            last = nc.scalar.activation(leaky[s][:, h, :], m.s1_wide[:, bass.ds(tiles[s] * P, P)],
                                                        ACT.Identity, bias=pair_in(feat, it, s)[:, h, D + 1:D + 2])
                        last.then_inc(placed[s], 1)

                    def expo(s):
                        act.wait_ge(shifted[s], it + 1)
                        act.wait_ge(summed[s], it)
                        nc.scalar.activation(prob[s][:], below[s][:], ACT.Exp).then_inc(exped[s], 1)

                    place(0)
                    place(1)
                    place(2)
                    expo(0)
                    place(3)
                    expo(1)
                    expo(2)
                    expo(3)

            @block.tensor
            def _(pe):
                n = runs(nc, pe, m)
                with pe.Fori(0, n) as it:
                    for s in range(SETS):
                        pe.wait_ge(exped[s], it + 1)
                        pe.wait_ge(added[s], it)
                        for h in range(PAIR):
                            last = nc.tensor.matmul(ps[s][:, 0:D + 1], prob[s][:, h, :],
                                                    pair_in(feat, it, s)[:, h, 0:D + 1],
                                                    start=h == 0, stop=h == PAIR - 1)
                        last.then_inc(summed[s], 1)

            @block.vector
            def _(dve):
                n = runs(nc, dve, m)
                last = last_run(nc, dve, m)

                def mask(it, s):
                    dve.wait_ge(loaded, it * 32 + 32)
                    dve.wait_ge(shifted[s], it)
                    nc.vector.tensor_scalar(bias[s][:], pair_in(adj, it, s), 0.0, -BIG, ALU.is_le, ALU.mult).then_inc(
                        biased[s], 1)

                def leak(it, s):
                    dve.wait_ge(placed[s], it + 1)
                    nc.vector.scalar_tensor_tensor(out=leaky[s][:], in0=leaky[s][:], scalar=ALPHA, in1=leaky[s][:],
                                                   op0=ALU.mult, op1=ALU.max).then_inc(leaked[s], 1)

                def move(it, s, tile):
                    dve.wait_ge(leaked[s], it + 1)
                    shift = m.shift1[:, bass.ds(tile * P, P)].rearrange("p (o i) -> p o i", o=1)
                    nc.vector.tensor_tensor(leaky[s][:], leaky[s][:], shift.broadcast_to([P, PAIR, P]),
                                            ALU.subtract).then_inc(moved[s], 1)

                def add(it, s, tile):
                    dve.wait_ge(summed[s], it + 1)
                    dve.wait_ge(added[s - 1], it + (s > 0))
                    at = m.acc[:, bass.ds(tile * (D + 1), D + 1)]
                    nc.vector.tensor_tensor(at, at, ps[s][:, 0:D + 1], ALU.add).then_inc(added[s], 1)

                tiles = tiles_of_step(nc, dve, m, 0)
                for s in range(SETS):
                    mask(0, s)
                    leak(0, s)
                    if s:
                        move(0, s - 1, tiles[s - 1])
                move(0, SETS - 1, tiles[SETS - 1])
                with dve.Fori(1, n) as it:
                    tiles = tiles_of_step(nc, dve, m, it)
                    before = tiles_of_step(nc, dve, m, it - 1)
                    for s in range(SETS):
                        mask(it, s)
                        leak(it, s)
                        add(it - 1, s, before[s])
                        move(it, s, tiles[s])
                tiles = tiles_of_step(nc, dve, m, last)
                for s in range(SETS):
                    add(last, s, tiles[s])


def stage_gat_dense(nc, m, a):
    with Stage(nc) as ctx:
        def sb(name, shape):
            return ctx.enter_context(nc.sbuf_tensor("d1_" + name, shape, F32))

        alone = sb("alone", [P, T])
        denom = sb("denom", [P, T])
        hsum = sb("hsum", [P, 1])
        hsum_wide = sb("hsum_wide", [P, P])
        mean = sb("mean", [P, D])
        out = [sb(f"out{u}", [P, D]) for u in range(2)]
        low = [sb(f"low{u}", [P, D]) for u in range(2)]
        ps = ctx.enter_context(nc.psum_tensor("d1_ps", [P, 512], F32))
        step, meaned = (ctx.sem("d1_" + x) for x in ("step", "meaned"))
        lowered, exped, chain = ([ctx.sem(f"d1_{x}{u}") for u in range(2)]
                                 for x in ("lowered", "exped", "chain"))
        acc = m.acc[:, 0:T * (D + 1)].rearrange("p (t d) -> p t d", d=D + 1)
        with nc.Block() as block:
            @block.tensor
            def _(pe):
                pe.wait_ge(step, 3)
                nc.tensor.matmul(ps[:, 0:D], hsum_wide[:], m.w1[:, 0:D], start=True, stop=True).then_inc(meaned, 1)

            @block.vector
            def _(dve):
                nc.vector.tensor_scalar(alone[:], m.best1[:, 0:T], -0.5 * BIG, None, ALU.is_lt).then_inc(step, 1)
                nc.vector.tensor_reduce(hsum[:], m.hsum[:], AX.X, ALU.add).then_inc(step, 1)
                dve.wait_ge(step, 2)
                nc.vector.tensor_scalar(hsum_wide[:], m.ones[:], hsum[:, 0:1], 1.0 / N, ALU.mult, ALU.mult).then_inc(step, 1)
                nc.vector.tensor_tensor(denom[:], acc[:, :, D], alone[:], ALU.add).then_inc(step, 1)
                dve.wait_ge(step, 4)
                nc.vector.reciprocal(denom[:], denom[:]).then_inc(step, 1)
                dve.wait_ge(meaned, 1)
                nc.vector.tensor_copy(mean[:], ps[:, 0:D]).then_inc(step, 1)
                dve.wait_ge(step, 6)
                with dve.Fori(0, T // 2) as it:
                    for u in range(2):
                        t = it * 2 + u
                        dve.wait_ge(chain[u], it * 4)
                        nc.vector.tensor_scalar(out[u][:], acc[:, bass.ds(t, 1), 0:D].rearrange("p o d -> p (o d)"),
                                                denom[:, bass.ds(t, 1)], None, ALU.mult).then_inc(chain[u], 1)
                        dve.wait_ge(chain[u], it * 4 + 1)
                        nc.vector.scalar_tensor_tensor(out=out[u][:], in0=mean[:], scalar=alone[:, bass.ds(t, 1)],
                                                       in1=out[u][:], op0=ALU.mult, op1=ALU.add).then_inc(chain[u], 1)
                        dve.wait_ge(chain[u], it * 4 + 2)
                        nc.vector.tensor_scalar(low[u][:], out[u][:], 0.0, None, ALU.min).then_inc(lowered[u], 1)
                    for u in range(2):
                        t = it * 2 + u
                        dve.wait_ge(exped[u], it + 1)
                        nc.vector.scalar_tensor_tensor(out=out[u][:], in0=out[u][:], scalar=0.0, in1=low[u][:],
                                                       op0=ALU.max, op1=ALU.add).then_inc(chain[u], 1)
                        dve.wait_ge(chain[u], it * 4 + 3)
                        at = m.x[:, bass.ds(t, 1), :].rearrange("p o d -> p (o d)")
                        nc.vector.scalar_tensor_tensor(out=at, in0=out[u][:], scalar=-1.0, in1=at, op0=ALU.add,
                                                       op1=ALU.add).then_inc(chain[u], 1)

            @block.scalar
            def _(act):
                with act.Fori(0, T // 2) as it:
                    for u in range(2):
                        act.wait_ge(lowered[u], it + 1)
                        nc.scalar.activation(low[u][:], low[u][:], ACT.Exp).then_inc(exped[u], 1)




def stage_signed_sums(nc, m, a):
    with Stage(nc) as ctx:
        w = Walk(nc, m, a, "g3", ctx)
        width = UV_END
        index = w.sb("index", [P, PAIR, 2], U32)
        adj = w.halves("adj", [SETS, PAIR, P])
        above = w.sb("above", [P, PAIR, P])
        below = w.sb("below", [P, PAIR, P])
        feat = w.sb("feat", [P, PAIR, width])
        ps = w.ps("ps", [P, 512])
        loaded = ctx.sem("g3_loaded")
        cutout = w.sb("cutout", [P, PAIR, P])
        index_ready, gathered, packed, compared, summed, added = (
            w.sem(x) for x in ("index_ready", "gathered", "packed", "compared", "summed", "added"))
        with nc.Block() as block:
            @block.gpsimd
            def _(pool):
                n = runs(nc, pool, m)
                with pool.Fori(0, n) as it:
                    for s in range(SETS):
                        pool.wait_ge(index_ready[s], it + 1)
                        pool.wait_ge(packed[s], 16 * it)
                        pool.wait_ge(summed[s], it)
                        pool.nop(nofuse=True)
                        for h in range(PAIR):
                            nc.gpsimd.indirect_dma_start(
                                out=feat[s][:, h, :], out_offset=None, in_=a["table2"],
                                in_offset=bass.IndirectOffsetOnAxis(ap=index[s][:, h, 1:2], axis=0)).then_inc(gathered[s], 16)

            @block.sync
            def _(sp):
                n = runs(nc, sp, m)
                sp.dma_start(half_of(adj, 0), step_of(a["off_pack"], 0)).then_inc(loaded, 16)
                sp.wait_ge(loaded, 16)
                sp.dma_start(half_of(adj, 1), step_of(a["off_pack"], 1)).then_inc(loaded, 16)
                with sp.Fori(2, n) as it:
                    sp.wait_ge(loaded, it * 16)
                    sp.nop(nofuse=True)
                    sp.wait_ge(compared[SETS - 1], 2 * (it - 1))
                    sp.nop(nofuse=True)
                    sp.dma_start(half_of(adj, it), step_of(a["off_pack"], it)).then_inc(loaded, 16)

            @block.scalar
            def _(act):
                n = runs(nc, act, m)
                for s in range(SETS):
                    nc.scalar.copy(index[s][:], m.index[:, s * PAIR:(s + 1) * PAIR, :]).then_inc(index_ready[s], 1)
                with act.Fori(0, n) as it:
                    for s in range(SETS):
                        act.wait_ge(loaded, it * 16 + 16)
                        act.wait_ge(summed[s], it)
                        nc.scalar.copy(cutout[s][:], pair_in(adj, it, s)).then_inc(compared[s], 1)
                        act.wait_ge(gathered[s], (it + 1) * (16 * PAIR))
                        nc.scalar.dma_start(pair_of(a["h_pack"], it, s), feat[s][:].rearrange("p h w -> p (h w)")
                                            ).then_inc(packed[s], 16)
                        nc.scalar.copy(index[s][:], m.index[:, bass.ds((it * SETS + SETS + s) * PAIR, PAIR), :]
                                       ).then_inc(index_ready[s], 1)
                for s in range(SETS):
                    act.wait_ge(packed[s], 16 * n)
                act.nop(nofuse=True)

            @block.tensor
            def _(pe):
                n = runs(nc, pe, m)
                with pe.Fori(0, n) as it:
                    for s in range(SETS):
                        pe.wait_ge(gathered[s], (it + 1) * (16 * PAIR))
                        pe.wait_ge(compared[s], 2 * it + 2)
                        pe.wait_ge(added[s], it)
                        for left, at, cols in ((cutout, slice(0, D), slice(0, D)),
                                               (above, slice(D, D + SIGN_W), slice(D, width)),
                                               (below, slice(D + SIGN_W, SUPPORT_W), slice(D, width))):
                            for h in range(PAIR):
                                last = nc.tensor.matmul(ps[s][:, at], left[s][:, h, :], feat[s][:, h, cols],
                                                        start=h == 0, stop=h == PAIR - 1)
                        last.then_inc(summed[s], 1)

            @block.vector
            def _(dve):
                last = last_run(nc, dve, m)

                def compare(it, s):
                    dve.wait_ge(loaded, it * 16 + 16)
                    dve.wait_ge(summed[s], it)
                    nc.vector.tensor_scalar(above[s][:], pair_in(adj, it, s), 0.0, None, ALU.is_gt)
                    nc.vector.tensor_scalar(below[s][:], pair_in(adj, it, s), 0.0, None, ALU.is_lt).then_inc(
                        compared[s], 1)

                def add(it, s, tile):
                    dve.wait_ge(summed[s], it + 1)
                    dve.wait_ge(added[s - 1], it + (s > 0))
                    at = m.acc[:, bass.ds(tile * SUPPORT_W, SUPPORT_W)]
                    nc.vector.tensor_tensor(at, at, ps[s][:, 0:SUPPORT_W], ALU.add).then_inc(added[s], 1)

                for s in range(SETS):
                    compare(0, s)
                with dve.Fori(0, last) as it:
                    tiles = tiles_of_step(nc, dve, m, it)
                    for s in range(SETS):
                        add(it, s, tiles[s])
                        compare(it + 1, s)
                tiles = tiles_of_step(nc, dve, m, last)
                for s in range(SETS):
                    add(last, s, tiles[s])


def stage_signed_scores(nc, m, a):
    with Stage(nc) as ctx:
        scores = [ctx.enter_context(nc.sbuf_tensor(f"sc_scores{g}", [P, T, 4], F32)) for g in range(2)]
        tenth = [ctx.enter_context(nc.sbuf_tensor(f"sc_tenth{g}", [P, T, 4], F32)) for g in range(2)]
        most = ctx.enter_context(nc.sbuf_tensor("sc_most", [P, 2], F32))
        flags = ctx.enter_context(nc.sbuf_tensor("sc_flags", [1, 2], F32))
        ps = ctx.enter_context(nc.psum_tensor("sc_ps", [P, 2 * P], F32))
        step, stored, counted, turned, flagged = (
            ctx.sem("sc_" + x) for x in ("step", "stored", "counted", "turned", "flagged"))
        acc = m.acc[:, 0:T * SUPPORT_W].rearrange("p (t w) -> p t w", w=SUPPORT_W)
        above = acc[:, :, D:D + 2 * HEADS].rearrange("p t (k o) -> p t k o", o=2)
        below = acc[:, :, D + SIGN_W:D + SIGN_W + 2 * HEADS].rearrange("p t (k o) -> p t k o", o=2)
        with nc.Block() as block:
            @block.vector
            def _(dve):
                for g, (first, second) in enumerate(((above, below), (below, above))):
                    nc.vector.memset(scores[g][:], 0.0).then_inc(step, 1)
                    dve.wait_ge(step, 4 * g + 1)
                    nc.vector.tensor_tensor(scores[g][:, :, 0:HEADS], first[:, :, :, 0], second[:, :, :, 1], ALU.add
                                            ).then_inc(step, 1)
                    dve.wait_ge(step, 4 * g + 2)
                    nc.vector.tensor_scalar(tenth[g][:], scores[g][:], ALPHA, None, ALU.mult).then_inc(step, 1)
                    dve.wait_ge(step, 4 * g + 3)
                    nc.vector.tensor_tensor(scores[g][:], scores[g][:], tenth[g][:], ALU.max).then_inc(step, 1)
                for c, count in enumerate((SUPPORT_W - 1, UV_END - 1)):
                    nc.vector.tensor_reduce(most[:, c:c + 1], acc[:, :, count], AX.X, ALU.max).then_inc(counted, 1)
                dve.wait_ge(turned, 1)
                for c in range(2):
                    nc.vector.tensor_reduce(flags[:, c:c + 1], ps[0:1, c * P:(c + 1) * P], AX.X, ALU.max).then_inc(
                        flagged, 1)
                dve.wait_ge(flagged, 2)
                nc.vector.tensor_scalar(m.meta[:, NEGATIVES:NEGATIVES + 1], flags[:, 0:1], 0.5, None, ALU.is_gt)
                nc.vector.tensor_scalar(m.meta[:, CROWDED:CROWDED + 1], flags[:, 1:2], TOPK - 0.5, None, ALU.is_gt)

            @block.tensor
            def _(pe):
                pe.wait_ge(counted, 2)
                for c in range(2):
                    last = nc.tensor.matmul(ps[0:1, c * P:(c + 1) * P], most[:, c:c + 1], m.ident[:], start=True,
                                            stop=True)
                last.then_inc(turned, 1)

            @block.sync
            def _(sp):
                for g in range(2):
                    sp.wait_ge(step, 4 * g + 4)
                    sp.dma_start(a["score_table"][g * N:(g + 1) * N, :].rearrange("(t p) k -> p t k", p=P),
                                 scores[g][:]).then_inc(stored, 16)
                sp.wait_ge(stored, 32)


def stage_signed_max(nc, m, a, sign):
    flag = None if sign > 0 else NEGATIVES
    with Stage(nc) as ctx:
        w = Walk(nc, m, a, f"g4{sign > 0:d}", ctx)
        index = w.sb("index", [P, PAIR], U32)
        adj = w.halves("adj", [SETS, PAIR, P])
        score = w.sb("score", [P, PAIR, 4])
        bias = w.sb("bias", [P, PAIR, P])
        masked = w.sb("masked", [P, HEADS, PAIR, P], sets=2)
        best = w.sb("best", [P, HEADS], sets=2)
        ps = w.ps("ps", [P, 1024], sets=2)
        loaded = ctx.sem(w.name + "_loaded")
        pack = a["score_pack1" if sign > 0 else "score_pack0"]
        index_ready, gathered, packed, biased, masked_ready, turned, reduced, kept = (
            w.sem(x) for x in ("index_ready", "gathered", "packed", "biased", "masked_ready", "turned", "reduced",
                               "kept"))

        def two_before(eng, semaphore, s, it):
            eng.wait_ge(semaphore[(s + 2) % SETS], it + (s >= 2))

        with nc.Block() as block:
            @block.gpsimd
            def _(pool):
                with where(pool, m, flag):
                    n = runs(nc, pool, m)
                    with pool.Fori(0, n) as it:
                        for s in range(SETS):
                            pool.wait_ge(index_ready[s], it + 1)
                            pool.wait_ge(packed[s], 16 * it)
                            pool.wait_ge(masked_ready[s], it)
                            pool.nop(nofuse=True)
                            for h in range(PAIR):
                                nc.gpsimd.indirect_dma_start(
                                    out=score[s][:, h, :], out_offset=None, in_=a["score_table"],
                                    in_offset=bass.IndirectOffsetOnAxis(ap=index[s][:, h:h + 1], axis=0)).then_inc(gathered[s], 16)

            @block.sync
            def _(sp):
                with where(sp, m, flag):
                    n = runs(nc, sp, m)
                    sp.dma_start(half_of(adj, 0), step_of(a["off_pack"], 0)).then_inc(loaded, 16)
                    sp.wait_ge(loaded, 16)
                    sp.dma_start(half_of(adj, 1), step_of(a["off_pack"], 1)).then_inc(loaded, 16)
                    with sp.Fori(2, n) as it:
                        sp.wait_ge(loaded, it * 16)
                        sp.nop(nofuse=True)
                        sp.wait_ge(biased[SETS - 1], it - 1)
                        sp.nop(nofuse=True)
                        sp.dma_start(half_of(adj, it), step_of(a["off_pack"], it)).then_inc(loaded, 16)

            @block.scalar
            def _(act):
                def index_of(s, at):
                    nc.scalar.activation(index[s][:], m.index[:, at, 1], ACT.Copy,
                                         bias=0.0 if sign > 0 else float(N)).then_inc(index_ready[s], 1)

                with where(act, m, flag):
                    n = runs(nc, act, m)
                    for s in range(SETS):
                        index_of(s, slice(s * PAIR, (s + 1) * PAIR))
                    with act.Fori(0, n) as it:
                        for s in range(SETS):
                            u = s % 2
                            act.wait_ge(gathered[s], (it + 1) * (16 * PAIR))
                            nc.scalar.dma_start(pair_of(pack, it, s), score[s][:].rearrange("p h w -> p (h w)")
                                                ).then_inc(packed[s], 16)
                            index_of(s, bass.ds((it * SETS + SETS + s) * PAIR, PAIR))
                            act.wait_ge(biased[s], it + 1)
                            two_before(act, turned, s, it)
                            for k in range(HEADS):
                                for h in range(PAIR):
                                    last = nc.scalar.activation(masked[u][:, k, h, :], bias[s][:, h, :], ACT.Identity,
                                                                bias=score[s][:, h, k:k + 1])
                            last.then_inc(masked_ready[s], 1)
                    for s in range(SETS):
                        act.wait_ge(packed[s], 16 * n)
                    act.nop(nofuse=True)

            @block.tensor
            def _(pe):
                with where(pe, m, flag):
                    n = runs(nc, pe, m)
                    with pe.Fori(0, n) as it:
                        for s in range(SETS):
                            u = s % 2
                            pe.wait_ge(masked_ready[s], it + 1)
                            two_before(pe, reduced, s, it)
                            for k in range(HEADS):
                                for h in range(PAIR):
                                    c = (k * PAIR + h) * P
                                    last = nc.tensor.transpose(ps[u][:, c:c + P], masked[u][:, k, h, :], m.ident[:])
                            last.then_inc(turned[s], 1)

            @block.vector
            def _(dve):
                with where(dve, m, flag):
                    last = last_run(nc, dve, m)

                    def mask(it, s):
                        dve.wait_ge(loaded, it * 16 + 16)
                        dve.wait_ge(masked_ready[s], it)
                        nc.vector.tensor_scalar(bias[s][:], pair_in(adj, it, s), 0.0, -BIG,
                                                ALU.is_le if sign > 0 else ALU.is_ge, ALU.mult).then_inc(biased[s], 1)

                    def reduce(it, s):
                        dve.wait_ge(turned[s], it + 1)
                        two_before(dve, kept, s, it)
                        nc.vector.tensor_reduce(best[s % 2][:], ps[s % 2][:, 0:HEADS * PAIR * P].rearrange(
                            "p (k s) -> p k s", k=HEADS), AX.X, ALU.max).then_inc(reduced[s], 1)

                    def keep(it, s, tile):
                        dve.wait_ge(reduced[s], it + 1)
                        dve.wait_ge(kept[s - 1], it + (s > 0))
                        at = m.best2[:, bass.ds(tile, 1), :].rearrange("p o k -> p (o k)")
                        nc.vector.tensor_tensor(at, at, best[s % 2][:], ALU.max).then_inc(kept[s], 1)

                    for s in range(SETS):
                        mask(0, s)
                    with dve.Fori(0, last) as it:
                        tiles = tiles_of_step(nc, dve, m, it)
                        for s in range(SETS):
                            reduce(it, s)
                            mask(it + 1, s)
                            keep(it, s, tiles[s])
                    tiles = tiles_of_step(nc, dve, m, last)
                    for s in range(SETS):
                        reduce(last, s)
                        keep(last, s, tiles[s])


def stage_signed_pairs(nc, m, a, sign):
    flag = None if sign > 0 else NEGATIVES
    with Stage(nc) as ctx:
        w = Walk(nc, m, a, f"g5{sign > 0:d}", ctx)
        adj = w.halves("adj", [SETS, PAIR, P])
        feat = w.halves("feat", [SETS, PAIR, UV_END])
        score = w.halves("score", [SETS, PAIR, 4])
        bias = w.sb("bias", [P, PAIR, P], sets=2)
        expo = w.sb("expo", [P, HEADS, PAIR, P])
        prob = w.sb("prob", [P, HEADS, PAIR, P], sets=2)
        total = w.sb("total", [P, HEADS, P], sets=2)
        ps = w.ps("ps", [P, 512])
        touch = ctx.enter_context(nc.sbuf_tensor(w.name + "_touch", [1, 1], F32))
        loaded, touched = (ctx.sem(w.name + x) for x in ("_loaded", "_touched"))
        biased, shifted, exped, totalled, weighted, summed, added = (
            w.sem(x) for x in ("biased", "shifted", "exped", "totalled", "weighted", "summed", "added"))
        loads = ((adj, a["off_pack"]), (score, a["score_pack1" if sign > 0 else "score_pack0"]), (feat, a["h_pack"]))

        with nc.Block() as block:
            @block.sync
            def _(sp):
                with where(sp, m, flag):
                    n = runs(nc, sp, m)

                    def load(it):
                        for dst, pack in loads:
                            sp.dma_start(half_of(dst, it), step_of(pack, it)).then_inc(loaded, 16)

                    load(0)
                    sp.wait_ge(loaded, 48)
                    load(1)
                    with sp.Fori(2, n) as it:
                        sp.wait_ge(loaded, it * 48)
                        sp.nop(nofuse=True)
                        sp.wait_ge(summed[SETS - 1], it - 1)
                        sp.nop(nofuse=True)
                        load(it)

            @block.vector
            def _(dve):
                with where(dve, m, flag):
                    n = runs(nc, dve, m)
                    last = last_run(nc, dve, m)

                    def mask(it, s):
                        dve.wait_ge(loaded, it * 48 + 48)
                        if s >= 2:
                            dve.wait_ge(shifted[s - 2], it + 1)
                        else:
                            dve.wait_ge(shifted[s + 2], it)
                        nc.vector.tensor_scalar(bias[s % 2][:], pair_in(adj, it, s), 0.0, -BIG,
                                                ALU.is_le if sign > 0 else ALU.is_ge, ALU.mult).then_inc(biased[s], 1)

                    def shift(it, s, tile):
                        dve.wait_ge(biased[s], it + 1)
                        dve.wait_ge(summed[s], it)
                        by_row = m.shift2[:, bass.ds(tile * (HEADS * P), HEADS * P)].rearrange(
                            "p (k o i) -> p k o i", k=HEADS, o=1)
                        nc.vector.tensor_tensor(
                            expo[s][:], bias[s % 2][:].rearrange("p (o h) i -> p o h i", o=1).broadcast_to(
                                [P, HEADS, PAIR, P]),
                            by_row.broadcast_to([P, HEADS, PAIR, P]), ALU.subtract).then_inc(shifted[s], 1)

                    def total_of(it, s):
                        dve.wait_ge(exped[s], it + 1)
                        dve.wait_ge(summed[(s + 2) % SETS], it + (s >= 2))
                        nc.vector.tensor_tensor(total[s % 2][:], expo[s][:, :, 0, :], expo[s][:, :, 1, :],
                                                ALU.add).then_inc(totalled[s], 1)

                    def add(it, s, tile):
                        dve.wait_ge(summed[s], it + 1)
                        dve.wait_ge(added[s - 1], it + (s > 0))
                        at = m.acc[:, bass.ds(tile * HEAD_W, HEAD_W)]
                        nc.vector.tensor_tensor(at, at, ps[s][:, 0:HEAD_W], ALU.add).then_inc(added[s], 1)

                    tiles = tiles_of_step(nc, dve, m, 0)
                    for s in range(SETS):
                        mask(0, s)
                        if s:
                            total_of(0, s - 1)
                        shift(0, s, tiles[s])
                    with dve.Fori(1, n) as it:
                        tiles = tiles_of_step(nc, dve, m, it)
                        before = tiles_of_step(nc, dve, m, it - 1)
                        for s in range(SETS):
                            mask(it, s)
                            total_of(it - (s == 0), s - 1 if s else SETS - 1)
                            add(it - 1, s, before[s])
                            shift(it, s, tiles[s])
                    tiles = tiles_of_step(nc, dve, m, last)
                    total_of(last, SETS - 1)
                    for s in range(SETS):
                        add(last, s, tiles[s])

            @block.scalar
            def _(act):
                with where(act, m, flag):
                    n = runs(nc, act, m)
                    with act.Fori(0, n) as it:
                        act.wait_ge(touched, it)
                        nc.scalar.activation(touch[:], m.ones[0:1, 0:1], ACT.Exp).then_inc(touched, 1)
                        for s in range(SETS):
                            act.wait_ge(shifted[s], it + 1)
                            for k in range(HEADS):
                                for h in range(PAIR):
                                    last = nc.scalar.activation(expo[s][:, k, h, :], expo[s][:, k, h, :], ACT.Exp,
                                                                bias=pair_in(score, it, s)[:, h, k:k + 1])
                            last.then_inc(exped[s], 1)

            @block.gpsimd
            def _(pool):
                with where(pool, m, flag):
                    n = runs(nc, pool, m)
                    with pool.Fori(0, n) as it:
                        for s in range(SETS):
                            u = s % 2
                            pool.wait_ge(summed[(s + 2) % SETS], it + (s >= 2))
                            pool.wait_ge(exped[s], it + 1)
                            nc.gpsimd.tensor_tensor(
                                prob[u][:], expo[s][:], pair_in(adj, it, s).rearrange(
                                    "p (o h) i -> p o h i", o=1).broadcast_to([P, HEADS, PAIR, P]),
                                ALU.mult).then_inc(weighted[s], 1)

            @block.tensor
            def _(pe):
                with where(pe, m, flag):
                    n = runs(nc, pe, m)
                    with pe.Fori(0, n) as it:
                        for s in range(SETS):
                            u = s % 2
                            pe.wait_ge(weighted[s], it + 1)
                            pe.wait_ge(added[s], it)
                            for k in range(HEADS):
                                c = k * (D + 1)
                                for h in range(PAIR):
                                    nc.tensor.matmul(ps[s][:, c:c + D], prob[u][:, k, h, :],
                                                     pair_in(feat, it, s)[:, h, 0:D],
                                                     start=h == 0, stop=h == PAIR - 1)
                            pe.wait_ge(totalled[s], it + 1)
                            for k in range(HEADS):
                                c = k * (D + 1)
                                last = nc.tensor.matmul(ps[s][:, c + D:c + D + 1], total[u][:, k, :], m.ones[:, 0:1],
                                                        start=True, stop=True)
                            last.then_inc(summed[s], 1)


def stage_gru(nc, m, a, which):
    heads = HEADS if which else 1
    tiles = 2
    span = tiles * P
    last_step = T // (2 * tiles) - 1
    with Stage(nc) as ctx:
        def sb(name, shape):
            return [ctx.enter_context(nc.sbuf_tensor(f"r{which}_{name}{u}", shape, F32)) for u in range(2)]

        def sem(name):
            return [ctx.sem(f"r{which}_{name}{u}") for u in range(2)]

        def ps(name):
            both = [ctx.enter_context(nc.psum_tensor(f"r{which}_{name}{u}", [P, 2 * span], F32)) for u in range(2)]
            return [[x[:, 0:span] for x in both], [x[:, span:2 * span] for x in both]]

        rden = sb("rden", [P, tiles, HEADS])
        part = sb("part", [P, heads, tiles, D])
        partT = sb("partT", [P, heads, span])
        sT = sb("sT", [P, span])
        r = sb("r", [P, span])
        z = sb("z", [P, span])
        hn = sb("hn", [P, span])
        cand = sb("cand", [P, span])
        new = sb("new", [P, span])
        scaled = sb("scaled", [P, tiles, D])
        ps_t = ps("ps_turned")
        third, ps_e = ps("ps_mixed")
        ps_t.append(third)
        ps_g = ps("ps_gates") + ps("ps_candidate")
        ps_b = ps_g[2]
        (parted, turned, copied, mixed, mixed_copied, gated, acts, gates_read, dv, tanhed, newed, back, added,
         divided) = (
            sem(x) for x in ("parted", "turned", "copied", "mixed", "mixed_copied", "gated", "acts", "gates_read",
                             "dve", "tanhed", "newed", "back", "added", "divided"))

        def group(tensor, it, u):
            return tensor[:, bass.ds(it * (2 * tiles) + u * tiles, tiles), :]

        with nc.Block() as block:
            @block.vector
            def _(dve):
                def supports(it, u):
                    dve.wait_ge(turned[u], it)
                    if which:
                        acc = m.acc[:, 0:T * HEAD_W].rearrange("p (t k w) -> p t k w", k=HEADS, w=D + 1)
                        rows = acc[:, bass.ds(it * (2 * tiles) + u * tiles, tiles), :, :]
                        dve.wait_ge(parted[u], it)
                        nc.vector.tensor_scalar(rden[u][:], rows[:, :, :, D], 1.0 / BIG, None, ALU.max).then_inc(
                            divided[u], 1)
                        dve.wait_ge(divided[u], it * 2 + 1)
                        nc.vector.reciprocal(rden[u][:], rden[u][:]).then_inc(divided[u], 1)
                        dve.wait_ge(divided[u], it * 2 + 2)
                        for k in range(HEADS):
                            last = nc.vector.tensor_tensor(part[u][:, k, :, :], rows[:, :, k, 0:D],
                                                           rden[u][:, :, k:k + 1].broadcast_to([P, tiles, D]), ALU.mult)
                        last.then_inc(parted[u], 1)
                    else:
                        acc = m.acc[:, 0:T * SUPPORT_W].rearrange("p (t w) -> p t w", w=SUPPORT_W)
                        nc.vector.tensor_copy(part[u][:, 0, :, :], group(acc, it, u)[:, :, 0:D]).then_inc(parted[u], 1)

                def step(it, more):
                    for u in range(2):
                        dve.wait_ge(acts[u], it + 1)
                        nc.vector.tensor_tensor(r[u][:], r[u][:], hn[u][:], ALU.mult).then_inc(dv[u], 1)
                    for u in range(2):
                        dve.wait_ge(dv[u], it * 3 + 1)
                        dve.wait_ge(newed[u], it)
                        nc.vector.tensor_tensor(cand[u][:], ps_g[2][u], r[u][:], ALU.add).then_inc(gates_read[u], 1)
                    if more:
                        supports(it + 1, 0)
                        supports(it + 1, 1)
                    for u in range(2):
                        dve.wait_ge(tanhed[u], it + 1)
                        dve.wait_ge(back[u], it)
                        h = m.hT[:, bass.ds(it * (2 * span) + u * span, span)]
                        nc.vector.tensor_tensor(new[u][:], h, cand[u][:], ALU.subtract).then_inc(dv[u], 1)
                    for u in range(2):
                        dve.wait_ge(dv[u], it * 3 + 2)
                        nc.vector.tensor_tensor(new[u][:], new[u][:], z[u][:], ALU.mult).then_inc(dv[u], 1)
                    for u in range(2):
                        dve.wait_ge(dv[u], it * 3 + 3)
                        nc.vector.tensor_tensor(new[u][:], new[u][:], cand[u][:], ALU.add).then_inc(newed[u], 1)
                    for u in range(2):
                        dve.wait_ge(back[u], it + 1)
                        dve.wait_ge(added[u], it * 2)
                        dia = m.diagonal[:, bass.ds(it * (2 * tiles) + u * tiles, tiles)].rearrange(
                            "p (g o) -> p g o", o=1)
                        nc.vector.tensor_tensor(scaled[u][:], ps_b[u].rearrange("p (g d) -> p g d", d=D),
                                                dia.broadcast_to([P, tiles, D]), ALU.mult).then_inc(added[u], 1)
                    for u in range(2):
                        dve.wait_ge(added[u], it * 2 + 1)
                        at = group(m.x, it, u)
                        nc.vector.tensor_tensor(at, at, scaled[u][:], ALU.add).then_inc(added[u], 1)

                supports(0, 0)
                supports(0, 1)
                with dve.Fori(0, last_step) as it:
                    step(it, more=True)
                step(last_step, more=False)

            @block.tensor
            def _(pe):
                def turn(it, u):
                    pe.wait_ge(parted[u], it + 1)
                    pe.wait_ge(copied[u], it)
                    for k in range(heads):
                        for g in range(tiles):
                            last = nc.tensor.transpose(ps_t[k][u][:, g * P:(g + 1) * P], part[u][:, k, g, :], m.ident[:])
                    last.then_inc(turned[u], 1)

                def step(it, more):
                    for u in range(2):
                        pe.wait_ge(copied[u], it + 1)
                        if which:
                            for k in range(HEADS):
                                last = nc.tensor.matmul(ps_e[u], m.w2[:, k, :], partT[u][:, k, :], start=k == 0,
                                                        stop=k == HEADS - 1)
                            last.then_inc(mixed[u], 1)
                    for u in range(2):
                        if which:
                            pe.wait_ge(mixed_copied[u], it + 1)
                        pe.wait_ge(gates_read[u], it)
                        pe.wait_ge(acts[u], it)
                        pe.wait_ge(added[u], it * 2)
                        support = sT[u][:] if which else partT[u][:, 0, :]
                        h = m.hT[:, bass.ds(it * (2 * span) + u * span, span)]
                        nc.tensor.matmul(ps_g[3][u], m.whh[:, which, 2 * D:3 * D], h, start=True, stop=True)
                        for k in range(2):
                            c = slice(k * D, (k + 1) * D)
                            nc.tensor.matmul(ps_g[k][u], m.wih[:, which, c], support, start=True, stop=False)
                            nc.tensor.matmul(ps_g[k][u], m.whh[:, which, c], h, start=False, stop=True)
                        nc.tensor.matmul(ps_g[2][u], m.wih[:, which, 2 * D:3 * D], support, start=True,
                                         stop=True).then_inc(gated[u], 1)
                    if more:
                        turn(it + 1, 0)
                        turn(it + 1, 1)
                    for u in range(2):
                        pe.wait_ge(newed[u], it + 1)
                        for g in range(tiles):
                            last = nc.tensor.transpose(ps_b[u][:, g * P:(g + 1) * P], new[u][:, g * P:(g + 1) * P],
                                                       m.ident[:])
                        last.then_inc(back[u], 1)

                turn(0, 0)
                turn(0, 1)
                with pe.Fori(0, last_step) as it:
                    step(it, more=True)
                step(last_step, more=False)

            @block.scalar
            def _(act):
                def copy(it, u):
                    act.wait_ge(turned[u], it + 1)
                    act.wait_ge(gated[u], it)
                    for k in range(heads):
                        last = nc.scalar.copy(partT[u][:, k, :], ps_t[k][u])
                    last.then_inc(copied[u], 1)

                def step(it, more):
                    if which:
                        for u in range(2):
                            act.wait_ge(mixed[u], it + 1)
                            nc.scalar.mul(sT[u][:], ps_e[u], 1.0 / HEADS).then_inc(mixed_copied[u], 1)
                    for u in range(2):
                        act.wait_ge(gated[u], it + 1)
                        act.wait_ge(newed[u], it)
                        nc.scalar.activation(r[u][:], ps_g[0][u], ACT.Sigmoid, bias=m.bsum[:, which, 0:1])
                        nc.scalar.activation(z[u][:], ps_g[1][u], ACT.Sigmoid, bias=m.bsum[:, which, 1:2])
                        nc.scalar.activation(hn[u][:], ps_g[3][u], ACT.Identity, bias=m.bhh[:, which, 2:3]).then_inc(
                            acts[u], 1)
                    for u in range(2):
                        act.wait_ge(gates_read[u], it + 1)
                        nc.scalar.activation(cand[u][:], cand[u][:], ACT.Tanh, bias=m.bih[:, which, 2:3]).then_inc(
                            tanhed[u], 1)
                    if more:
                        copy(it + 1, 0)
                        copy(it + 1, 1)

                copy(0, 0)
                copy(0, 1)
                with act.Fori(0, last_step) as it:
                    step(it, more=True)
                step(last_step, more=False)


def stage_select(nc, m, a):
    rounds = -(-TOPK // 8)
    with Stage(nc) as ctx:
        adj, filtered, left = (m.shift2[:, i * N:(i + 1) * N] for i in range(3))
        top = ctx.enter_context(nc.sbuf_tensor("tk_top", [P, 8], F32))
        turned = ctx.enter_context(nc.sbuf_tensor("tk_turned", [P, 4, P], F32))
        ps = ctx.enter_context(nc.psum_tensor("tk_ps", [P, 4, P], F32))
        loaded, squared, tanhed, dv, chosen, turns, copies, stores = (
            ctx.sem("tk_" + x) for x in ("loaded", "squared", "tanhed", "dve", "chosen", "turns", "copies", "stores"))
        blocks = T // 4
        dst = a["selected"].rearrange("(q b j) i -> j q b i", b=4, j=P)
        own = 2 * rounds + 3
        with nc.Block() as block:
            @block.sync
            def _(sp):
                with where(sp, m, CROWDED):
                    with sp.Fori(0, T) as t:
                        sp.wait_ge(turns, t * blocks)
                        sp.nop(nofuse=True)
                        sp.dma_start(adj, a["adj"][bass.ds(t * P, P), :]).then_inc(loaded, 16)
                        for q in range(blocks):
                            sp.wait_ge(copies, t * blocks + (q + 1))
                            sp.nop(nofuse=True)
                            sp.dma_start(dst[:, q:q + 1, :, bass.ds(t * P, P)].rearrange("j o b i -> j (o b) i"),
                                         turned[:]).then_inc(stores, 16)
                    sp.wait_ge(stores, 16 * T * blocks)

            @block.scalar
            def _(act):
                with where(act, m, CROWDED):
                    with act.Fori(0, T) as t:
                        act.wait_ge(squared, t + 1)
                        nc.scalar.activation(filtered, filtered, ACT.Tanh).then_inc(tanhed, 1)
                        for q in range(blocks):
                            act.wait_ge(turns, t * blocks + (q + 1))
                            act.wait_ge(stores, t * (blocks * 16) + q * 16)
                            nc.scalar.copy(turned[:], ps[:]).then_inc(copies, 1)

            @block.tensor
            def _(pe):
                with where(pe, m, CROWDED):
                    with pe.Fori(0, T) as t:
                        pe.wait_ge(chosen, t + 1)
                        for q in range(blocks):
                            pe.wait_ge(copies, t * blocks + q)
                            for b in range(4):
                                last = nc.tensor.transpose(ps[:, b, :], adj[:, (q * 4 + b) * P:(q * 4 + b + 1) * P], m.ident[:])
                            last.then_inc(turns, 1)

            @block.vector
            def _(dve):
                with where(dve, m, CROWDED):
                    with dve.Fori(0, T) as t:
                        dve.wait_ge(loaded, t * 16 + 16)
                        dve.wait_ge(chosen, t)
                        nc.vector.scalar_tensor_tensor(out=filtered, in0=adj, scalar=0.0, in1=adj, op0=ALU.max,
                                                       op1=ALU.mult).then_inc(squared, 1)
                        dve.wait_ge(tanhed, t + 1)
                        nc.vector.tensor_copy(left, filtered).then_inc(dv, 1)
                        dve.wait_ge(dv, t * own + 1)
                        dve.nop(nofuse=True)
                        with dve.Fori(0, rounds - 1) as r:
                            nc.vector.max(out=top[:], in_=left).then_inc(dv, 1)
                            dve.wait_ge(dv, t * own + r * 2 + 2)
                            dve.nop(nofuse=True)
                            nc.vector.match_replace(out=left, in_to_replace=top[:], in_values=left,
                                                    imm_value=-1.0).then_inc(dv, 1)
                            dve.wait_ge(dv, t * own + r * 2 + 3)
                            dve.nop(nofuse=True)
                        nc.vector.max(out=top[:], in_=left).then_inc(dv, 1)
                        dve.wait_ge(dv, t * own + 2 * rounds)
                        nc.vector.memset(top[:, 8 - (8 * rounds - TOPK):8], -2.0).then_inc(dv, 1)
                        dve.wait_ge(dv, t * own + (2 * rounds + 1))
                        dve.nop(nofuse=True)
                        nc.vector.match_replace(out=left, in_to_replace=top[:], in_values=left,
                                                imm_value=-1.0).then_inc(dv, 1)
                        dve.wait_ge(dv, t * own + (2 * rounds + 2))
                        nc.vector.tensor_scalar(left, left, 0.0, None, ALU.is_lt).then_inc(dv, 1)
                        dve.wait_ge(dv, t * own + (2 * rounds + 3))
                        nc.vector.tensor_tensor(adj, adj, left, ALU.mult).then_inc(chosen, 1)


def stage_repack(nc, m, a):
    with Stage(nc) as ctx:
        index = ctx.enter_context(nc.sbuf_tensor("rp_index", [P, PAIR], U32))
        adj = ctx.enter_context(nc.sbuf_tensor("rp_adj", [P, PAIR, P], F32))
        index_ready, gathered, packed = (ctx.sem("rp_" + x) for x in ("index_ready", "gathered", "packed"))
        rows = a["selected"].rearrange("j (t i) -> (j t) i", i=P)
        with nc.Block() as block:
            @block.scalar
            def _(act):
                with where(act, m, CROWDED):
                    n = runs(nc, act, m)
                    with act.Fori(0, n * SETS) as g:
                        act.wait_ge(gathered, g * (16 * PAIR))
                        nc.scalar.copy(index[:], m.index[:, bass.ds(g * PAIR, PAIR), 0]).then_inc(index_ready, 1)

            @block.gpsimd
            def _(pool):
                with where(pool, m, CROWDED):
                    n = runs(nc, pool, m)
                    with pool.Fori(0, n * SETS) as g:
                        pool.wait_ge(index_ready, g + 1)
                        pool.wait_ge(packed, g * 16)
                        pool.nop(nofuse=True)
                        for h in range(PAIR):
                            nc.gpsimd.indirect_dma_start(
                                out=adj[:, h, :], out_offset=None, in_=rows,
                                in_offset=bass.IndirectOffsetOnAxis(ap=index[:, h:h + 1], axis=0)).then_inc(gathered, 16)

            @block.sync
            def _(sp):
                with where(sp, m, CROWDED):
                    n = runs(nc, sp, m)
                    with sp.Fori(0, n * SETS) as g:
                        sp.wait_ge(gathered, (g + 1) * (16 * PAIR))
                        sp.dma_start(a["adj_pack"][:, bass.ds(g, 1), :].rearrange("p o w -> p (o w)"),
                                     adj[:].rearrange("p h i -> p (h i)")).then_inc(packed, 16)
                    sp.wait_ge(packed, n * (SETS * 16))
                    sp.nop(nofuse=True)


def stage_filter_pairs(nc, m, a):
    with Stage(nc) as ctx:
        w = Walk(nc, m, a, "g6", ctx)
        index = w.sb("index", [P, PAIR, 2], U32)
        adj = w.sb("adj", [P, PAIR, P])
        square = w.sb("square", [P, PAIR, P])
        feat = w.sb("feat", [P, PAIR, D])
        ps = w.ps("ps", [P, 512])
        index_ready, gathered, adj_loaded, squared, filtered, summed, added = (
            w.sem(x) for x in ("index_ready", "gathered", "adj_loaded", "squared", "filtered", "summed", "added"))
        with nc.Block() as block:
            @block.gpsimd
            def _(pool):
                n = runs(nc, pool, m)
                with pool.Fori(0, n) as it:
                    for s in range(SETS):
                        pool.wait_ge(index_ready[s], it + 1)
                        pool.wait_ge(summed[s], it)
                        pool.nop(nofuse=True)
                        for h in range(PAIR):
                            nc.gpsimd.indirect_dma_start(
                                out=feat[s][:, h, :], out_offset=None, in_=a["table3"],
                                in_offset=bass.IndirectOffsetOnAxis(ap=index[s][:, h, 1:2], axis=0)).then_inc(gathered[s], 16)

            @block.sync
            def _(sp):
                n = runs(nc, sp, m)
                with sp.Fori(0, n) as it:
                    for s in range(SETS):
                        sp.wait_ge(squared[s], it)
                        sp.dma_start(adj[s][:].rearrange("p h i -> p (h i)"), pair_of(a["adj_pack"], it, s)).then_inc(
                            adj_loaded[s], 16)

            @block.scalar
            def _(act):
                n = runs(nc, act, m)
                with act.Fori(0, n) as it:
                    for s in range(SETS):
                        act.wait_ge(gathered[s], it * (16 * PAIR))
                        nc.scalar.copy(index[s][:], m.index[:, bass.ds((it * SETS + s) * PAIR, PAIR), :]).then_inc(
                            index_ready[s], 1)
                    for s in range(SETS):
                        act.wait_ge(squared[s], it + 1)
                        nc.scalar.activation(square[s][:], square[s][:], ACT.Tanh).then_inc(filtered[s], 1)

            @block.tensor
            def _(pe):
                n = runs(nc, pe, m)
                with pe.Fori(0, n) as it:
                    for s in range(SETS):
                        pe.wait_ge(gathered[s], (it + 1) * (16 * PAIR))
                        pe.wait_ge(filtered[s], it + 1)
                        pe.wait_ge(added[s], it)
                        for h in range(PAIR):
                            last = nc.tensor.matmul(ps[s][:, 0:D], square[s][:, h, :], feat[s][:, h, :],
                                                    start=h == 0, stop=h == PAIR - 1)
                        last.then_inc(summed[s], 1)

            @block.vector
            def _(dve):
                n = runs(nc, dve, m)
                with dve.Fori(0, n) as it:
                    for s in range(SETS):
                        dve.wait_ge(adj_loaded[s], it * 16 + 16)
                        dve.wait_ge(summed[s], it)
                        nc.vector.scalar_tensor_tensor(out=square[s][:], in0=adj[s][:], scalar=0.0, in1=adj[s][:],
                                                       op0=ALU.max, op1=ALU.mult).then_inc(squared[s], 1)
                    tiles = tiles_of_step(nc, dve, m, it)
                    for s in range(SETS):
                        dve.wait_ge(summed[s], it + 1)
                        dve.wait_ge(added[s - 1], it + (s > 0))
                        at = m.acc[:, bass.ds(tiles[s] * D, D)]
                        nc.vector.tensor_tensor(at, at, ps[s][:, 0:D], ALU.add).then_inc(added[s], 1)


def stage_output(nc, m, a):
    with Stage(nc) as ctx:
        step, stored = (ctx.sem("out_" + x) for x in ("step", "stored"))
        parts = 4
        size = T // parts
        out = a["out"].rearrange("(t p) d -> p t d", p=P)
        acc = m.acc[:, 0:T * D].rearrange("p (t d) -> p t d", d=D)
        with nc.Block() as block:
            @block.vector
            def _(dve):
                for c in range(parts):
                    at = slice(c * size, (c + 1) * size)
                    bias = m.bg[:].rearrange("p (o d) -> p o d", o=1).broadcast_to([P, size, D])
                    nc.vector.tensor_tensor(acc[:, at, :], acc[:, at, :], bias, ALU.add).then_inc(step, 1)
                    dve.wait_ge(step, 2 * c + 1)
                    nc.vector.scalar_tensor_tensor(
                        out=m.x[:, at, :].rearrange("p t d -> p (t d)"), in0=acc[:, at, :].rearrange("p t d -> p (t d)"),
                        scalar=0.0, in1=m.x[:, at, :].rearrange("p t d -> p (t d)"), op0=ALU.max,
                        op1=ALU.add).then_inc(step, 1)

            @block.sync
            def _(sp):
                for c in range(parts):
                    at = slice(c * size, (c + 1) * size)
                    sp.wait_ge(step, 2 * c + 2)
                    sp.dma_start(out[:, at, :], m.x[:, at, :]).then_inc(stored, 16)
                sp.wait_ge(stored, 16 * parts)


def stage_clear(nc, m, a, what):
    with Stage(nc) as ctx:
        done = ctx.sem(f"clear_{what}")
        with nc.Block() as block:
            @block.vector
            def _(dve):
                if what == "best":
                    nc.vector.memset(m.best1[:], -BIG).then_inc(done, 1)
                    nc.vector.memset(m.best2[:], -BIG).then_inc(done, 1)
                    nc.vector.memset(m.s1_wide[:, N:N + P], 0.0).then_inc(done, 1)
                    nc.vector.memset(m.shift1[:, N:N + P], BIG).then_inc(done, 1)
                    nc.vector.memset(m.shift2[:, T * HEADS * P:], BIG).then_inc(done, 1)
                else:
                    nc.vector.memset(m.acc[:], 0.0).then_inc(done, 1)


SCRATCH = {
    "selected": (N, N), "table0": (N, 2 * D), "table1": (N, D + 2), "table2": (N, UV_END), "table3": (N, D),
    "score_table": (2 * N, 4), "row_scratch": (T * HEADS * P,),
    "adj_pack": (P, CAP, PAIR * P), "off_pack": (P, CAP, PAIR * P), "wh_pack": (P, CAP, PAIR * (D + 2)),
    "h_pack": (P, CAP, PAIR * UV_END), "score_pack0": (P, CAP, PAIR * 4), "score_pack1": (P, CAP, PAIR * 4),
}


def build(nc, a):
    for name, shape in SCRATCH.items():
        a[name] = nc.dram_tensor("scratch_" + name, shape, F32, kind="Internal").ap()
    with ExitStack() as ctx:
        def sb(name, shape, dt=F32):
            return ctx.enter_context(nc.sbuf_tensor("m_" + name, shape, dt))

        m = Space()
        m.x = sb("x", [P, T, D])
        m.acc = sb("acc", [P, (T + 1) * HEAD_W])
        m.hT = sb("hT", [P, N])
        m.shift2 = sb("shift2", [P, T * HEADS * P + HEADS * P])
        m.s1_wide = m.shift2[:, 0:N + P]
        m.shift1 = m.shift2[:, N + P:2 * (N + P)]
        m.index = sb("index", [P, CAP * PAIR + MAX_PAIRS * PAIR, 2], U32)
        m.meta = sb("meta", [1, 5], I32)
        m.tiles = sb("tiles", [1, CAP // SETS], I32)
        m.best1 = sb("best1", [P, T + 1])
        m.best1c = sb("best1c", [P, T])
        m.best2 = sb("best2", [P, T + 1, HEADS])
        m.hsum = sb("hsum", [P, GROUPS])
        m.ident = sb("ident", [P, P])
        m.identb = sb("identb", [P, P], BF16)
        m.ones = sb("ones", [P, P])
        m.row_ramp = sb("row_ramp", [P, P])
        m.class_of = sb("class_of", [P, 1])
        m.class_over = sb("class_over", [P, CLASSES - 1])
        m.sixteens = sb("sixteens", [P, CLASSES - 1])
        m.b0 = sb("b0", [P, 6])
        m.bm = sb("bm", [1, D])
        m.eps = sb("eps", [P, 2])
        m.w1 = sb("w1", [P, D + 1])
        m.w1t = sb("w1t", [P, D])
        m.a1 = sb("a1", [P, 2])
        m.wa1 = sb("wa1", [P, 1])
        m.wa1_wide = sb("wa1_wide", [P, P])
        m.w2 = sb("w2", [P, HEADS, D])
        m.w2t = sb("w2t", [P, HEADS, D])
        m.a2 = sb("a2", [P, HEADS, 2])
        m.uv = sb("uv", [P, 2 * HEADS])
        m.wih = sb("wih", [P, 2, 3 * D])
        m.whh = sb("whh", [P, 2, 3 * D])
        m.bih = sb("bih", [P, 2, 3])
        m.bhh = sb("bhh", [P, 2, 3])
        m.bsum = sb("bsum", [P, 2, 3])
        m.wp = sb("wp", [P, D])
        m.bp = sb("bp", [P, 1])
        m.wg = sb("wg", [P, D])
        m.bg = sb("bg", [P, D])
        m.diagonal = sb("diagonal", [P, T])

        m.best2c = sb("best2c", [P, T * HEADS])
        early = ExitStack()
        m.relative = early.enter_context(nc.sbuf_tensor("m_relative", [P, CAP * PAIR + MAX_PAIRS * PAIR], F32))
        m.active = early.enter_context(nc.sbuf_tensor("m_active", [P, 4, CLASSES, T], F32))
        m.w0 = early.enter_context(nc.sbuf_tensor("m_w0", [P, 6, D], F32))
        m.wm = early.enter_context(nc.sbuf_tensor("m_wm", [P, 2, D], F32))
        stage_weights(nc, m, a)
        stage_scan(nc, m, a)
        stage_clear(nc, m, a, "best")
        stage_index(nc, m, a)
        stage_norm(nc, m, a, 0)
        stage_gin_pairs(nc, m, a)
        stage_gin_dense(nc, m, a)
        early.close()
        stage_norm(nc, m, a, 1)
        stage_gat_max(nc, m, a)
        stage_gat_shift(nc, m, a)
        stage_gat_pairs(nc, m, a)
        stage_gat_dense(nc, m, a)
        stage_norm(nc, m, a, 2)
        stage_signed_sums(nc, m, a)
        stage_signed_scores(nc, m, a)
        stage_gru(nc, m, a, 0)
        stage_clear(nc, m, a, "sums")
        stage_signed_max(nc, m, a, 1)
        stage_signed_max(nc, m, a, -1)

        def before(dve, ready):
            nc.vector.tensor_scalar(m.best2c[:], m.best2[:, 0:T, :].rearrange("p t k -> p (t k)"), -0.1 * BIG, None,
                                    ALU.max).then_inc(ready, 1)

        spread_rows(nc, m, a, "sh2", m.best2c[:], m.shift2[:, 0:T * HEADS * P], a["row_scratch"], T * HEADS, before)
        stage_signed_pairs(nc, m, a, 1)
        stage_signed_pairs(nc, m, a, -1)
        stage_gru(nc, m, a, 1)
        stage_norm(nc, m, a, 3)
        stage_select(nc, m, a)
        stage_repack(nc, m, a)
        stage_filter_pairs(nc, m, a)
        stage_output(nc, m, a)


_AS_THEY_ARE = ["x", "L0_gnn_x2", "L0_gnn_eps1", "L0_gnn_eps2", "L0_gnn_bm", "L1_gnn_W", "L1_gnn_a", "L2_gnn_gat_W",
                "L2_gnn_gat_a", "L3_gnn_W_proj", "L3_gnn_b_proj", "L3_gnn_W_gcn", "L3_gnn_b_gcn"]


def layout(inputs):
    import numpy as _np

    i = {k: _np.asarray(v) for k, v in inputs.items()}
    c = _np.ascontiguousarray
    arrays = {k: c(i[k]) for k in _AS_THEY_ARE}
    arrays["adj"] = c(i["adj"])
    arrays["adjT"] = c(i["adj"].T)
    arrays["adj_diagonal"] = c(_np.diagonal(i["adj"]).reshape(T, P).T)
    arrays["L0_WT"] = c(_np.stack([i["L0_gnn_W1"], i["L0_gnn_W2"]]).transpose(0, 1, 3, 2))
    arrays["L0_bT"] = c(_np.stack([i["L0_gnn_b1"], i["L0_gnn_b2"]]))
    arrays["L0_WmT"] = c(i["L0_gnn_Wm"].T)
    arrays["L1_WT"] = c(i["L1_gnn_W"].T)
    arrays["L2_WT"] = c(i["L2_gnn_gat_W"].transpose(0, 2, 1))
    arrays["L2_WihT"] = c(_np.stack([i["L2_gnn_edge_Wih"].T, i["L2_gnn_node_Wih"].T]))
    arrays["L2_WhhT"] = c(_np.stack([i["L2_gnn_edge_Whh"].T, i["L2_gnn_node_Whh"].T]))
    arrays["L2_bih"] = c(_np.stack([i["L2_gnn_edge_bih"], i["L2_gnn_node_bih"]]))
    arrays["L2_bhh"] = c(_np.stack([i["L2_gnn_edge_bhh"], i["L2_gnn_node_bhh"]]))
    return arrays


def kernel(**inputs):
    import concourse.bacc as _bacc
    from concourse import mybir as _mybir
    from concourse.bass_utils import run_bass_kernel_spmd as _run

    nc = _bacc.Bacc("TRN2", target_bir_lowering=False, num_devices=1)
    arrays = {f"in_{k}_dram": v for k, v in layout(inputs).items()}
    args = {k[3:-5]: nc.dram_tensor(k, v.shape, _mybir.dt.from_np(v.dtype), kind="ExternalInput").ap()
            for k, v in arrays.items()}
    args["out"] = nc.dram_tensor("out_0_dram", (N, D), F32, kind="ExternalOutput").ap()
    build(nc, args)
    r = _run(nc, [arrays], core_ids=[0])
    return r.results[0]["out_0_dram"]
```

```python
from contextlib import ExitStack, contextmanager

import concourse.bass as bass
from concourse import mybir

F32 = mybir.dt.float32
BF16 = mybir.dt.bfloat16
I32 = mybir.dt.int32
U32 = mybir.dt.uint32
ALU = mybir.AluOpType
ACT = mybir.ActivationFunctionType
AX = mybir.AxisListType

N = 4096
D = 128
P = 128
T = N // P
CLASSES = 8
QUARTERS = 4
SIDES = 2
JJ = N // CLASSES
PAIR = 2
TAKEN = PAIR * P // CLASSES
MAX_PAIRS = JJ // TAKEN
CAP = T * MAX_PAIRS
SETS = 4
HEADS = 3
GROUP = 4
GROUPS = T // GROUP
WIDE = GROUP * P
ALPHA = 0.2
EPS = 1e-5
BIG = 1e30
TOPK = 350
STEPS, ROUNDS, NEGATIVES, CROWDED, LAST = range(5)


UV_END = D + 2 * HEADS + 1
SIGN_W = UV_END - D
SUPPORT_W = D + 2 * SIGN_W
HEAD_W = HEADS * (D + 1)


class Space:
    pass


class Stage(ExitStack):

    def __init__(self, nc):
        super().__init__()
        self.nc, self.sems = nc, []

    def sem(self, name):
        self.sems.append(self.nc.alloc_semaphore(name=name))
        return self.sems[-1]

    def __exit__(self, *exc):
        if exc[0] is None:
            self.nc.clear_and_free_semaphores(self.sems)
            self.nc.all_engine_barrier()
        return super().__exit__(*exc)


def runs(nc, eng, m):
    return eng.value_load(m.meta[0:1, STEPS:STEPS + 1], min_val=1, max_val=CAP // SETS)


def last_run(nc, eng, m):
    return eng.value_load(m.meta[0:1, LAST:LAST + 1], min_val=T // SETS - 1, max_val=CAP // SETS - 1)


@contextmanager
def where(eng, m, flag):
    if flag is None:
        yield
        return
    with eng.If(eng.value_load(m.meta[0:1, flag:flag + 1], min_val=0, max_val=1) > 0):
        yield
        eng.nop(nofuse=True)


def row_stats(nc, dve, m, first, count):
    for i in range(count):
        ins = nc.vector.bn_stats(m.stats[:, bass.ds(first + i, 1), :].rearrange("p o w -> p (o w)"),
                                 m.x[:, bass.ds(first + i, 1), :].rearrange("p o d -> p (o d)"))
    return ins


def word_of_step(nc, eng, m, step):
    return eng.value_load(m.tiles[0:1, bass.ds(step, 1)], min_val=0, max_val=(1 << 24) - 1)


def tiles_in(nc, eng, word):
    return [nc.s_assert_within(eng.snap((word >> (6 * s)) & 63), 0, T,
                               skip_runtime_bounds_check_because="the table holds 0 to T") for s in range(SETS)]


def tiles_of_step(nc, eng, m, step):
    return tiles_in(nc, eng, word_of_step(nc, eng, m, step))


def stage_scan(nc, m, a):
    with Stage(nc) as ctx:
        ring = [m.acc[:, b * N:(b + 1) * N] for b in range(3)] + [m.shift2[:, 0:N]]
        block_loaded = [ctx.sem(f"scan_loaded{i}") for i in range(4)]
        reduced = [ctx.sem(f"scan_reduced{i}") for i in range(4)]
        src = a["adjT"].rearrange("(part p c) i -> c part p i", part=4, c=CLASSES)
        x_loaded, loaded, identity_step, folded, vec, copied, aggregated, rooted, scaled = (
            ctx.sem("w_" + x) for x in ("x_loaded", "loaded", "identity_step", "folded", "vector", "copied",
                                        "aggregated", "rooted", "scaled"))
        normed, stored = ([ctx.sem(f"w_{x}{u}") for u in range(2)] for x in ("normed", "stored"))
        variance, scale, shift = (ctx.enter_context(nc.sbuf_tensor("w_" + x, [P, T], F32))
                                  for x in ("variance", "scale", "shift"))
        rows = [ctx.enter_context(nc.sbuf_tensor(f"w_rows{u}", [P, GROUP, D], F32)) for u in range(2)]
        ps = ctx.enter_context(nc.psum_tensor("w_ps", [P, 8], F32))
        table = a["table0"].rearrange("(t p) w -> p t w", p=P)
        loads = [
            (m.w0, a["L0_WT"].rearrange("b l i o -> i (b l) o")),
            (m.wm, a["L0_WmT"].rearrange("(b i) o -> i b o", b=2)),
            (m.b0, a["L0_bT"].rearrange("b l d -> d (b l)")),
            (m.bm, a["L0_gnn_bm"].rearrange("(a d) -> a d", a=1)),
            (m.eps[:, 0:1], a["L0_gnn_eps1"].rearrange("(a d) -> a d", a=1).broadcast_to([P, 1])),
            (m.eps[:, 1:2], a["L0_gnn_eps2"].rearrange("(a d) -> a d", a=1).broadcast_to([P, 1])),
            (m.w1[:, 0:D], a["L1_gnn_W"]),
            (m.w1t, a["L1_WT"]),
            (m.a1, a["L1_gnn_a"].rearrange("(s d) o -> d (s o)", s=2)),
            (m.w2, a["L2_gnn_gat_W"].rearrange("k i o -> i k o")),
            (m.w2t, a["L2_WT"].rearrange("k o i -> o k i")),
            (m.a2, a["L2_gnn_gat_a"].rearrange("k (s d) o -> d k (s o)", s=2)),
            (m.wih, a["L2_WihT"].rearrange("g i o -> i g o")),
            (m.whh, a["L2_WhhT"].rearrange("g i o -> i g o")),
            (m.bih, a["L2_bih"].rearrange("g (c d) -> d g c", d=D)),
            (m.bhh, a["L2_bhh"].rearrange("g (c d) -> d g c", d=D)),
            (m.wp, a["L3_gnn_W_proj"]),
            (m.bp, a["L3_gnn_b_proj"].rearrange("(d a) -> d a", a=1)),
            (m.wg, a["L3_gnn_W_gcn"]),
            (m.bg, a["L3_gnn_b_gcn"].rearrange("(a d) -> a d", a=1).broadcast_to([P, D])),
            (m.diagonal, a["adj_diagonal"]),
            (a["table0"][:, D:2 * D], a["L0_gnn_x2"]),
        ]
        with nc.Block() as block:
            @block.sync
            def _(sp):
                with sp.Fori(0, CLASSES) as c:
                    for part in range(4):
                        sp.wait_ge(reduced[part], c)
                        sp.dma_start(ring[part], src[bass.ds(c, 1), part, :, :].rearrange("c p i -> p (c i)")
                                     ).then_inc(block_loaded[part], 16)

            @block.scalar
            def _(act):
                act.dma_start(m.x[:], a["x"].rearrange("(t p) d -> p t d", p=P)).then_inc(x_loaded, 16)
                with nc.allow_non_contiguous_dma(reason="biases and the diagonal, once"):
                    for dst, src in loads:
                        act.dma_start(dst if isinstance(dst, bass.AP) else dst[:], src).then_inc(loaded, 16)
                act.wait_ge(aggregated, T + 1)
                nc.scalar.activation(variance[:], variance[:], ACT.Sqrt).then_inc(rooted, 1)
                act.wait_ge(scaled, 1)
                with act.Fori(0, GROUPS // 2) as it:
                    for u in range(2):
                        act.wait_ge(stored[u], 16 * it)
                        for i in range(GROUP):
                            tile = it * (2 * GROUP) + (u * GROUP + i)
                            last = nc.scalar.activation(
                                rows[u][:, i, :], m.x[:, bass.ds(tile, 1), :].rearrange("p o d -> p (o d)"),
                                ACT.Relu, bias=shift[:, bass.ds(tile, 1)], scale=scale[:, bass.ds(tile, 1)])
                        last.then_inc(normed[u], 1)
                        act.wait_ge(normed[u], it + 1)
                        act.dma_start(table[:, bass.ds(it * (2 * GROUP) + u * GROUP, GROUP), 0:D], rows[u][:]
                                      ).then_inc(stored[u], 16)
                for u in range(2):
                    act.wait_ge(stored[u], 16 * (GROUPS // 2))
                act.wait_ge(loaded, 16 * len(loads))

            @block.gpsimd
            def _(pool):
                nc.gpsimd.memset(m.ident[:], 0.0).then_inc(identity_step, 1)
                pool.wait_ge(identity_step, 1)
                nc.gpsimd.affine_select(out=m.ident[:], in_=m.ident[:], compare_op=ALU.not_equal, fill=1.0,
                                        base=0, pattern=[[-1, P]], channel_multiplier=1).then_inc(identity_step, 1)
                nc.gpsimd.memset(m.identb[:], 0.0).then_inc(identity_step, 1)
                pool.wait_ge(identity_step, 3)
                nc.gpsimd.affine_select(out=m.identb[:], in_=m.identb[:], compare_op=ALU.not_equal, fill=1.0,
                                        base=0, pattern=[[-1, P]], channel_multiplier=1).then_inc(identity_step, 1)

            @block.tensor
            def _(pe):
                pe.wait_ge(loaded, 16 * len(loads))
                nc.tensor.matmul(ps[:, 0:2], m.w1t[:], m.a1[:], start=True, stop=True)
                for k in range(HEADS):
                    last = nc.tensor.matmul(ps[:, 2 + 2 * k:4 + 2 * k], m.w2t[:, k, :], m.a2[:, k, :],
                                            start=True, stop=True)
                last.then_inc(folded, 1)

            @block.vector
            def _(dve):
                nc.vector.memset(m.ones[:], 1.0).then_inc(vec, 1)
                dve.wait_ge(x_loaded, 16)
                for t in range(0, T, GROUP):
                    row_stats(nc, dve, m, t, GROUP).then_inc(copied, 1)
                dve.wait_ge(copied, GROUPS)
                scales_of_rows(nc, dve, m, variance, scale, shift, aggregated, rooted, scaled)
                with dve.Fori(0, CLASSES) as c:
                    for part in range(4):
                        dve.wait_ge(block_loaded[part], 16 * c + 16)
                        nc.vector.tensor_reduce(
                            m.active[:, part, bass.ds(c, 1), :], ring[part].rearrange("p (t i) -> p t i", i=P),
                            AX.X, ALU.max, apply_absolute_value=True).then_inc(reduced[part], 1)
                dve.wait_ge(loaded, 16 * len(loads))
                dve.wait_ge(folded, 1)
                nc.vector.tensor_copy(m.w1[:, D:D + 1], ps[:, 1:2]).then_inc(vec, 1)
                nc.vector.tensor_copy(m.uv[:], ps[:, 2:8]).then_inc(vec, 1)
                nc.vector.tensor_copy(m.wa1[:], ps[:, 0:1]).then_inc(vec, 1)
                dve.wait_ge(vec, 4)
                nc.vector.tensor_scalar(m.wa1_wide[:], m.ones[:], m.wa1[:, 0:1], None, ALU.mult).then_inc(vec, 1)
                nc.vector.tensor_scalar(m.eps[:], m.eps[:], 2.0, None, ALU.add).then_inc(vec, 1)
                nc.vector.tensor_tensor(m.bsum[:], m.bih[:], m.bhh[:], ALU.add).then_inc(vec, 1)
                dve.wait_ge(vec, 7)
                nc.vector.tensor_scalar(m.bsum[:], m.bsum[:], 0.5, None, ALU.mult).then_inc(vec, 1)
                nc.vector.tensor_scalar(m.bhh[:], m.bhh[:], 0.5, None, ALU.mult).then_inc(vec, 1)


def stage_index(nc, m, a):
    with Stage(nc) as ctx:
        def sb(name, shape, dt=F32):
            return ctx.enter_context(nc.sbuf_tensor("ix_" + name, shape, dt))

        def sem(name):
            return ctx.sem("ix_" + name)

        flags = sb("flags", [P, 4, SIDES, P], BF16)
        ramp = sb("ramp", [P, SIDES, JJ])
        keys = sb("keys", [P, SIDES, JJ])
        step32 = sb("step32", [P, MAX_PAIRS])
        counts = sb("counts", [P, SIDES])
        most = sb("most", [P, 1])
        over = sb("over", [P, MAX_PAIRS])
        pairs_of_list = sb("pairs_of_list", [P, 1])
        pairs = sb("pairs", [1, T])
        ends = sb("ends", [1, 2, T])
        starts = sb("starts", [1, T])
        starts_two = sb("starts_two", [1, T // 2])
        starts_i = sb("starts_i", [1, T // 2], I32)
        step4 = sb("step4", [1, CAP // SETS])
        over4 = sb("over4", [1, CAP // SETS])
        meta_f = sb("meta_f", [1, 2])
        ends_col = sb("ends_col", [T, 1])
        pair_ramp = sb("pair_ramp", [T, CAP])
        passed = sb("passed", [T, CAP])
        packed = sb("packed", [1, CAP // SETS])
        taken = sb("taken", [P, PAIR, SIDES, TAKEN // PAIR])
        turned = sb("turned", [P, PAIR, SIDES * TAKEN // PAIR])
        lists = sb("lists", [P, MAX_PAIRS * PAIR, T])
        high = sb("high", [P, MAX_PAIRS * PAIR, T])
        tile_ramp = sb("tile_ramp", [P, MAX_PAIRS * PAIR, T])
        offset = sb("offset", [P, 1])
        ps_keys = ctx.enter_context(nc.psum_tensor("ix_ps_keys", [P, SIDES, JJ], F32))
        ps_small = ctx.enter_context(nc.psum_tensor("ix_ps_small", [P, 512], F32))
        ps_tiles = ctx.enter_context(nc.psum_tensor("ix_ps_tiles", [P, CAP], F32))
        pool_step, flagged, keyed, listed, row, col, col_done, tiled, dv = (
            sem(x) for x in ("pool_step", "flagged", "keyed", "listed", "row", "col", "col_done", "tiled", "dve_step"))
        took = sem("took")
        copied = sem("copied")

        with nc.Block() as block:
            @block.gpsimd
            def _(pool):
                nc.gpsimd.iota(ramp[:], pattern=[[0, SIDES], [-1, JJ]], base=JJ - 1, channel_multiplier=0,
                               allow_small_or_imprecise_dtypes=True).then_inc(pool_step, 1)
                nc.gpsimd.iota(step32[:], pattern=[[TAKEN, MAX_PAIRS]], base=0, channel_multiplier=0,
                               allow_small_or_imprecise_dtypes=True).then_inc(pool_step, 1)
                nc.gpsimd.iota(step4[:], pattern=[[SETS, CAP // SETS]], base=0, channel_multiplier=0,
                               allow_small_or_imprecise_dtypes=True).then_inc(pool_step, 1)
                nc.gpsimd.iota(pair_ramp[:], pattern=[[1, CAP]], base=0, channel_multiplier=0,
                               allow_small_or_imprecise_dtypes=True).then_inc(pool_step, 1)
                nc.gpsimd.iota(tile_ramp[:], pattern=[[0, MAX_PAIRS * PAIR], [1, T]], base=0, channel_multiplier=0,
                               allow_small_or_imprecise_dtypes=True).then_inc(pool_step, 1)
                nc.gpsimd.iota(m.row_ramp[:], pattern=[[1, P]], base=0, channel_multiplier=0,
                               allow_small_or_imprecise_dtypes=True).then_inc(pool_step, 1)
                nc.gpsimd.iota(m.class_of[:], pattern=[[0, 1]], base=0, channel_multiplier=1,
                               allow_small_or_imprecise_dtypes=True).then_inc(pool_step, 1)
                nc.gpsimd.iota(m.sixteens[:], pattern=[[16, CLASSES - 1]], base=16, channel_multiplier=0,
                               allow_small_or_imprecise_dtypes=True).then_inc(pool_step, 1)
                nc.gpsimd.memset(m.acc[:], 0.0)

            @block.tensor
            def _(pe):
                pe.wait_ge(flagged, 1)
                for side in range(SIDES):
                    for part in range(4):
                        last = nc.tensor.matmul(ps_keys[:, side, part * P:(part + 1) * P], flags[:, part, side, :],
                                                m.identb[:], start=True, stop=True)
                last.then_inc(keyed, 1)
                pe.wait_ge(listed, 1)
                nc.tensor.matmul(ps_small[0:1, 0:P], pairs_of_list[:], m.ident[:], start=True, stop=True).then_inc(row, 1)
                pe.wait_ge(col, 1)
                nc.tensor.matmul(ps_small[0:T, 128:129], ends[:, 1, :], m.ones[0:1, 0:1], start=True,
                                 stop=True).then_inc(col_done, 1)
                pe.wait_ge(tiled, 1)
                nc.tensor.matmul(ps_tiles[0:1, :], m.ones[0:T, 0:1], passed[:], start=True, stop=True).then_inc(tiled, 1)

            @block.vector
            def _(dve):
                steps = [0]

                def done(ins):
                    steps[0] += 1
                    ins.then_inc(dv, 1)
                    dve.wait_ge(dv, steps[0])

                dve.wait_ge(pool_step, 8)
                done(nc.vector.tensor_scalar(m.class_over[:], m.sixteens[:], m.class_of[:, 0:1], None, ALU.is_le))
                done(nc.vector.tensor_reduce(m.class_of[:], m.class_over[:], AX.X, ALU.add))
                by_side = m.active[:].rearrange("p a (q s) t -> p a s q t", s=SIDES)
                for side in range(SIDES):
                    last = nc.vector.tensor_scalar(
                        flags[:, :, side, :].rearrange("p a (q t) -> p a q t", q=QUARTERS), by_side[:, :, side, :, :],
                        0.0, None, ALU.is_gt)
                last.then_inc(flagged, 1)
                dve.wait_ge(keyed, 1)
                done(nc.vector.scalar_tensor_tensor(out=keys[:], in0=ps_keys[:], scalar=2.0 * JJ, in1=ramp[:],
                                                    op0=ALU.mult, op1=ALU.add))
                done(nc.vector.tensor_reduce(counts[:], ps_keys[:], AX.X, ALU.add))
                done(nc.vector.tensor_reduce(most[:], counts[:], AX.X, ALU.max))
                done(nc.vector.tensor_scalar(over[:], step32[:], most[:, 0:1], None, ALU.is_lt))
                nc.vector.tensor_reduce(pairs_of_list[:], over[:], AX.X, ALU.add).then_inc(listed, 1)
                dve.wait_ge(row, 1)
                done(nc.vector.tensor_reduce(pairs[:], ps_small[0:1, 0:P].rearrange("o (q t) -> o t q", q=QUARTERS),
                                             AX.X, ALU.max))
                done(nc.vector.tensor_scalar(pairs[:], pairs[:], 1.0, None, ALU.max))
                done(nc.vector.tensor_reduce(meta_f[:, 1:2], pairs[:], AX.X, ALU.max))
                done(nc.vector.tensor_copy(ends[:, 0, :], pairs[:]))
                src = 0
                for shift in (1, 2, 4, 8, 16):
                    dst = 1 - src
                    done(nc.vector.tensor_copy(ends[:, dst, 0:shift], ends[:, src, 0:shift]))
                    done(nc.vector.tensor_tensor(ends[:, dst, shift:T], ends[:, src, shift:T],
                                                 ends[:, src, 0:T - shift], ALU.add))
                    src = dst
                nc.vector.tensor_tensor(starts[:], ends[:, 1, :], pairs[:], ALU.subtract).then_inc(col, 1)
                dve.wait_ge(col, 1)
                by_two = starts[:].rearrange("o (n u) -> o u n", u=2)
                done(nc.vector.scalar_tensor_tensor(out=starts_two[:], in0=by_two[:, 1, :], scalar=1024.0,
                                                    in1=by_two[:, 0, :], op0=ALU.mult, op1=ALU.add))
                done(nc.vector.tensor_copy(starts_i[:], starts_two[:]))
                done(nc.vector.tensor_scalar(over4[:], step4[:], ends[:, 1, T - 1:T], None, ALU.is_lt))
                done(nc.vector.tensor_reduce(meta_f[:, 0:1], over4[:], AX.X, ALU.add))
                done(nc.vector.tensor_copy(m.meta[:, 0:2], meta_f[:]))
                done(nc.vector.tensor_scalar(m.meta[:, LAST:LAST + 1], meta_f[:, 0:1], -1.0, None, ALU.add))
                dve.wait_ge(col_done, 1)
                done(nc.vector.tensor_copy(ends_col[:], ps_small[0:T, 128:129]))
                nc.vector.tensor_scalar(passed[:], pair_ramp[:], ends_col[:, 0:1], None, ALU.is_ge).then_inc(tiled, 1)
                dve.wait_ge(tiled, 2)
                by_set = ps_tiles[0:1, :].rearrange("o (n s) -> o s n", s=SETS)
                done(nc.vector.tensor_copy(packed[:], by_set[:, 0, :]))
                for s in range(1, SETS):
                    done(nc.vector.scalar_tensor_tensor(out=packed[:], in0=by_set[:, s, :], scalar=float(64 ** s),
                                                        in1=packed[:], op0=ALU.mult, op1=ALU.add))
                done(nc.vector.tensor_copy(m.tiles[:], packed[:]))
                done(nc.vector.memset(lists[:], 0.0))
                half = TAKEN // PAIR
                rounds = dve.value_load(m.meta[0:1, ROUNDS:ROUNDS + 1], min_val=1, max_val=MAX_PAIRS)
                per_round = 2 * PAIR * SIDES * (half // 8) + 1
                with dve.Fori(0, rounds) as r:
                    k = 0
                    for part in range(TAKEN // 8):
                        h, e = divmod(part * 8, half)
                        for side in range(SIDES):
                            nc.vector.max(out=taken[:, h, side, e:e + 8], in_=keys[:, side, :]).then_inc(took, 1)
                        k += SIDES
                        dve.wait_ge(took, r * per_round + k)
                        dve.nop(nofuse=True)
                        for side in range(SIDES):
                            nc.vector.match_replace(out=keys[:, side, :], in_to_replace=taken[:, h, side, e:e + 8],
                                                    in_values=keys[:, side, :], imm_value=-1.0).then_inc(took, 1)
                        k += SIDES
                        dve.wait_ge(took, r * per_round + k)
                        dve.nop(nofuse=True)
                    for h in range(PAIR):
                        last = nc.vector.transpose(turned[:, h, :], taken[:, h, :, :].rearrange("p s e -> p (s e)"))
                    last.then_inc(took, 1)
                    dve.wait_ge(took, r * per_round + k + 1)
                    nc.vector.tensor_copy(lists[:, bass.ds(r * PAIR, PAIR), :], turned[:]).then_inc(copied, 1)
                    dve.wait_ge(copied, r + 1)
                flat = lists[:]
                done(nc.vector.tensor_scalar(high[:], flat, 2.0 * JJ, -2.0 * JJ, ALU.is_ge, ALU.mult))
                done(nc.vector.tensor_tensor(flat, flat, high[:], ALU.add))
                done(nc.vector.tensor_scalar(offset[:], m.class_of[:], float(CLASSES * (JJ - 1)), None, ALU.add))
                done(nc.vector.tensor_scalar(flat, flat, -float(CLASSES), offset[:, 0:1], ALU.mult, ALU.add))
                done(nc.vector.scalar_tensor_tensor(out=high[:], in0=flat, scalar=float(T), in1=tile_ramp[:],
                                                    op0=ALU.mult, op1=ALU.add))
                done(nc.vector.scalar_tensor_tensor(out=tile_ramp[:], in0=tile_ramp[:], scalar=-float(P), in1=flat,
                                                    op0=ALU.mult, op1=ALU.add))
                done(nc.vector.memset(m.index[:], 0))
                done(nc.vector.memset(m.relative[:], 0.0))
                base = steps[0]
                with dve.Fori(0, T // 2) as t2:
                    word = dve.value_load(starts_i[0:1, bass.ds(t2, 1)], min_val=0, max_val=(1 << 20) - 1)
                    length = MAX_PAIRS * PAIR
                    for u in range(2):
                        t = t2 * 2 + u
                        start = nc.s_assert_within(dve.snap((word >> (10 * u)) & 1023), 0, CAP - 1,
                                                   skip_runtime_bounds_check_because="a start is a pair's number")
                        for kind, what in ((0, high), (1, flat)):
                            nc.vector.tensor_copy(
                                m.index[:, bass.ds(start * PAIR, length), kind:kind + 1],
                                what[:, :, bass.ds(t, 1)]).then_inc(dv, 1)
                        nc.vector.tensor_copy(m.relative[:, bass.ds(start * PAIR, length)],
                                              tile_ramp[:, :, bass.ds(t, 1)].rearrange("p l o -> p (l o)")).then_inc(dv, 1)
                        dve.wait_ge(dv, t2 * 6 + (base + 3 * u + 3))


def scales_of_rows(nc, dve, m, variance, scale, shift, aggregated, rooted, scaled):
    for t in range(T):
        nc.vector.bn_aggr(m.moments[:, t, :], m.stats[:, t, :]).then_inc(aggregated, 1)
    dve.wait_ge(aggregated, T)
    nc.vector.tensor_scalar(variance[:], m.moments[:, :, 1], EPS, None, ALU.add).then_inc(aggregated, 1)
    dve.wait_ge(rooted, 1)
    nc.vector.reciprocal(scale[:], variance[:]).then_inc(aggregated, 1)
    dve.wait_ge(aggregated, T + 2)
    nc.vector.scalar_tensor_tensor(out=shift[:], in0=m.moments[:, :, 0], scalar=-1.0, in1=scale[:],
                                   op0=ALU.mult, op1=ALU.mult).then_inc(scaled, 1)


def stage_norm(nc, m, a, layer):
    with Stage(nc) as ctx:
        def sb(name, shape, dt=F32):
            return [ctx.enter_context(nc.sbuf_tensor(f"n{layer}_{name}{u}", shape, dt)) for u in range(2)]

        def sem(name):
            return [ctx.sem(f"n{layer}_{name}{u}") for u in range(2)]

        width = {1: D + 2, 2: UV_END, 3: D}[layer]
        variance = ctx.enter_context(nc.sbuf_tensor(f"n{layer}_variance", [P, T], F32))
        scale = ctx.enter_context(nc.sbuf_tensor(f"n{layer}_scale", [P, T], F32))
        shift = ctx.enter_context(nc.sbuf_tensor(f"n{layer}_shift", [P, T], F32))
        rows = sb("rows", [P, GROUP, width])
        hrow = sb("hrow", [P, GROUP, D])
        hT = sb("hT", [P, WIDE])
        h2T = sb("h2T", [P, WIDE]) if layer == 3 else None
        ps_t = [ctx.enter_context(nc.psum_tensor(f"n{layer}_ps_t{u}", [P, WIDE], F32)) for u in range(2)]
        ps_w = [ctx.enter_context(nc.psum_tensor(f"n{layer}_ps_w{u}", [P, GROUP, 256 if layer == 1 else 128], F32))
                for u in range(2)]
        ps_s = ([ctx.enter_context(nc.psum_tensor(f"n{layer}_ps_s{u}", [P, WIDE], F32)) for u in range(2)]
                if layer in (1, 3) else None)
        ones_set = ctx.sem(f"n{layer}_ones_set")
        aggregated, rooted, scaled = (ctx.sem(f"n{layer}_{x}") for x in ("aggregated", "rooted", "scaled"))
        normed, turned, hT_ready, projected, rows_ready, stored, s_done, s_read, h2_ready = (
            sem(x) for x in ("normed", "turned", "hT_ready", "projected", "rows_ready", "stored", "s_done", "s_read",
                             "h2_ready"))
        dst = a[f"table{layer}"].rearrange("(t p) w -> p t w", p=P)
        steps = GROUPS // 2

        def tiles(tensor, it, u):
            return tensor[:, bass.ds(it * (2 * GROUP) + u * GROUP, GROUP), :]

        with nc.Block() as block:
            @block.gpsimd
            def _(pool):
                nc.gpsimd.memset(m.acc[:], 0.0)

            @block.vector
            def _(dve):
                if layer in (1, 2):
                    for u in range(2):
                        one = D if layer == 1 else UV_END - 1
                        nc.vector.memset(rows[u][:, :, one:one + 1], 1.0).then_inc(ones_set, 1)
                    dve.wait_ge(ones_set, 2)
                scales_of_rows(nc, dve, m, variance, scale, shift, aggregated, rooted, scaled)
                with dve.Fori(0, steps) as it:
                    def finish(u, it):
                        dve.wait_ge(stored[u], 16 * it)
                        if layer == 2:
                            dve.wait_ge(normed[u], it + 1)
                            nc.vector.tensor_copy(rows[u][:, :, 0:D], hrow[u][:]).then_inc(rows_ready[u], 1)
                        dve.wait_ge(projected[u], it + 1)
                        if layer == 1:
                            nc.vector.tensor_copy(rows[u][:, :, 0:D], ps_w[u][:, :, 0:D]).then_inc(rows_ready[u], 1)
                            nc.vector.tensor_copy(rows[u][:, :, D + 1:D + 2], ps_w[u][:, :, D:D + 1]).then_inc(
                                rows_ready[u], 1)
                            nc.vector.tensor_reduce(m.hsum[:, bass.ds(it * 2 + u, 1)], hT[u][:], AX.X, ALU.add
                                                    ).then_inc(rows_ready[u], 1)
                        elif layer == 2:
                            nc.vector.tensor_copy(rows[u][:, :, D:D + 2 * HEADS], ps_w[u][:, :, 0:2 * HEADS]).then_inc(
                                rows_ready[u], 1)
                        else:
                            nc.vector.tensor_copy(rows[u][:], ps_w[u][:]).then_inc(rows_ready[u], 1)

                    finish(0, it)
                    finish(1, it)

            @block.scalar
            def _(act):
                act.wait_ge(aggregated, T + 1)
                nc.scalar.activation(variance[:], variance[:], ACT.Sqrt).then_inc(rooted, 1)
                act.wait_ge(scaled, 1)

                def norm(it, u):
                    act.wait_ge(turned[u], it)
                    if layer == 2:
                        act.wait_ge(rows_ready[u], 2 * it)
                    for i in range(GROUP):
                        tile = it * (2 * GROUP) + (u * GROUP + i)
                        last = nc.scalar.activation(
                            hrow[u][:, i, 0:D], m.x[:, bass.ds(tile, 1), :].rearrange("p o d -> p (o d)"),
                            ACT.Relu, bias=shift[:, bass.ds(tile, 1)], scale=scale[:, bass.ds(tile, 1)])
                    last.then_inc(normed[u], 1)

                def turn(it, u):
                    act.wait_ge(turned[u], it + 1)
                    act.wait_ge(projected[u], it)
                    if layer == 1:
                        act.wait_ge(s_done[u], it)
                        act.wait_ge(rows_ready[u], 3 * it)
                    nc.scalar.copy(hT[u][:], ps_t[u][:]).then_inc(hT_ready[u], 1)
                    if layer == 2:
                        nc.scalar.copy(m.hT[:, bass.ds(it * (2 * WIDE) + u * WIDE, WIDE)], ps_t[u][:]).then_inc(
                            hT_ready[u], 1)

                def second(it, u):
                    if layer == 1:
                        act.wait_ge(s_done[u], it + 1)
                        nc.scalar.copy(m.s1_wide[:, bass.ds(it * (2 * WIDE) + u * WIDE, WIDE)], ps_s[u][:]).then_inc(
                            s_read[u], 1)
                    if layer == 3:
                        act.wait_ge(s_done[u], it + 1)
                        act.wait_ge(projected[u], it)
                        nc.scalar.activation(h2T[u][:], ps_s[u][:], ACT.Tanh, bias=m.bp[:, 0:1]).then_inc(
                            h2_ready[u], 1)

                def step(it, more):
                    turn(it, 0)
                    turn(it, 1)
                    for u in range(2):
                        if more:
                            norm(it + 1, u)
                        second(it, u)

                norm(0, 0)
                norm(0, 1)
                with act.Fori(0, steps - 1) as it:
                    step(it, more=True)
                step(steps - 1, more=False)

            @block.tensor
            def _(pe):
                with pe.Fori(0, steps) as it:
                    for u in range(2):
                        pe.wait_ge(normed[u], it + 1)
                        pe.wait_ge(hT_ready[u], (2 if layer == 2 else 1) * it)
                        for i in range(GROUP):
                            last = nc.tensor.transpose(ps_t[u][:, i * P:(i + 1) * P], hrow[u][:, i, 0:D], m.ident[:])
                        last.then_inc(turned[u], 1)
                    for u in range(2):
                        pe.wait_ge(hT_ready[u], (2 if layer == 2 else 1) * it + 1)
                        if layer == 1:
                            pe.wait_ge(s_read[u], it)
                            nc.tensor.matmul(ps_s[u][:], m.wa1_wide[:], hT[u][:], start=True, stop=True).then_inc(
                                s_done[u], 1)
                            pe.wait_ge(rows_ready[u], 3 * it)
                            for i in range(GROUP):
                                last = nc.tensor.matmul(ps_w[u][:, i, 0:D + 1], hT[u][:, i * P:(i + 1) * P], m.w1[:],
                                                        start=True, stop=True)
                        elif layer == 2:
                            pe.wait_ge(rows_ready[u], 2 * it)
                            for i in range(GROUP):
                                last = nc.tensor.matmul(ps_w[u][:, i, 0:2 * HEADS], hT[u][:, i * P:(i + 1) * P],
                                                        m.uv[:], start=True, stop=True)
                        else:
                            pe.wait_ge(h2_ready[u], it)
                            nc.tensor.matmul(ps_s[u][:], m.wp[:], hT[u][:], start=True, stop=True).then_inc(
                                s_done[u], 1)
                            pe.wait_ge(h2_ready[u], it + 1)
                            pe.wait_ge(rows_ready[u], it)
                            for i in range(GROUP):
                                last = nc.tensor.matmul(ps_w[u][:, i, :], h2T[u][:, i * P:(i + 1) * P], m.wg[:],
                                                        start=True, stop=True)
                        last.then_inc(projected[u], 1)

            @block.sync
            def _(sp):
                with sp.Fori(0, steps) as it:
                    for u in range(2):
                        sp.wait_ge(rows_ready[u], (it + 1) * {1: 3, 2: 2, 3: 1}[layer])
                        sp.dma_start(tiles(dst, it, u)[:, :, 0:width], rows[u][:]).then_inc(stored[u], 16)
                for u in range(2):
                    sp.wait_ge(stored[u], 16 * steps)


class Walk:

    def __init__(self, nc, m, a, name, ctx):
        self.nc, self.m, self.a, self.name, self.ctx = nc, m, a, name, ctx

    def sb(self, name, shape, dt=F32, sets=SETS):
        return [self.ctx.enter_context(self.nc.sbuf_tensor(f"{self.name}_{name}{s}", shape, dt)) for s in range(sets)]

    def halves(self, name, shape, dt=F32):
        return self.ctx.enter_context(self.nc.sbuf_tensor(f"{self.name}_{name}", [P, 2] + shape, dt))

    def ps(self, name, shape, sets=SETS):
        return [self.ctx.enter_context(self.nc.psum_tensor(f"{self.name}_{name}{s}", shape, F32)) for s in range(sets)]

    def sem(self, name, sets=SETS):
        return [self.ctx.sem(f"{self.name}_{name}{s}") for s in range(sets)]


def pair_of(tensor, it, s):
    return tensor[:, bass.ds(it * SETS + s, 1), :].rearrange("p o w -> p (o w)")


def step_of(tensor, it):
    return tensor[:, bass.ds(it * SETS, SETS), :].rearrange("p s w -> p (s w)")


def half_of(buffer, it):
    return buffer[:, bass.ds(it & 1, 1), :, :, :].rearrange("p o s h w -> p (o s h w)")


def pair_in(buffer, it, s):
    return buffer[:, bass.ds(it & 1, 1), s:s + 1, :, :].rearrange("p a b h w -> p (a b h) w")


def stage_gin_pairs(nc, m, a):
    with Stage(nc) as ctx:
        w = Walk(nc, m, a, "g0", ctx)
        index = w.sb("index", [P, PAIR, 2], U32)
        adj = w.sb("adj", [P, PAIR, P])
        off = w.sb("off", [P, PAIR, P])
        feat = w.sb("feat", [P, PAIR, 2 * D])
        ps = w.ps("ps", [P, 512])
        index_ready, gathered, summed, off_ready, packed, off_packed, added = (
            w.sem(x) for x in ("index_ready", "gathered", "summed", "off_ready", "packed", "off_packed", "added"))
        lows = ctx.enter_context(nc.sbuf_tensor("g0_lows", [P, CAP], F32))
        low = ctx.enter_context(nc.sbuf_tensor("g0_low", [P, 2], F32))
        cleared, lowest, turned = (ctx.sem("g0_" + x) for x in ("cleared", "lowest", "turned"))
        gathers = 16 * 2 * PAIR
        adj_rows = a["adjT"].rearrange("j (t i) -> (j t) i", i=P)
        with nc.Block() as block:
            @block.scalar
            def _(act):
                n = runs(nc, act, m)
                with act.Fori(0, n) as it:
                    for s in range(SETS):
                        act.wait_ge(gathered[s], it * gathers)
                        nc.scalar.copy(index[s][:], m.index[:, bass.ds((it * SETS + s) * PAIR, PAIR), :]).then_inc(
                            index_ready[s], 1)

            @block.gpsimd
            def _(pool):
                n = runs(nc, pool, m)
                with pool.Fori(0, n) as it:
                    for s in range(SETS):
                        pool.wait_ge(index_ready[s], it + 1)
                        pool.wait_ge(summed[s], it)
                        pool.wait_ge(off_ready[s], it * 2)
                        pool.wait_ge(packed[s], 16 * it)
                        pool.nop(nofuse=True)
                        for h in range(PAIR):
                            nc.gpsimd.indirect_dma_start(
                                out=adj[s][:, h, :], out_offset=None, in_=adj_rows,
                                in_offset=bass.IndirectOffsetOnAxis(ap=index[s][:, h, 0:1], axis=0)).then_inc(gathered[s], 16)
                            nc.gpsimd.indirect_dma_start(
                                out=feat[s][:, h, :], out_offset=None, in_=a["table0"],
                                in_offset=bass.IndirectOffsetOnAxis(ap=index[s][:, h, 1:2], axis=0)).then_inc(gathered[s], 16)

            @block.tensor
            def _(pe):
                n = runs(nc, pe, m)
                with pe.Fori(0, n) as it:
                    for s in range(SETS):
                        pe.wait_ge(gathered[s], (it + 1) * gathers)
                        pe.wait_ge(added[s], it)
                        for h in range(PAIR):
                            last = nc.tensor.matmul(ps[s][:, 0:2 * D], adj[s][:, h, :], feat[s][:, h, :],
                                                    start=h == 0, stop=h == PAIR - 1)
                        last.then_inc(summed[s], 1)
                pe.wait_ge(lowest, 1)
                nc.tensor.matmul(ps[0][0:1, 2 * D:2 * D + P], low[:, 0:1], m.ident[:], start=True, stop=True).then_inc(
                    turned, 1)

            @block.vector
            def _(dve):
                n = runs(nc, dve, m)
                nc.vector.memset(lows[:], 0.0).then_inc(cleared, 1)
                dve.wait_ge(cleared, 1)
                with dve.Fori(0, n) as it:
                    tiles = tiles_of_step(nc, dve, m, it)
                    for s in range(SETS):
                        dve.wait_ge(gathered[s], (it + 1) * gathers)
                        dve.wait_ge(off_packed[s], 16 * it)
                        for h in range(PAIR):
                            last = nc.vector.scalar_tensor_tensor(
                                out=off[s][:, h, :], in0=m.row_ramp[:],
                                scalar=m.relative[:, bass.ds((it * SETS + s) * PAIR + h, 1)], in1=adj[s][:, h, :],
                                op0=ALU.not_equal, op1=ALU.mult)
                        last.then_inc(off_ready[s], 1)
                        dve.wait_ge(summed[s], it + 1)
                        dve.wait_ge(added[s - 1], it + (s > 0))
                        at = m.acc[:, bass.ds(tiles[s] * (2 * D), 2 * D)]
                        nc.vector.tensor_tensor(at, at, ps[s][:, 0:2 * D], ALU.add).then_inc(added[s], 1)
                        dve.wait_ge(off_ready[s], it * 2 + 1)
                        nc.vector.tensor_reduce(lows[:, bass.ds(it * SETS + s, 1)],
                                                off[s][:].rearrange("p h i -> p (h i)"), AX.X, ALU.min).then_inc(
                                                    off_ready[s], 1)
                for s in range(SETS):
                    dve.wait_ge(off_ready[s], n * 2)
                nc.vector.tensor_reduce(low[:, 0:1], lows[:], AX.X, ALU.min).then_inc(lowest, 1)
                dve.wait_ge(turned, 1)
                nc.vector.tensor_reduce(low[0:1, 1:2], ps[0][0:1, 2 * D:2 * D + P], AX.X, ALU.min).then_inc(lowest, 1)
                dve.wait_ge(lowest, 2)
                nc.vector.tensor_scalar(m.meta[:, NEGATIVES:NEGATIVES + 1], low[0:1, 1:2], 0.0, None, ALU.is_lt)

            @block.sync
            def _(sp):
                n = runs(nc, sp, m)
                with sp.Fori(0, n) as it:
                    for s in range(SETS):
                        sp.wait_ge(gathered[s], (it + 1) * gathers)
                        sp.dma_start(pair_of(a["adj_pack"], it, s), adj[s][:].rearrange("p h i -> p (h i)")).then_inc(
                            packed[s], 16)
                        sp.wait_ge(off_ready[s], it * 2 + 1)
                        sp.dma_start(pair_of(a["off_pack"], it, s), off[s][:].rearrange("p h i -> p (h i)")).then_inc(
                            off_packed[s], 16)
                for s in range(SETS):
                    sp.wait_ge(packed[s], 16 * n)
                    sp.wait_ge(off_packed[s], 16 * n)
                    sp.nop(nofuse=True)


def stage_gin_dense(nc, m, a):
    with Stage(nc) as ctx:
        def sb(name, shape):
            return [ctx.enter_context(nc.sbuf_tensor(f"d0_{name}{b}", shape, F32)) for b in range(2)]

        def ps(name):
            return [ctx.enter_context(nc.psum_tensor(f"d0_{name}{b}", [P, WIDE], F32)) for b in range(2)]

        def sem(name):
            return [ctx.sem(f"d0_{name}{b}") for b in range(2)]

        scaled = sb("scaled", [P, GROUP, D])
        act_in = [sb(f"layer{l}_", [P, WIDE]) for l in range(4)]
        ps_t = ps("ps_t")
        ps_l = ps("ps_l")
        ps_o = ps("ps_o")
        scaled_ready, turned, multiplied, activated, merged, added = (
            sem(x) for x in ("scaled_ready", "turned", "multiplied", "activated", "merged", "added"))
        acc = m.acc[:, 0:T * 2 * D].rearrange("p (t b d) -> p t b d", b=2, d=D)
        with nc.Block() as block:
            @block.vector
            def _(dve):
                def add(u, it):
                    dve.wait_ge(merged[u], it + 1)
                    at = m.x[:, bass.ds(it * (2 * GROUP) + u * GROUP, GROUP), :]
                    nc.vector.tensor_tensor(at, at, ps_o[u][:].rearrange("p (g d) -> p g d", d=D), ALU.add).then_inc(
                        added[u], 1)

                def scale(u, it):
                    for b in range(2):
                        dve.wait_ge(turned[b], it * 2 + u)
                        nc.vector.tensor_scalar(
                            scaled[b][:], acc[:, bass.ds(it * (2 * GROUP) + u * GROUP, GROUP), b, :],
                            m.eps[:, b:b + 1], None, ALU.mult).then_inc(scaled_ready[b], 1)

                def step(it, more):
                    scale(1, it)
                    add(0, it)
                    if more:
                        scale(0, it + 1)
                    dve.wait_ge(added[0], it + 1)
                    row_stats(nc, dve, m, it * (2 * GROUP), GROUP)
                    add(1, it)
                    dve.wait_ge(added[1], it + 1)
                    row_stats(nc, dve, m, it * (2 * GROUP) + GROUP, GROUP)

                scale(0, 0)
                with dve.Fori(0, GROUPS // 2 - 1) as it:
                    step(it, more=True)
                step(GROUPS // 2 - 1, more=False)

            @block.tensor
            def _(pe):
                with pe.Fori(0, GROUPS // 2) as it:
                    for u in range(2):
                        g = it * 2 + u
                        for b in range(2):
                            pe.wait_ge(scaled_ready[b], g + 1)
                            pe.wait_ge(activated[b], g * 4)
                            for i in range(GROUP):
                                last = nc.tensor.transpose(ps_t[b][:, i * P:(i + 1) * P], scaled[b][:, i, :], m.ident[:])
                            last.then_inc(turned[b], 1)
                        for l in range(3):
                            for b in range(2):
                                pe.wait_ge(activated[b], g * 4 + (l + 1))
                                nc.tensor.matmul(ps_l[b][:], m.w0[:, b * 3 + l, :], act_in[l][b][:], start=True,
                                                 stop=True).then_inc(multiplied[b], 1)
                        for b in range(2):
                            pe.wait_ge(activated[b], g * 4 + 4)
                        pe.wait_ge(added[u], it)
                        for i in range(GROUP):
                            out = ps_o[u][:, i * P:(i + 1) * P]
                            for b in range(2):
                                nc.tensor.matmul(out, act_in[3][b][:, i * P:(i + 1) * P], m.wm[:, b, :],
                                                 start=b == 0, stop=False)
                            last = nc.tensor.matmul(out, m.ones[0:1, :], m.bm[:], start=False, stop=True)
                        last.then_inc(merged[u], 1)

            @block.scalar
            def _(act):
                with act.Fori(0, GROUPS // 2) as it:
                    for u in range(2):
                        g = it * 2 + u
                        for b in range(2):
                            act.wait_ge(turned[b], g + 1)
                            if u:
                                act.wait_ge(merged[0], it + 1)
                            else:
                                act.wait_ge(merged[1], it)
                            nc.scalar.copy(act_in[0][b][:], ps_t[b][:]).then_inc(activated[b], 1)
                        for l in range(3):
                            for b in range(2):
                                act.wait_ge(multiplied[b], g * 3 + (l + 1))
                                nc.scalar.activation(act_in[l + 1][b][:], ps_l[b][:], ACT.Relu,
                                                     bias=m.b0[:, b * 3 + l:b * 3 + l + 1]).then_inc(activated[b], 1)


def stage_gat_max(nc, m, a):
    with Stage(nc) as ctx:
        w = Walk(nc, m, a, "g1", ctx)
        width = D + 2
        index = w.sb("index", [P, PAIR, 2], U32)
        adj = w.halves("adj", [SETS, PAIR, P])
        feat = w.sb("feat", [P, PAIR, width])
        bias = w.sb("bias", [P, PAIR, P])
        masked = w.sb("masked", [P, PAIR, P])
        best = w.sb("best", [P, 1])
        ps = w.ps("ps", [P, 512])
        loaded = ctx.sem("g1_loaded")
        index_ready, gathered, packed, biased, masked_ready, turned, reduced, kept = (
            w.sem(x) for x in ("index_ready", "gathered", "packed", "biased", "masked_ready", "turned", "reduced",
                               "kept"))
        with nc.Block() as block:
            @block.gpsimd
            def _(pool):
                n = runs(nc, pool, m)
                with pool.Fori(0, n) as it:
                    for s in range(SETS):
                        pool.wait_ge(index_ready[s], it + 1)
                        pool.wait_ge(packed[s], 16 * it)
                        pool.wait_ge(masked_ready[s], it)
                        pool.nop(nofuse=True)
                        for h in range(PAIR):
                            nc.gpsimd.indirect_dma_start(
                                out=feat[s][:, h, :], out_offset=None, in_=a["table1"],
                                in_offset=bass.IndirectOffsetOnAxis(ap=index[s][:, h, 1:2], axis=0)).then_inc(gathered[s], 16)

            @block.sync
            def _(sp):
                n = runs(nc, sp, m)
                sp.dma_start(half_of(adj, 0), step_of(a["adj_pack"], 0)).then_inc(loaded, 16)
                sp.wait_ge(loaded, 16)
                sp.dma_start(half_of(adj, 1), step_of(a["adj_pack"], 1)).then_inc(loaded, 16)
                with sp.Fori(2, n) as it:
                    sp.wait_ge(loaded, it * 16)
                    sp.nop(nofuse=True)
                    sp.wait_ge(biased[SETS - 1], it - 1)
                    sp.nop(nofuse=True)
                    sp.dma_start(half_of(adj, it), step_of(a["adj_pack"], it)).then_inc(loaded, 16)

            @block.scalar
            def _(act):
                n = runs(nc, act, m)
                for s in range(SETS):
                    nc.scalar.copy(index[s][:], m.index[:, s * PAIR:(s + 1) * PAIR, :]).then_inc(index_ready[s], 1)
                with act.Fori(0, n) as it:
                    for s in range(SETS):
                        act.wait_ge(gathered[s], (it + 1) * (16 * PAIR))
                        nc.scalar.dma_start(pair_of(a["wh_pack"], it, s), feat[s][:].rearrange("p h w -> p (h w)")
                                            ).then_inc(packed[s], 16)
                        nc.scalar.copy(index[s][:], m.index[:, bass.ds((it * SETS + SETS + s) * PAIR, PAIR), :]
                                       ).then_inc(index_ready[s], 1)
                        act.wait_ge(biased[s], it + 1)
                        act.wait_ge(turned[s], it)
                        for h in range(PAIR):
                            last = nc.scalar.activation(masked[s][:, h, :], bias[s][:, h, :], ACT.Identity,
                                                        bias=feat[s][:, h, D + 1:D + 2])
                        last.then_inc(masked_ready[s], 1)
                for s in range(SETS):
                    act.wait_ge(packed[s], 16 * n)
                act.nop(nofuse=True)

            @block.tensor
            def _(pe):
                n = runs(nc, pe, m)
                with pe.Fori(0, n) as it:
                    for s in range(SETS):
                        pe.wait_ge(masked_ready[s], it + 1)
                        pe.wait_ge(reduced[s], it)
                        for h in range(PAIR):
                            last = nc.tensor.transpose(ps[s][:, h * P:(h + 1) * P], masked[s][:, h, :], m.ident[:])
                        last.then_inc(turned[s], 1)

            @block.vector
            def _(dve):
                last = last_run(nc, dve, m)

                def mask(it, s):
                    dve.wait_ge(loaded, it * 16 + 16)
                    dve.wait_ge(masked_ready[s], it)
                    nc.vector.tensor_scalar(bias[s][:], pair_in(adj, it, s), 0.0, -BIG, ALU.is_le, ALU.mult).then_inc(
                        biased[s], 1)

                def reduce(it, s):
                    dve.wait_ge(turned[s], it + 1)
                    nc.vector.tensor_reduce(best[s][:], ps[s][:, 0:PAIR * P], AX.X, ALU.max).then_inc(reduced[s], 1)

                def keep(it, s, tile):
                    dve.wait_ge(reduced[s], it + 1)
                    dve.wait_ge(kept[s - 1], it + (s > 0))
                    at = m.best1[:, bass.ds(tile, 1)]
                    nc.vector.tensor_tensor(at, at, best[s][:], ALU.max).then_inc(kept[s], 1)

                for s in range(SETS):
                    mask(0, s)
                with dve.Fori(0, last) as it:
                    tiles = tiles_of_step(nc, dve, m, it)
                    for s in range(SETS):
                        reduce(it, s)
                        mask(it + 1, s)
                        keep(it, s, tiles[s])
                tiles = tiles_of_step(nc, dve, m, last)
                for s in range(SETS):
                    reduce(last, s)
                    keep(last, s, tiles[s])


def spread_rows(nc, m, a, name, value, wide, scratch, columns, before, clear=False):
    with Stage(nc) as ctx:
        turned, copied, stored, loaded = (
            ctx.sem(f"{name}_{x}") for x in ("turned", "copied", "stored", "loaded"))
        ps = ctx.enter_context(nc.psum_tensor(f"{name}_ps", [P, P], F32))
        rows = ctx.enter_context(nc.sbuf_tensor(f"{name}_rows", [P, P], F32))
        ready = ctx.sem(f"{name}_ready")
        with nc.Block() as block:
            @block.vector
            def _(dve):
                before(dve, ready)
                dve.wait_ge(turned, 1)
                nc.vector.tensor_copy(rows[0:columns, :], ps[0:columns, :]).then_inc(copied, 1)

            @block.gpsimd
            def _(pool):
                if clear:
                    nc.gpsimd.memset(m.acc[:], 0.0)

            @block.tensor
            def _(pe):
                pe.wait_ge(ready, 1)
                nc.tensor.transpose(ps[0:columns, :], value, m.ident[:]).then_inc(turned, 1)

            @block.sync
            def _(sp):
                sp.wait_ge(copied, 1)
                sp.dma_start(scratch.rearrange("(c i) -> c i", i=P), rows[0:columns, :]).then_inc(stored, 16)
                sp.wait_ge(stored, 16)
                sp.dma_start(wide, scratch.rearrange("(a n) -> a n", a=1).broadcast_to([P, columns * P])).then_inc(
                    loaded, 16)
                sp.wait_ge(loaded, 16)


def stage_gat_shift(nc, m, a):
    with Stage(nc) as ctx:
        def sb(name, shape):
            return ctx.enter_context(nc.sbuf_tensor("sh_" + name, shape, F32))

        best_wide = sb("best_wide", [P, N])
        step = ctx.sem("sh_step")

        def before(dve, ready):
            nc.vector.tensor_copy(m.best1c[:], m.best1[:, 0:T]).then_inc(ready, 1)

        spread_rows(nc, m, a, "sh1", m.best1c[:], best_wide[:], a["row_scratch"][0:N], T, before)
        with nc.Block() as block:
            @block.vector
            def _(dve):
                k = 0
                for c in range(4):
                    part = slice(c * 1024, (c + 1) * 1024)
                    nc.vector.tensor_tensor(best_wide[:, part], best_wide[:, part], m.s1_wide[:, part], ALU.add
                                            ).then_inc(step, 1)
                    k += 1
                    dve.wait_ge(step, k)
                    nc.vector.scalar_tensor_tensor(out=m.shift1[:, part], in0=best_wide[:, part], scalar=ALPHA,
                                                   in1=best_wide[:, part], op0=ALU.mult, op1=ALU.max).then_inc(step, 1)
                    k += 1


def stage_gat_pairs(nc, m, a):
    with Stage(nc) as ctx:
        w = Walk(nc, m, a, "g2", ctx)
        adj = w.halves("adj", [SETS, PAIR, P])
        feat = w.halves("feat", [SETS, PAIR, D + 2])
        bias = w.sb("bias", [P, PAIR, P])
        leaky = w.sb("leaky", [P, PAIR, P])
        below = w.sb("below", [P, PAIR, P])
        prob = w.sb("prob", [P, PAIR, P])
        ps = w.ps("ps", [P, 512])
        touch = ctx.enter_context(nc.sbuf_tensor("g2_touch", [1, 1], F32))
        touched = ctx.sem("g2_touched")
        adj_loaded, feat_loaded = w.sem("adj_loaded"), w.sem("feat_loaded")
        biased, placed, leaked, moved, shifted, exped, summed, added = (
            w.sem(x) for x in ("biased", "placed", "leaked", "moved", "shifted", "exped", "summed", "added"))
        with nc.Block() as block:
            @block.sync
            def _(sp):
                n = runs(nc, sp, m)

                def load(it, s, buffer, pack, loaded):
                    sp.dma_start(pair_in(buffer, it, s).rearrange("p h w -> p (h w)"), pair_of(pack, it, s)).then_inc(
                        loaded[s], 16)

                for s in range(SETS):
                    load(0, s, adj, a["adj_pack"], adj_loaded)
                    load(0, s, feat, a["wh_pack"], feat_loaded)
                for s in range(SETS):
                    sp.wait_ge(adj_loaded[s], 16)
                    load(1, s, adj, a["adj_pack"], adj_loaded)
                    sp.wait_ge(feat_loaded[s], 16)
                    load(1, s, feat, a["wh_pack"], feat_loaded)
                with sp.Fori(2, n) as it:
                    for s in range(SETS):
                        sp.wait_ge(adj_loaded[s], it * 16)
                        sp.nop(nofuse=True)
                        sp.wait_ge(biased[s], it - 1)
                        sp.nop(nofuse=True)
                        load(it, s, adj, a["adj_pack"], adj_loaded)
                        sp.wait_ge(feat_loaded[s], it * 16)
                        sp.nop(nofuse=True)
                        sp.wait_ge(summed[s], it - 1)
                        sp.nop(nofuse=True)
                        load(it, s, feat, a["wh_pack"], feat_loaded)

            @block.gpsimd
            def _(pool):
                n = runs(nc, pool, m)
                with pool.Fori(0, n) as it:
                    for s in range(SETS):
                        pool.wait_ge(moved[s], it + 1)
                        pool.wait_ge(biased[s], it + 1)
                        pool.wait_ge(exped[s], it)
                        nc.gpsimd.tensor_tensor(below[s][:], bias[s][:], leaky[s][:], ALU.add).then_inc(shifted[s], 1)

            @block.scalar
            def _(act):
                n = runs(nc, act, m)
                last = last_run(nc, act, m)

                def place(it, s, tile):
                    act.wait_ge(feat_loaded[s], it * 16 + 16)
                    act.wait_ge(shifted[s], it)
                    for h in range(PAIR):
                        ins = nc.scalar.activation(leaky[s][:, h, :], m.s1_wide[:, bass.ds(tile * P, P)],
                                                   ACT.Identity, bias=pair_in(feat, it, s)[:, h, D + 1:D + 2])
                    ins.then_inc(placed[s], 1)

                def expo(it, s):
                    act.wait_ge(shifted[s], it + 1)
                    act.wait_ge(summed[s], it)
                    nc.scalar.activation(prob[s][:], below[s][:], ACT.Exp).then_inc(exped[s], 1)

                tiles = tiles_of_step(nc, act, m, 0)
                for s in range(SETS):
                    place(0, s, tiles[s])
                    if s >= 2:
                        expo(0, s - 2)
                with act.Fori(1, n) as it:
                    act.wait_ge(touched, it - 1)
                    nc.scalar.activation(touch[:], m.ones[0:1, 0:1], ACT.Exp).then_inc(touched, 1)
                    tiles = tiles_of_step(nc, act, m, it)
                    for s in range(SETS):
                        place(it, s, tiles[s])
                        expo(it - (s < 2), (s + 2) % SETS)
                expo(last, 2)
                expo(last, 3)

            @block.tensor
            def _(pe):
                n = runs(nc, pe, m)
                with pe.Fori(0, n) as it:
                    for s in range(SETS):
                        pe.wait_ge(exped[s], it + 1)
                        pe.wait_ge(added[s], it)
                        for h in range(PAIR):
                            last = nc.tensor.matmul(ps[s][:, 0:D + 1], prob[s][:, h, :],
                                                    pair_in(feat, it, s)[:, h, 0:D + 1],
                                                    start=h == 0, stop=h == PAIR - 1)
                        last.then_inc(summed[s], 1)

            @block.vector
            def _(dve):
                n = runs(nc, dve, m)
                last = last_run(nc, dve, m)

                def mask(it, s):
                    dve.wait_ge(adj_loaded[s], it * 16 + 16)
                    dve.wait_ge(shifted[s], it)
                    nc.vector.tensor_scalar(bias[s][:], pair_in(adj, it, s), 0.0, -BIG, ALU.is_le, ALU.mult).then_inc(
                        biased[s], 1)

                def leak(it, s):
                    dve.wait_ge(placed[s], it + 1)
                    nc.vector.scalar_tensor_tensor(out=leaky[s][:], in0=leaky[s][:], scalar=ALPHA, in1=leaky[s][:],
                                                   op0=ALU.mult, op1=ALU.max).then_inc(leaked[s], 1)

                def move(it, s, tile):
                    dve.wait_ge(leaked[s], it + 1)
                    shift = m.shift1[:, bass.ds(tile * P, P)].rearrange("p (o i) -> p o i", o=1)
                    nc.vector.tensor_tensor(leaky[s][:], leaky[s][:], shift.broadcast_to([P, PAIR, P]),
                                            ALU.subtract).then_inc(moved[s], 1)

                def add(it, s, tile):
                    dve.wait_ge(summed[s], it + 1)
                    dve.wait_ge(added[s - 1], it + (s > 0))
                    at = m.acc[:, bass.ds(tile * (D + 1), D + 1)]
                    nc.vector.tensor_tensor(at, at, ps[s][:, 0:D + 1], ALU.add).then_inc(added[s], 1)

                kept_word = dve.alloc_register()
                word = word_of_step(nc, dve, m, 0)
                dve.reg_mov(kept_word, word)
                tiles = tiles_in(nc, dve, word)
                for s in range(SETS):
                    mask(0, s)
                    leak(0, s)
                    if s:
                        move(0, s - 1, tiles[s - 1])
                move(0, SETS - 1, tiles[SETS - 1])
                with dve.Fori(1, n) as it:
                    before = tiles_in(nc, dve, dve.snap(kept_word))
                    word = word_of_step(nc, dve, m, it)
                    dve.reg_mov(kept_word, word)
                    tiles = tiles_in(nc, dve, word)
                    for s in range(SETS):
                        mask(it, s)
                        leak(it, s)
                        add(it - 1, s, before[s])
                        move(it, s, tiles[s])
                tiles = tiles_of_step(nc, dve, m, last)
                for s in range(SETS):
                    add(last, s, tiles[s])


def stage_gat_dense(nc, m, a):
    with Stage(nc) as ctx:
        def sb(name, shape):
            return ctx.enter_context(nc.sbuf_tensor("d1_" + name, shape, F32))

        alone = sb("alone", [P, T])
        denom = sb("denom", [P, T])
        hsum = sb("hsum", [P, 1])
        hsum_wide = sb("hsum_wide", [P, P])
        mean = sb("mean", [P, D])
        out = [sb(f"out{u}", [P, GROUP, D]) for u in range(2)]
        low = [sb(f"low{u}", [P, GROUP, D]) for u in range(2)]
        spare = [sb(f"spare{u}", [P, GROUP, D]) for u in range(2)]
        ps = ctx.enter_context(nc.psum_tensor("d1_ps", [P, 512], F32))
        step, meaned = (ctx.sem("d1_" + x) for x in ("step", "meaned"))
        spared, scaled, filled, lowered, exped, summed, added = (
            [ctx.sem(f"d1_{x}{u}") for u in range(2)]
            for x in ("spared", "scaled", "filled", "lowered", "exped", "summed", "added"))
        acc = m.acc[:, 0:T * (D + 1)].rearrange("p (t d) -> p t d", d=D + 1)
        with nc.Block() as block:
            @block.tensor
            def _(pe):
                pe.wait_ge(step, 3)
                nc.tensor.matmul(ps[:, 0:D], hsum_wide[:], m.w1[:, 0:D], start=True, stop=True).then_inc(meaned, 1)

            @block.vector
            def _(dve):
                nc.vector.tensor_scalar(alone[:], m.best1[:, 0:T], -0.5 * BIG, None, ALU.is_lt).then_inc(step, 1)
                nc.vector.tensor_reduce(hsum[:], m.hsum[:], AX.X, ALU.add).then_inc(step, 1)
                dve.wait_ge(step, 2)
                nc.vector.tensor_scalar(hsum_wide[:], m.ones[:], hsum[:, 0:1], 1.0 / N, ALU.mult, ALU.mult).then_inc(step, 1)
                nc.vector.tensor_tensor(denom[:], acc[:, :, D], alone[:], ALU.add).then_inc(step, 1)
                dve.wait_ge(step, 4)
                nc.vector.reciprocal(denom[:], denom[:]).then_inc(step, 1)
                dve.wait_ge(meaned, 1)
                nc.vector.tensor_copy(mean[:], ps[:, 0:D]).then_inc(step, 1)
                dve.wait_ge(step, 6)
                wide = [P, GROUP, D]
                mean_wide = mean[:].rearrange("p (o d) -> p o d", o=1).broadcast_to(wide)
                with dve.Fori(0, GROUPS // 2) as it:
                    def tile(u):
                        return it * (2 * GROUP) + u * GROUP

                    for u in range(2):
                        dve.wait_ge(added[u], it)
                        lonely = alone[:, bass.ds(tile(u), GROUP)].rearrange("p (g o) -> p g o", o=1)
                        part = denom[:, bass.ds(tile(u), GROUP)].rearrange("p (g o) -> p g o", o=1)
                        nc.vector.tensor_tensor(spare[u][:], mean_wide, lonely.broadcast_to(wide), ALU.mult).then_inc(
                            spared[u], 1)
                        nc.vector.tensor_tensor(out[u][:], acc[:, bass.ds(tile(u), GROUP), 0:D],
                                                part.broadcast_to(wide), ALU.mult).then_inc(scaled[u], 1)
                    for u in range(2):
                        dve.wait_ge(spared[u], it + 1)
                        dve.wait_ge(scaled[u], it + 1)
                        nc.vector.tensor_tensor(out[u][:], out[u][:], spare[u][:], ALU.add).then_inc(filled[u], 1)
                    for u in range(2):
                        dve.wait_ge(filled[u], it + 1)
                        nc.vector.tensor_scalar(low[u][:], out[u][:], 0.0, None, ALU.min).then_inc(lowered[u], 1)
                    for u in range(2):
                        dve.wait_ge(exped[u], it + 1)
                        nc.vector.scalar_tensor_tensor(out=out[u][:], in0=out[u][:], scalar=0.0, in1=low[u][:],
                                                       op0=ALU.max, op1=ALU.add).then_inc(summed[u], 1)
                    for u in range(2):
                        dve.wait_ge(summed[u], it + 1)
                        at = m.x[:, bass.ds(tile(u), GROUP), :]
                        nc.vector.scalar_tensor_tensor(out=at, in0=out[u][:], scalar=-1.0, in1=at, op0=ALU.add,
                                                       op1=ALU.add).then_inc(added[u], 1)
                    for u in range(2):
                        dve.wait_ge(added[u], it + 1)
                        row_stats(nc, dve, m, tile(u), GROUP)

            @block.scalar
            def _(act):
                with act.Fori(0, GROUPS // 2) as it:
                    for u in range(2):
                        act.wait_ge(lowered[u], it + 1)
                        nc.scalar.activation(low[u][:], low[u][:], ACT.Exp).then_inc(exped[u], 1)




def stage_signed_sums(nc, m, a):
    with Stage(nc) as ctx:
        w = Walk(nc, m, a, "g3", ctx)
        width = UV_END
        index = w.sb("index", [P, PAIR, 2], U32)
        adj = w.halves("adj", [SETS, PAIR, P])
        above = w.sb("above", [P, PAIR, P])
        feat = w.sb("feat", [P, PAIR, width])
        ps = w.ps("ps", [P, 512])
        loaded = ctx.sem("g3_loaded")
        cutout = w.sb("cutout", [P, PAIR, P])
        index_ready, gathered, packed, compared, summed, added = (
            w.sem(x) for x in ("index_ready", "gathered", "packed", "compared", "summed", "added"))
        with nc.Block() as block:
            @block.gpsimd
            def _(pool):
                n = runs(nc, pool, m)
                with pool.Fori(0, n) as it:
                    for s in range(SETS):
                        pool.wait_ge(index_ready[s], it + 1)
                        pool.wait_ge(packed[s], 16 * it)
                        pool.wait_ge(summed[s], it)
                        pool.nop(nofuse=True)
                        for h in range(PAIR):
                            nc.gpsimd.indirect_dma_start(
                                out=feat[s][:, h, :], out_offset=None, in_=a["table2"],
                                in_offset=bass.IndirectOffsetOnAxis(ap=index[s][:, h, 1:2], axis=0)).then_inc(gathered[s], 16)

            @block.sync
            def _(sp):
                n = runs(nc, sp, m)
                sp.dma_start(half_of(adj, 0), step_of(a["off_pack"], 0)).then_inc(loaded, 16)
                sp.wait_ge(loaded, 16)
                sp.dma_start(half_of(adj, 1), step_of(a["off_pack"], 1)).then_inc(loaded, 16)
                with sp.Fori(2, n) as it:
                    sp.wait_ge(loaded, it * 16)
                    sp.nop(nofuse=True)
                    sp.wait_ge(compared[SETS - 1], 2 * (it - 1))
                    sp.nop(nofuse=True)
                    sp.dma_start(half_of(adj, it), step_of(a["off_pack"], it)).then_inc(loaded, 16)

            @block.scalar
            def _(act):
                n = runs(nc, act, m)
                for s in range(SETS):
                    nc.scalar.copy(index[s][:], m.index[:, s * PAIR:(s + 1) * PAIR, :]).then_inc(index_ready[s], 1)
                with act.Fori(0, n) as it:
                    for s in range(SETS):
                        act.wait_ge(loaded, it * 16 + 16)
                        act.wait_ge(summed[s], it)
                        nc.scalar.copy(cutout[s][:], pair_in(adj, it, s)).then_inc(compared[s], 1)
                        act.wait_ge(gathered[s], (it + 1) * (16 * PAIR))
                        nc.scalar.dma_start(pair_of(a["h_pack"], it, s), feat[s][:].rearrange("p h w -> p (h w)")
                                            ).then_inc(packed[s], 16)
                        nc.scalar.copy(index[s][:], m.index[:, bass.ds((it * SETS + SETS + s) * PAIR, PAIR), :]
                                       ).then_inc(index_ready[s], 1)
                for s in range(SETS):
                    act.wait_ge(packed[s], 16 * n)
                act.nop(nofuse=True)

            @block.tensor
            def _(pe):
                n = runs(nc, pe, m)
                with pe.Fori(0, n) as it:
                    for s in range(SETS):
                        pe.wait_ge(gathered[s], (it + 1) * (16 * PAIR))
                        pe.wait_ge(compared[s], 2 * it + 2)
                        pe.wait_ge(added[s], it)
                        for left, at, cols in ((cutout, slice(0, D), slice(0, D)),
                                               (above, slice(D, D + SIGN_W), slice(D, width))):
                            for h in range(PAIR):
                                last = nc.tensor.matmul(ps[s][:, at], left[s][:, h, :], feat[s][:, h, cols],
                                                        start=h == 0, stop=h == PAIR - 1)
                        last.then_inc(summed[s], 1)

            @block.vector
            def _(dve):
                last = last_run(nc, dve, m)

                def compare(it, s):
                    dve.wait_ge(loaded, it * 16 + 16)
                    dve.wait_ge(summed[s], it)
                    nc.vector.tensor_scalar(above[s][:], pair_in(adj, it, s), 0.0, None, ALU.is_gt).then_inc(
                        compared[s], 1)

                def add(it, s, tile):
                    dve.wait_ge(summed[s], it + 1)
                    dve.wait_ge(added[s - 1], it + (s > 0))
                    at = m.acc[:, bass.ds(tile * SUPPORT_W, D + SIGN_W)]
                    nc.vector.tensor_tensor(at, at, ps[s][:, 0:D + SIGN_W], ALU.add).then_inc(added[s], 1)

                for s in range(SETS):
                    compare(0, s)
                with dve.Fori(0, last) as it:
                    tiles = tiles_of_step(nc, dve, m, it)
                    for s in range(SETS):
                        add(it, s, tiles[s])
                        compare(it + 1, s)
                tiles = tiles_of_step(nc, dve, m, last)
                for s in range(SETS):
                    add(last, s, tiles[s])


def stage_below_sums(nc, m, a):
    with Stage(nc) as ctx:
        w = Walk(nc, m, a, "g7", ctx)
        adj = w.sb("adj", [P, PAIR, P])
        below = w.sb("below", [P, PAIR, P])
        feat = w.sb("feat", [P, PAIR, UV_END])
        ps = w.ps("ps", [P, 512])
        loaded, compared, summed, added = (w.sem(x) for x in ("loaded", "compared", "summed", "added"))
        with nc.Block() as block:
            @block.sync
            def _(sp):
                with where(sp, m, NEGATIVES):
                    n = runs(nc, sp, m)
                    with sp.Fori(0, n) as it:
                        for s in range(SETS):
                            sp.wait_ge(summed[s], it)
                            sp.nop(nofuse=True)
                            sp.dma_start(adj[s][:].rearrange("p h i -> p (h i)"), pair_of(a["off_pack"], it, s)
                                         ).then_inc(loaded[s], 16)
                            sp.dma_start(feat[s][:].rearrange("p h w -> p (h w)"), pair_of(a["h_pack"], it, s)
                                         ).then_inc(loaded[s], 16)

            @block.tensor
            def _(pe):
                with where(pe, m, NEGATIVES):
                    n = runs(nc, pe, m)
                    with pe.Fori(0, n) as it:
                        for s in range(SETS):
                            pe.wait_ge(loaded[s], it * 32 + 32)
                            pe.wait_ge(compared[s], it + 1)
                            pe.wait_ge(added[s], it)
                            for h in range(PAIR):
                                last = nc.tensor.matmul(ps[s][:, 0:SIGN_W], below[s][:, h, :], feat[s][:, h, D:UV_END],
                                                        start=h == 0, stop=h == PAIR - 1)
                            last.then_inc(summed[s], 1)

            @block.vector
            def _(dve):
                with where(dve, m, NEGATIVES):
                    n = runs(nc, dve, m)
                    with dve.Fori(0, n) as it:
                        tiles = tiles_of_step(nc, dve, m, it)
                        for s in range(SETS):
                            dve.wait_ge(loaded[s], it * 32 + 32)
                            nc.vector.tensor_scalar(below[s][:], adj[s][:], 0.0, None, ALU.is_lt).then_inc(
                                compared[s], 1)
                        for s in range(SETS):
                            dve.wait_ge(summed[s], it + 1)
                            dve.wait_ge(added[s - 1], it + (s > 0))
                            at = m.acc[:, bass.ds(tiles[s] * SUPPORT_W + D + SIGN_W, SIGN_W)]
                            nc.vector.tensor_tensor(at, at, ps[s][:, 0:SIGN_W], ALU.add).then_inc(added[s], 1)


def stage_signed_scores(nc, m, a):
    with Stage(nc) as ctx:
        scores = [ctx.enter_context(nc.sbuf_tensor(f"sc_scores{g}", [P, T, 4], F32)) for g in range(2)]
        tenth = [ctx.enter_context(nc.sbuf_tensor(f"sc_tenth{g}", [P, T, 4], F32)) for g in range(2)]
        most = ctx.enter_context(nc.sbuf_tensor("sc_most", [P, 2], F32))
        ps = ctx.enter_context(nc.psum_tensor("sc_ps", [P, P], F32))
        step, stored, counted, turned, flagged = (
            ctx.sem("sc_" + x) for x in ("step", "stored", "counted", "turned", "flagged"))
        acc = m.acc[:, 0:T * SUPPORT_W].rearrange("p (t w) -> p t w", w=SUPPORT_W)
        above = acc[:, :, D:D + 2 * HEADS].rearrange("p t (k o) -> p t k o", o=2)
        below = acc[:, :, D + SIGN_W:D + SIGN_W + 2 * HEADS].rearrange("p t (k o) -> p t k o", o=2)
        with nc.Block() as block:
            @block.vector
            def _(dve):
                for g, (first, second) in enumerate(((above, below), (below, above))):
                    nc.vector.memset(scores[g][:], 0.0).then_inc(step, 1)
                    dve.wait_ge(step, 4 * g + 1)
                    nc.vector.tensor_tensor(scores[g][:, :, 0:HEADS], first[:, :, :, 0], second[:, :, :, 1], ALU.add
                                            ).then_inc(step, 1)
                    dve.wait_ge(step, 4 * g + 2)
                    nc.vector.tensor_scalar(tenth[g][:], scores[g][:], ALPHA, None, ALU.mult).then_inc(step, 1)
                    dve.wait_ge(step, 4 * g + 3)
                    nc.vector.tensor_tensor(scores[g][:], scores[g][:], tenth[g][:], ALU.max).then_inc(step, 1)
                nc.vector.tensor_reduce(most[:, 0:1], acc[:, :, UV_END - 1], AX.X, ALU.max).then_inc(counted, 1)
                dve.wait_ge(turned, 1)
                nc.vector.tensor_reduce(most[0:1, 1:2], ps[0:1, :], AX.X, ALU.max).then_inc(flagged, 1)
                dve.wait_ge(flagged, 1)
                nc.vector.tensor_scalar(m.meta[:, CROWDED:CROWDED + 1], most[0:1, 1:2], TOPK - 0.5, None, ALU.is_gt)

            @block.tensor
            def _(pe):
                pe.wait_ge(counted, 1)
                nc.tensor.matmul(ps[0:1, :], most[:, 0:1], m.ident[:], start=True, stop=True).then_inc(turned, 1)

            @block.sync
            def _(sp):
                for g in range(2):
                    sp.wait_ge(step, 4 * g + 4)
                    sp.dma_start(a["score_table"][g * N:(g + 1) * N, :].rearrange("(t p) k -> p t k", p=P),
                                 scores[g][:]).then_inc(stored, 16)
                sp.wait_ge(stored, 32)


def stage_signed_max(nc, m, a, sign):
    flag = None if sign > 0 else NEGATIVES
    with Stage(nc) as ctx:
        w = Walk(nc, m, a, f"g4{sign > 0:d}", ctx)
        index = w.sb("index", [P, PAIR], U32)
        adj = w.halves("adj", [SETS, PAIR, P])
        score = w.sb("score", [P, PAIR, 4])
        bias = w.sb("bias", [P, PAIR, P])
        masked = w.sb("masked", [P, HEADS, PAIR, P], sets=2)
        best = w.sb("best", [P, HEADS], sets=2)
        ps = w.ps("ps", [P, 1024], sets=2)
        loaded = ctx.sem(w.name + "_loaded")
        pack = a["score_pack1" if sign > 0 else "score_pack0"]
        index_ready, gathered, packed, biased, masked_ready, turned, reduced, kept = (
            w.sem(x) for x in ("index_ready", "gathered", "packed", "biased", "masked_ready", "turned", "reduced",
                               "kept"))

        def two_before(eng, semaphore, s, it):
            eng.wait_ge(semaphore[(s + 2) % SETS], it + (s >= 2))

        with nc.Block() as block:
            @block.gpsimd
            def _(pool):
                with where(pool, m, flag):
                    n = runs(nc, pool, m)
                    with pool.Fori(0, n) as it:
                        for s in range(SETS):
                            pool.wait_ge(index_ready[s], it + 1)
                            pool.wait_ge(packed[s], 16 * it)
                            pool.wait_ge(masked_ready[s], it)
                            pool.nop(nofuse=True)
                            for h in range(PAIR):
                                nc.gpsimd.indirect_dma_start(
                                    out=score[s][:, h, :], out_offset=None, in_=a["score_table"],
                                    in_offset=bass.IndirectOffsetOnAxis(ap=index[s][:, h:h + 1], axis=0)).then_inc(gathered[s], 16)

            @block.sync
            def _(sp):
                with where(sp, m, flag):
                    n = runs(nc, sp, m)
                    sp.dma_start(half_of(adj, 0), step_of(a["off_pack"], 0)).then_inc(loaded, 16)
                    sp.wait_ge(loaded, 16)
                    sp.dma_start(half_of(adj, 1), step_of(a["off_pack"], 1)).then_inc(loaded, 16)
                    with sp.Fori(2, n) as it:
                        sp.wait_ge(loaded, it * 16)
                        sp.nop(nofuse=True)
                        sp.wait_ge(biased[SETS - 1], it - 1)
                        sp.nop(nofuse=True)
                        sp.dma_start(half_of(adj, it), step_of(a["off_pack"], it)).then_inc(loaded, 16)

            @block.scalar
            def _(act):
                def index_of(s, at):
                    nc.scalar.activation(index[s][:], m.index[:, at, 1], ACT.Copy,
                                         bias=0.0 if sign > 0 else float(N)).then_inc(index_ready[s], 1)

                with where(act, m, flag):
                    n = runs(nc, act, m)
                    for s in range(SETS):
                        index_of(s, slice(s * PAIR, (s + 1) * PAIR))
                    with act.Fori(0, n) as it:
                        for s in range(SETS):
                            u = s % 2
                            act.wait_ge(gathered[s], (it + 1) * (16 * PAIR))
                            nc.scalar.dma_start(pair_of(pack, it, s), score[s][:].rearrange("p h w -> p (h w)")
                                                ).then_inc(packed[s], 16)
                            index_of(s, bass.ds((it * SETS + SETS + s) * PAIR, PAIR))
                            act.wait_ge(biased[s], it + 1)
                            two_before(act, turned, s, it)
                            for k in range(HEADS):
                                for h in range(PAIR):
                                    last = nc.scalar.activation(masked[u][:, k, h, :], bias[s][:, h, :], ACT.Identity,
                                                                bias=score[s][:, h, k:k + 1])
                            last.then_inc(masked_ready[s], 1)
                    for s in range(SETS):
                        act.wait_ge(packed[s], 16 * n)
                    act.nop(nofuse=True)

            @block.tensor
            def _(pe):
                with where(pe, m, flag):
                    n = runs(nc, pe, m)
                    with pe.Fori(0, n) as it:
                        for s in range(SETS):
                            u = s % 2
                            pe.wait_ge(masked_ready[s], it + 1)
                            two_before(pe, reduced, s, it)
                            for k in range(HEADS):
                                for h in range(PAIR):
                                    c = (k * PAIR + h) * P
                                    last = nc.tensor.transpose(ps[u][:, c:c + P], masked[u][:, k, h, :], m.ident[:])
                            last.then_inc(turned[s], 1)

            @block.vector
            def _(dve):
                with where(dve, m, flag):
                    last = last_run(nc, dve, m)

                    def mask(it, s):
                        dve.wait_ge(loaded, it * 16 + 16)
                        dve.wait_ge(masked_ready[s], it)
                        nc.vector.tensor_scalar(bias[s][:], pair_in(adj, it, s), 0.0, -BIG,
                                                ALU.is_le if sign > 0 else ALU.is_ge, ALU.mult).then_inc(biased[s], 1)

                    def reduce(it, s):
                        dve.wait_ge(turned[s], it + 1)
                        two_before(dve, kept, s, it)
                        nc.vector.tensor_reduce(best[s % 2][:], ps[s % 2][:, 0:HEADS * PAIR * P].rearrange(
                            "p (k s) -> p k s", k=HEADS), AX.X, ALU.max).then_inc(reduced[s], 1)

                    def keep(it, s, tile):
                        dve.wait_ge(reduced[s], it + 1)
                        dve.wait_ge(kept[s - 1], it + (s > 0))
                        at = m.best2[:, bass.ds(tile, 1), :].rearrange("p o k -> p (o k)")
                        nc.vector.tensor_tensor(at, at, best[s % 2][:], ALU.max).then_inc(kept[s], 1)

                    for s in range(SETS):
                        mask(0, s)
                    with dve.Fori(0, last) as it:
                        tiles = tiles_of_step(nc, dve, m, it)
                        for s in range(SETS):
                            reduce(it, s)
                            mask(it + 1, s)
                            keep(it, s, tiles[s])
                    tiles = tiles_of_step(nc, dve, m, last)
                    for s in range(SETS):
                        reduce(last, s)
                        keep(last, s, tiles[s])


def stage_signed_pairs(nc, m, a, sign):
    flag = None if sign > 0 else NEGATIVES
    with Stage(nc) as ctx:
        w = Walk(nc, m, a, f"g5{sign > 0:d}", ctx)
        adj = w.halves("adj", [SETS, PAIR, P])
        feat = w.halves("feat", [SETS, PAIR, UV_END])
        score = w.halves("score", [SETS, PAIR, 4])
        bias = w.sb("bias", [P, PAIR, P], sets=2)
        expo = w.sb("expo", [P, HEADS, PAIR, P])
        prob = w.sb("prob", [P, HEADS, PAIR, P], sets=2)
        total = w.sb("total", [P, HEADS, P], sets=2)
        ps = w.ps("ps", [P, 512])
        touch = ctx.enter_context(nc.sbuf_tensor(w.name + "_touch", [1, 1], F32))
        score_loaded, touched = (ctx.sem(w.name + x) for x in ("_score_loaded", "_touched"))
        adj_loaded, feat_loaded = w.sem("adj_loaded"), w.sem("feat_loaded")
        biased, shifted, exped, totalled, weighted, summed, added = (
            w.sem(x) for x in ("biased", "shifted", "exped", "totalled", "weighted", "summed", "added"))
        pack = a["score_pack1" if sign > 0 else "score_pack0"]

        with nc.Block() as block:
            @block.sync
            def _(sp):
                with where(sp, m, flag):
                    n = runs(nc, sp, m)

                    def load(it, s, buffer, source, loaded):
                        sp.dma_start(pair_in(buffer, it, s).rearrange("p h w -> p (h w)"), pair_of(source, it, s)
                                     ).then_inc(loaded[s], 16)

                    sp.dma_start(half_of(score, 0), step_of(pack, 0)).then_inc(score_loaded, 16)
                    for s in range(SETS):
                        load(0, s, adj, a["off_pack"], adj_loaded)
                        load(0, s, feat, a["h_pack"], feat_loaded)
                    sp.wait_ge(score_loaded, 16)
                    sp.dma_start(half_of(score, 1), step_of(pack, 1)).then_inc(score_loaded, 16)
                    for s in range(SETS):
                        sp.wait_ge(adj_loaded[s], 16)
                        load(1, s, adj, a["off_pack"], adj_loaded)
                        sp.wait_ge(feat_loaded[s], 16)
                        load(1, s, feat, a["h_pack"], feat_loaded)
                    with sp.Fori(2, n) as it:
                        for s in range(SETS):
                            sp.wait_ge(adj_loaded[s], it * 16)
                            sp.nop(nofuse=True)
                            sp.wait_ge(weighted[s], it - 1)
                            sp.nop(nofuse=True)
                            load(it, s, adj, a["off_pack"], adj_loaded)
                            sp.wait_ge(feat_loaded[s], it * 16)
                            sp.nop(nofuse=True)
                            sp.wait_ge(summed[s], it - 1)
                            sp.nop(nofuse=True)
                            load(it, s, feat, a["h_pack"], feat_loaded)
                        sp.wait_ge(score_loaded, it * 16)
                        sp.nop(nofuse=True)
                        sp.dma_start(half_of(score, it), step_of(pack, it)).then_inc(score_loaded, 16)

            @block.vector
            def _(dve):
                with where(dve, m, flag):
                    n = runs(nc, dve, m)
                    last = last_run(nc, dve, m)

                    def mask(it, s):
                        dve.wait_ge(adj_loaded[s], it * 16 + 16)
                        if s >= 2:
                            dve.wait_ge(shifted[s - 2], it + 1)
                        else:
                            dve.wait_ge(shifted[s + 2], it)
                        nc.vector.tensor_scalar(bias[s % 2][:], pair_in(adj, it, s), 0.0, -BIG,
                                                ALU.is_le if sign > 0 else ALU.is_ge, ALU.mult).then_inc(biased[s], 1)

                    def shift(it, s, tile):
                        dve.wait_ge(biased[s], it + 1)
                        dve.wait_ge(summed[s], it)
                        by_row = m.shift2[:, bass.ds(tile * (HEADS * P), HEADS * P)].rearrange(
                            "p (k o i) -> p k o i", k=HEADS, o=1)
                        nc.vector.tensor_tensor(
                            expo[s][:], bias[s % 2][:].rearrange("p (o h) i -> p o h i", o=1).broadcast_to(
                                [P, HEADS, PAIR, P]),
                            by_row.broadcast_to([P, HEADS, PAIR, P]), ALU.subtract).then_inc(shifted[s], 1)

                    def total_of(it, s):
                        dve.wait_ge(exped[s], it + 1)
                        dve.wait_ge(summed[(s + 2) % SETS], it + (s >= 2))
                        nc.vector.tensor_tensor(total[s % 2][:], expo[s][:, :, 0, :], expo[s][:, :, 1, :],
                                                ALU.add).then_inc(totalled[s], 1)

                    def add(it, s, tile):
                        dve.wait_ge(summed[s], it + 1)
                        dve.wait_ge(added[s - 1], it + (s > 0))
                        at = m.acc[:, bass.ds(tile * HEAD_W, HEAD_W)]
                        nc.vector.tensor_tensor(at, at, ps[s][:, 0:HEAD_W], ALU.add).then_inc(added[s], 1)

                    kept_word = dve.alloc_register()
                    word = word_of_step(nc, dve, m, 0)
                    dve.reg_mov(kept_word, word)
                    tiles = tiles_in(nc, dve, word)
                    for s in range(SETS):
                        mask(0, s)
                        if s >= 2:
                            total_of(0, s - 2)
                        shift(0, s, tiles[s])
                    with dve.Fori(1, n) as it:
                        before = tiles_in(nc, dve, dve.snap(kept_word))
                        word = word_of_step(nc, dve, m, it)
                        dve.reg_mov(kept_word, word)
                        tiles = tiles_in(nc, dve, word)
                        for s in range(SETS):
                            mask(it, s)
                            total_of(it - (s < 2), (s + 2) % SETS)
                            add(it - 1, s, before[s])
                            shift(it, s, tiles[s])
                    tiles = tiles_of_step(nc, dve, m, last)
                    total_of(last, SETS - 2)
                    total_of(last, SETS - 1)
                    for s in range(SETS):
                        add(last, s, tiles[s])

            @block.scalar
            def _(act):
                with where(act, m, flag):
                    n = runs(nc, act, m)
                    with act.Fori(0, n) as it:
                        act.wait_ge(touched, it)
                        nc.scalar.activation(touch[:], m.ones[0:1, 0:1], ACT.Exp).then_inc(touched, 1)
                        for s in range(SETS):
                            act.wait_ge(shifted[s], it + 1)
                            act.wait_ge(score_loaded, it * 16 + 16)
                            for k in range(HEADS):
                                for h in range(PAIR):
                                    last = nc.scalar.activation(expo[s][:, k, h, :], expo[s][:, k, h, :], ACT.Exp,
                                                                bias=pair_in(score, it, s)[:, h, k:k + 1])
                            last.then_inc(exped[s], 1)

            @block.gpsimd
            def _(pool):
                with where(pool, m, flag):
                    n = runs(nc, pool, m)
                    with pool.Fori(0, n) as it:
                        for s in range(SETS):
                            u = s % 2
                            pool.wait_ge(summed[(s + 2) % SETS], it + (s >= 2))
                            pool.wait_ge(exped[s], it + 1)
                            nc.gpsimd.tensor_tensor(
                                prob[u][:], expo[s][:], pair_in(adj, it, s).rearrange(
                                    "p (o h) i -> p o h i", o=1).broadcast_to([P, HEADS, PAIR, P]),
                                ALU.mult).then_inc(weighted[s], 1)

            @block.tensor
            def _(pe):
                with where(pe, m, flag):
                    n = runs(nc, pe, m)
                    with pe.Fori(0, n) as it:
                        for s in range(SETS):
                            u = s % 2
                            pe.wait_ge(feat_loaded[s], it * 16 + 16)
                            pe.wait_ge(weighted[s], it + 1)
                            pe.wait_ge(added[s], it)
                            for k in range(HEADS):
                                c = k * (D + 1)
                                for h in range(PAIR):
                                    nc.tensor.matmul(ps[s][:, c:c + D], prob[u][:, k, h, :],
                                                     pair_in(feat, it, s)[:, h, 0:D],
                                                     start=h == 0, stop=h == PAIR - 1)
                            pe.wait_ge(totalled[s], it + 1)
                            for k in range(HEADS):
                                c = k * (D + 1)
                                last = nc.tensor.matmul(ps[s][:, c + D:c + D + 1], total[u][:, k, :], m.ones[:, 0:1],
                                                        start=True, stop=True)
                            last.then_inc(summed[s], 1)


def stage_gru(nc, m, a, which):
    heads = HEADS if which else 1
    tiles = 2
    span = tiles * P
    last_step = T // (2 * tiles) - 1
    with Stage(nc) as ctx:
        def sb(name, shape):
            return [ctx.enter_context(nc.sbuf_tensor(f"r{which}_{name}{u}", shape, F32)) for u in range(2)]

        def sem(name):
            return [ctx.sem(f"r{which}_{name}{u}") for u in range(2)]

        def ps(name):
            both = [ctx.enter_context(nc.psum_tensor(f"r{which}_{name}{u}", [P, 2 * span], F32)) for u in range(2)]
            return [[x[:, 0:span] for x in both], [x[:, span:2 * span] for x in both]]

        rden = sb("rden", [P, tiles, HEADS])
        part = sb("part", [P, heads, tiles, D])
        partT = sb("partT", [P, heads, span])
        sT = sb("sT", [P, span])
        r = sb("r", [P, span])
        z = sb("z", [P, span])
        hn = sb("hn", [P, span])
        cand = sb("cand", [P, span])
        new = sb("new", [P, span])
        scaled = sb("scaled", [P, tiles, D])
        ps_t = ps("ps_turned")
        third, ps_e = ps("ps_mixed")
        ps_t.append(third)
        ps_g = ps("ps_gates") + ps("ps_candidate")
        ps_b = ps_g[2]
        (parted, turned, copied, mixed, mixed_copied, gated, acts, gates_read, dv, tanhed, newed, back, added,
         divided) = (
            sem(x) for x in ("parted", "turned", "copied", "mixed", "mixed_copied", "gated", "acts", "gates_read",
                             "dve", "tanhed", "newed", "back", "added", "divided"))

        def group(tensor, it, u):
            return tensor[:, bass.ds(it * (2 * tiles) + u * tiles, tiles), :]

        with nc.Block() as block:
            @block.vector
            def _(dve):
                def supports(it, u):
                    dve.wait_ge(turned[u], it)
                    if which:
                        acc = m.acc[:, 0:T * HEAD_W].rearrange("p (t k w) -> p t k w", k=HEADS, w=D + 1)
                        rows = acc[:, bass.ds(it * (2 * tiles) + u * tiles, tiles), :, :]
                        dve.wait_ge(parted[u], it)
                        nc.vector.tensor_scalar(rden[u][:], rows[:, :, :, D], 1.0 / BIG, None, ALU.max).then_inc(
                            divided[u], 1)
                        dve.wait_ge(divided[u], it * 2 + 1)
                        nc.vector.reciprocal(rden[u][:], rden[u][:]).then_inc(divided[u], 1)
                        dve.wait_ge(divided[u], it * 2 + 2)
                        for k in range(HEADS):
                            last = nc.vector.tensor_tensor(part[u][:, k, :, :], rows[:, :, k, 0:D],
                                                           rden[u][:, :, k:k + 1].broadcast_to([P, tiles, D]), ALU.mult)
                        last.then_inc(parted[u], 1)
                    else:
                        acc = m.acc[:, 0:T * SUPPORT_W].rearrange("p (t w) -> p t w", w=SUPPORT_W)
                        nc.vector.tensor_copy(part[u][:, 0, :, :], group(acc, it, u)[:, :, 0:D]).then_inc(parted[u], 1)

                def step(it, more):
                    for u in range(2):
                        dve.wait_ge(acts[u], it + 1)
                        nc.vector.scalar_tensor_tensor(out=r[u][:], in0=r[u][:], scalar=1.0, in1=hn[u][:],
                                                       op0=ALU.add, op1=ALU.mult).then_inc(dv[u], 1)
                    for u in range(2):
                        dve.wait_ge(dv[u], it * 3 + 1)
                        dve.wait_ge(newed[u], it)
                        nc.vector.tensor_tensor(cand[u][:], ps_g[2][u], r[u][:], ALU.add).then_inc(gates_read[u], 1)
                    if more:
                        supports(it + 1, 0)
                        supports(it + 1, 1)
                    for u in range(2):
                        dve.wait_ge(tanhed[u], it + 1)
                        dve.wait_ge(back[u], it)
                        h = m.hT[:, bass.ds(it * (2 * span) + u * span, span)]
                        nc.vector.tensor_tensor(new[u][:], h, cand[u][:], ALU.subtract).then_inc(dv[u], 1)
                    for u in range(2):
                        dve.wait_ge(dv[u], it * 3 + 2)
                        nc.vector.scalar_tensor_tensor(out=new[u][:], in0=z[u][:], scalar=1.0, in1=new[u][:],
                                                       op0=ALU.add, op1=ALU.mult).then_inc(dv[u], 1)
                    for u in range(2):
                        dve.wait_ge(dv[u], it * 3 + 3)
                        nc.vector.scalar_tensor_tensor(out=new[u][:], in0=new[u][:], scalar=0.5, in1=cand[u][:],
                                                       op0=ALU.mult, op1=ALU.add).then_inc(newed[u], 1)
                    for u in range(2):
                        dve.wait_ge(back[u], it + 1)
                        dve.wait_ge(added[u], it * 2)
                        dia = m.diagonal[:, bass.ds(it * (2 * tiles) + u * tiles, tiles)].rearrange(
                            "p (g o) -> p g o", o=1)
                        nc.vector.tensor_tensor(scaled[u][:], ps_b[u].rearrange("p (g d) -> p g d", d=D),
                                                dia.broadcast_to([P, tiles, D]), ALU.mult).then_inc(added[u], 1)
                    for u in range(2):
                        dve.wait_ge(added[u], it * 2 + 1)
                        at = group(m.x, it, u)
                        nc.vector.tensor_tensor(at, at, scaled[u][:], ALU.add).then_inc(added[u], 1)
                    if which:
                        for u in range(2):
                            dve.wait_ge(added[u], it * 2 + 2)
                            row_stats(nc, dve, m, it * (2 * tiles) + u * tiles, tiles)

                supports(0, 0)
                supports(0, 1)
                with dve.Fori(0, last_step) as it:
                    step(it, more=True)
                step(last_step, more=False)

            @block.tensor
            def _(pe):
                def turn(it, u):
                    pe.wait_ge(parted[u], it + 1)
                    pe.wait_ge(copied[u], it)
                    for k in range(heads):
                        for g in range(tiles):
                            last = nc.tensor.transpose(ps_t[k][u][:, g * P:(g + 1) * P], part[u][:, k, g, :], m.ident[:])
                    last.then_inc(turned[u], 1)

                def state(it, u):
                    return m.hT[:, bass.ds(it * (2 * span) + u * span, span)]

                def support(u):
                    return sT[u][:] if which else partT[u][:, 0, :]

                def step(it, more):
                    for u in range(2):
                        pe.wait_ge(copied[u], it + 1)
                        if which:
                            for k in range(HEADS):
                                last = nc.tensor.matmul(ps_e[u], m.w2[:, k, :], partT[u][:, k, :], start=k == 0,
                                                        stop=k == HEADS - 1)
                            last.then_inc(mixed[u], 1)
                    for u in range(2):
                        if which:
                            pe.wait_ge(mixed_copied[u], it + 1)
                        pe.wait_ge(acts[u], it)
                        for k in range(2):
                            c = slice(k * D, (k + 1) * D)
                            nc.tensor.matmul(ps_g[k][u], m.whh[:, which, c], state(it, u), start=True, stop=False)
                            nc.tensor.matmul(ps_g[k][u], m.wih[:, which, c], support(u), start=False, stop=True)
                        pe.wait_ge(gates_read[u], it)
                        pe.wait_ge(added[u], it * 2)
                        nc.tensor.matmul(ps_g[3][u], m.whh[:, which, 2 * D:3 * D], state(it, u), start=True, stop=True)
                        nc.tensor.matmul(ps_g[2][u], m.wih[:, which, 2 * D:3 * D], support(u), start=True,
                                         stop=True).then_inc(gated[u], 1)
                    if more:
                        turn(it + 1, 0)
                        turn(it + 1, 1)
                    for u in range(2):
                        pe.wait_ge(newed[u], it + 1)
                        for g in range(tiles):
                            last = nc.tensor.transpose(ps_b[u][:, g * P:(g + 1) * P], new[u][:, g * P:(g + 1) * P],
                                                       m.ident[:])
                        last.then_inc(back[u], 1)

                turn(0, 0)
                turn(0, 1)
                with pe.Fori(0, last_step) as it:
                    step(it, more=True)
                step(last_step, more=False)

            @block.scalar
            def _(act):
                def copy(it, u):
                    act.wait_ge(turned[u], it + 1)
                    act.wait_ge(gated[u], it)
                    for k in range(heads):
                        last = nc.scalar.copy(partT[u][:, k, :], ps_t[k][u])
                    last.then_inc(copied[u], 1)

                def step(it, more):
                    if which:
                        for u in range(2):
                            act.wait_ge(mixed[u], it + 1)
                            nc.scalar.mul(sT[u][:], ps_e[u], 1.0 / HEADS).then_inc(mixed_copied[u], 1)
                    for u in range(2):
                        act.wait_ge(gated[u], it + 1)
                        act.wait_ge(newed[u], it)
                        nc.scalar.activation(r[u][:], ps_g[0][u], ACT.Tanh, bias=m.bsum[:, which, 0:1], scale=0.5)
                        nc.scalar.activation(z[u][:], ps_g[1][u], ACT.Tanh, bias=m.bsum[:, which, 1:2], scale=0.5)
                        nc.scalar.activation(hn[u][:], ps_g[3][u], ACT.Identity, bias=m.bhh[:, which, 2:3],
                                             scale=0.5).then_inc(acts[u], 1)
                    for u in range(2):
                        act.wait_ge(gates_read[u], it + 1)
                        nc.scalar.activation(cand[u][:], cand[u][:], ACT.Tanh, bias=m.bih[:, which, 2:3]).then_inc(
                            tanhed[u], 1)
                    if more:
                        copy(it + 1, 0)
                        copy(it + 1, 1)

                copy(0, 0)
                copy(0, 1)
                with act.Fori(0, last_step) as it:
                    step(it, more=True)
                step(last_step, more=False)


def stage_select(nc, m, a):
    rounds = -(-TOPK // 8)
    with Stage(nc) as ctx:
        adj, filtered, left = (m.shift2[:, i * N:(i + 1) * N] for i in range(3))
        top = ctx.enter_context(nc.sbuf_tensor("tk_top", [P, 8], F32))
        turned = ctx.enter_context(nc.sbuf_tensor("tk_turned", [P, 4, P], F32))
        ps = ctx.enter_context(nc.psum_tensor("tk_ps", [P, 4, P], F32))
        loaded, squared, tanhed, dv, chosen, turns, copies, stores = (
            ctx.sem("tk_" + x) for x in ("loaded", "squared", "tanhed", "dve", "chosen", "turns", "copies", "stores"))
        blocks = T // 4
        dst = a["selected"].rearrange("(q b j) i -> j q b i", b=4, j=P)
        own = 2 * rounds + 3
        with nc.Block() as block:
            @block.sync
            def _(sp):
                with where(sp, m, CROWDED):
                    with sp.Fori(0, T) as t:
                        sp.wait_ge(turns, t * blocks)
                        sp.nop(nofuse=True)
                        sp.dma_start(adj, a["adj"][bass.ds(t * P, P), :]).then_inc(loaded, 16)
                        for q in range(blocks):
                            sp.wait_ge(copies, t * blocks + (q + 1))
                            sp.nop(nofuse=True)
                            sp.dma_start(dst[:, q:q + 1, :, bass.ds(t * P, P)].rearrange("j o b i -> j (o b) i"),
                                         turned[:]).then_inc(stores, 16)
                    sp.wait_ge(stores, 16 * T * blocks)

            @block.scalar
            def _(act):
                with where(act, m, CROWDED):
                    with act.Fori(0, T) as t:
                        act.wait_ge(squared, t + 1)
                        nc.scalar.activation(filtered, filtered, ACT.Tanh).then_inc(tanhed, 1)
                        for q in range(blocks):
                            act.wait_ge(turns, t * blocks + (q + 1))
                            act.wait_ge(stores, t * (blocks * 16) + q * 16)
                            nc.scalar.copy(turned[:], ps[:]).then_inc(copies, 1)

            @block.tensor
            def _(pe):
                with where(pe, m, CROWDED):
                    with pe.Fori(0, T) as t:
                        pe.wait_ge(chosen, t + 1)
                        for q in range(blocks):
                            pe.wait_ge(copies, t * blocks + q)
                            for b in range(4):
                                last = nc.tensor.transpose(ps[:, b, :], adj[:, (q * 4 + b) * P:(q * 4 + b + 1) * P], m.ident[:])
                            last.then_inc(turns, 1)

            @block.vector
            def _(dve):
                with where(dve, m, CROWDED):
                    with dve.Fori(0, T) as t:
                        dve.wait_ge(loaded, t * 16 + 16)
                        dve.wait_ge(chosen, t)
                        nc.vector.scalar_tensor_tensor(out=filtered, in0=adj, scalar=0.0, in1=adj, op0=ALU.max,
                                                       op1=ALU.mult).then_inc(squared, 1)
                        dve.wait_ge(tanhed, t + 1)
                        nc.vector.tensor_copy(left, filtered).then_inc(dv, 1)
                        dve.wait_ge(dv, t * own + 1)
                        dve.nop(nofuse=True)
                        with dve.Fori(0, rounds - 1) as r:
                            nc.vector.max(out=top[:], in_=left).then_inc(dv, 1)
                            dve.wait_ge(dv, t * own + r * 2 + 2)
                            dve.nop(nofuse=True)
                            nc.vector.match_replace(out=left, in_to_replace=top[:], in_values=left,
                                                    imm_value=-1.0).then_inc(dv, 1)
                            dve.wait_ge(dv, t * own + r * 2 + 3)
                            dve.nop(nofuse=True)
                        nc.vector.max(out=top[:], in_=left).then_inc(dv, 1)
                        dve.wait_ge(dv, t * own + 2 * rounds)
                        nc.vector.memset(top[:, 8 - (8 * rounds - TOPK):8], -2.0).then_inc(dv, 1)
                        dve.wait_ge(dv, t * own + (2 * rounds + 1))
                        dve.nop(nofuse=True)
                        nc.vector.match_replace(out=left, in_to_replace=top[:], in_values=left,
                                                imm_value=-1.0).then_inc(dv, 1)
                        dve.wait_ge(dv, t * own + (2 * rounds + 2))
                        nc.vector.tensor_scalar(left, left, 0.0, None, ALU.is_lt).then_inc(dv, 1)
                        dve.wait_ge(dv, t * own + (2 * rounds + 3))
                        nc.vector.tensor_tensor(adj, adj, left, ALU.mult).then_inc(chosen, 1)


def stage_repack(nc, m, a):
    with Stage(nc) as ctx:
        index = ctx.enter_context(nc.sbuf_tensor("rp_index", [P, PAIR], U32))
        adj = ctx.enter_context(nc.sbuf_tensor("rp_adj", [P, PAIR, P], F32))
        index_ready, gathered, packed = (ctx.sem("rp_" + x) for x in ("index_ready", "gathered", "packed"))
        rows = a["selected"].rearrange("j (t i) -> (j t) i", i=P)
        with nc.Block() as block:
            @block.scalar
            def _(act):
                with where(act, m, CROWDED):
                    n = runs(nc, act, m)
                    with act.Fori(0, n * SETS) as g:
                        act.wait_ge(gathered, g * (16 * PAIR))
                        nc.scalar.copy(index[:], m.index[:, bass.ds(g * PAIR, PAIR), 0]).then_inc(index_ready, 1)

            @block.gpsimd
            def _(pool):
                with where(pool, m, CROWDED):
                    n = runs(nc, pool, m)
                    with pool.Fori(0, n * SETS) as g:
                        pool.wait_ge(index_ready, g + 1)
                        pool.wait_ge(packed, g * 16)
                        pool.nop(nofuse=True)
                        for h in range(PAIR):
                            nc.gpsimd.indirect_dma_start(
                                out=adj[:, h, :], out_offset=None, in_=rows,
                                in_offset=bass.IndirectOffsetOnAxis(ap=index[:, h:h + 1], axis=0)).then_inc(gathered, 16)

            @block.sync
            def _(sp):
                with where(sp, m, CROWDED):
                    n = runs(nc, sp, m)
                    with sp.Fori(0, n * SETS) as g:
                        sp.wait_ge(gathered, (g + 1) * (16 * PAIR))
                        sp.dma_start(a["adj_pack"][:, bass.ds(g, 1), :].rearrange("p o w -> p (o w)"),
                                     adj[:].rearrange("p h i -> p (h i)")).then_inc(packed, 16)
                    sp.wait_ge(packed, n * (SETS * 16))
                    sp.nop(nofuse=True)


def stage_filter_pairs(nc, m, a):
    with Stage(nc) as ctx:
        w = Walk(nc, m, a, "g6", ctx)
        index = w.sb("index", [P, PAIR, 2], U32)
        adj = w.sb("adj", [P, PAIR, P])
        square = w.sb("square", [P, PAIR, P])
        feat = w.sb("feat", [P, PAIR, D])
        ps = w.ps("ps", [P, 512])
        index_ready, gathered, adj_loaded, squared, filtered, summed, added = (
            w.sem(x) for x in ("index_ready", "gathered", "adj_loaded", "squared", "filtered", "summed", "added"))
        with nc.Block() as block:
            @block.gpsimd
            def _(pool):
                n = runs(nc, pool, m)
                with pool.Fori(0, n) as it:
                    for s in range(SETS):
                        pool.wait_ge(index_ready[s], it + 1)
                        pool.wait_ge(summed[s], it)
                        pool.nop(nofuse=True)
                        for h in range(PAIR):
                            nc.gpsimd.indirect_dma_start(
                                out=feat[s][:, h, :], out_offset=None, in_=a["table3"],
                                in_offset=bass.IndirectOffsetOnAxis(ap=index[s][:, h, 1:2], axis=0)).then_inc(gathered[s], 16)

            @block.sync
            def _(sp):
                n = runs(nc, sp, m)
                with sp.Fori(0, n) as it:
                    for s in range(SETS):
                        sp.wait_ge(squared[s], it)
                        sp.dma_start(adj[s][:].rearrange("p h i -> p (h i)"), pair_of(a["adj_pack"], it, s)).then_inc(
                            adj_loaded[s], 16)

            @block.scalar
            def _(act):
                n = runs(nc, act, m)
                with act.Fori(0, n) as it:
                    for s in range(SETS):
                        act.wait_ge(gathered[s], it * (16 * PAIR))
                        nc.scalar.copy(index[s][:], m.index[:, bass.ds((it * SETS + s) * PAIR, PAIR), :]).then_inc(
                            index_ready[s], 1)
                    for s in range(SETS):
                        act.wait_ge(squared[s], it + 1)
                        nc.scalar.activation(square[s][:], square[s][:], ACT.Tanh).then_inc(filtered[s], 1)

            @block.tensor
            def _(pe):
                n = runs(nc, pe, m)
                with pe.Fori(0, n) as it:
                    for s in range(SETS):
                        pe.wait_ge(gathered[s], (it + 1) * (16 * PAIR))
                        pe.wait_ge(filtered[s], it + 1)
                        pe.wait_ge(added[s], it)
                        for h in range(PAIR):
                            last = nc.tensor.matmul(ps[s][:, 0:D], square[s][:, h, :], feat[s][:, h, :],
                                                    start=h == 0, stop=h == PAIR - 1)
                        last.then_inc(summed[s], 1)

            @block.vector
            def _(dve):
                n = runs(nc, dve, m)
                with dve.Fori(0, n) as it:
                    for s in range(SETS):
                        dve.wait_ge(adj_loaded[s], it * 16 + 16)
                        dve.wait_ge(summed[s], it)
                        nc.vector.scalar_tensor_tensor(out=square[s][:], in0=adj[s][:], scalar=0.0, in1=adj[s][:],
                                                       op0=ALU.max, op1=ALU.mult).then_inc(squared[s], 1)
                    tiles = tiles_of_step(nc, dve, m, it)
                    for s in range(SETS):
                        dve.wait_ge(summed[s], it + 1)
                        dve.wait_ge(added[s - 1], it + (s > 0))
                        at = m.acc[:, bass.ds(tiles[s] * D, D)]
                        nc.vector.tensor_tensor(at, at, ps[s][:, 0:D], ALU.add).then_inc(added[s], 1)


def stage_output(nc, m, a):
    with Stage(nc) as ctx:
        step, stored = (ctx.sem("out_" + x) for x in ("step", "stored"))
        parts = 4
        size = T // parts
        out = a["out"].rearrange("(t p) d -> p t d", p=P)
        acc = m.acc[:, 0:T * D].rearrange("p (t d) -> p t d", d=D)
        with nc.Block() as block:
            @block.vector
            def _(dve):
                for c in range(parts):
                    at = slice(c * size, (c + 1) * size)
                    bias = m.bg[:].rearrange("p (o d) -> p o d", o=1).broadcast_to([P, size, D])
                    nc.vector.tensor_tensor(acc[:, at, :], acc[:, at, :], bias, ALU.add).then_inc(step, 1)
                    dve.wait_ge(step, 2 * c + 1)
                    nc.vector.scalar_tensor_tensor(
                        out=m.x[:, at, :].rearrange("p t d -> p (t d)"), in0=acc[:, at, :].rearrange("p t d -> p (t d)"),
                        scalar=0.0, in1=m.x[:, at, :].rearrange("p t d -> p (t d)"), op0=ALU.max,
                        op1=ALU.add).then_inc(step, 1)

            @block.sync
            def _(sp):
                for c in range(parts):
                    at = slice(c * size, (c + 1) * size)
                    sp.wait_ge(step, 2 * c + 2)
                    sp.dma_start(out[:, at, :], m.x[:, at, :]).then_inc(stored, 16)
                sp.wait_ge(stored, 16 * parts)


def stage_clear(nc, m):
    with Stage(nc) as ctx:
        done = ctx.sem("clear_done")
        with nc.Block() as block:
            @block.vector
            def _(dve):
                nc.vector.memset(m.best1[:], -BIG).then_inc(done, 1)
                nc.vector.memset(m.best2[:], -BIG).then_inc(done, 1)
                nc.vector.memset(m.s1_wide[:, N:N + P], 0.0).then_inc(done, 1)
                nc.vector.memset(m.shift1[:, N:N + P], BIG).then_inc(done, 1)
                nc.vector.memset(m.shift2[:, T * HEADS * P:], BIG).then_inc(done, 1)


SCRATCH = {
    "selected": (N, N), "table0": (N, 2 * D), "table1": (N, D + 2), "table2": (N, UV_END), "table3": (N, D),
    "score_table": (2 * N, 4), "row_scratch": (T * HEADS * P,),
    "adj_pack": (P, CAP, PAIR * P), "off_pack": (P, CAP, PAIR * P), "wh_pack": (P, CAP, PAIR * (D + 2)),
    "h_pack": (P, CAP, PAIR * UV_END), "score_pack0": (P, CAP, PAIR * 4), "score_pack1": (P, CAP, PAIR * 4),
}


def build(nc, a):
    for name, shape in SCRATCH.items():
        a[name] = nc.dram_tensor("scratch_" + name, shape, F32, kind="Internal").ap()
    with ExitStack() as ctx:
        def sb(name, shape, dt=F32):
            return ctx.enter_context(nc.sbuf_tensor("m_" + name, shape, dt))

        m = Space()
        m.x = sb("x", [P, T, D])
        m.acc = sb("acc", [P, (T + 1) * HEAD_W])
        m.hT = sb("hT", [P, N])
        m.shift2 = sb("shift2", [P, T * HEADS * P + HEADS * P])
        m.s1_wide = m.shift2[:, 0:N + P]
        m.shift1 = m.shift2[:, N + P:2 * (N + P)]
        m.index = sb("index", [P, CAP * PAIR + MAX_PAIRS * PAIR, 2], U32)
        m.meta = sb("meta", [1, 5], I32)
        m.tiles = sb("tiles", [1, CAP // SETS], I32)
        m.best1 = sb("best1", [P, T + 1])
        m.best1c = sb("best1c", [P, T])
        m.best2 = sb("best2", [P, T + 1, HEADS])
        m.hsum = sb("hsum", [P, GROUPS])
        m.stats = sb("stats", [P, T, nc.vector.BN_STATS_DIM])
        m.moments = sb("moments", [P, T, nc.vector.BN_AGGR_DIM])
        m.ident = sb("ident", [P, P])
        m.identb = sb("identb", [P, P], BF16)
        m.ones = sb("ones", [P, P])
        m.row_ramp = sb("row_ramp", [P, P])
        m.class_of = sb("class_of", [P, 1])
        m.class_over = sb("class_over", [P, CLASSES - 1])
        m.sixteens = sb("sixteens", [P, CLASSES - 1])
        m.b0 = sb("b0", [P, 6])
        m.bm = sb("bm", [1, D])
        m.eps = sb("eps", [P, 2])
        m.w1 = sb("w1", [P, D + 1])
        m.w1t = sb("w1t", [P, D])
        m.a1 = sb("a1", [P, 2])
        m.wa1 = sb("wa1", [P, 1])
        m.wa1_wide = sb("wa1_wide", [P, P])
        m.w2 = sb("w2", [P, HEADS, D])
        m.w2t = sb("w2t", [P, HEADS, D])
        m.a2 = sb("a2", [P, HEADS, 2])
        m.uv = sb("uv", [P, 2 * HEADS])
        m.wih = sb("wih", [P, 2, 3 * D])
        m.whh = sb("whh", [P, 2, 3 * D])
        m.bih = sb("bih", [P, 2, 3])
        m.bhh = sb("bhh", [P, 2, 3])
        m.bsum = sb("bsum", [P, 2, 3])
        m.wp = sb("wp", [P, D])
        m.bp = sb("bp", [P, 1])
        m.wg = sb("wg", [P, D])
        m.bg = sb("bg", [P, D])
        m.diagonal = sb("diagonal", [P, T])

        m.best2c = sb("best2c", [P, T * HEADS])
        early = ExitStack()
        m.relative = early.enter_context(nc.sbuf_tensor("m_relative", [P, CAP * PAIR + MAX_PAIRS * PAIR], F32))
        m.active = early.enter_context(nc.sbuf_tensor("m_active", [P, 4, CLASSES, T], F32))
        m.w0 = early.enter_context(nc.sbuf_tensor("m_w0", [P, 6, D], F32))
        m.wm = early.enter_context(nc.sbuf_tensor("m_wm", [P, 2, D], F32))
        stage_scan(nc, m, a)
        stage_clear(nc, m)
        stage_index(nc, m, a)
        stage_gin_pairs(nc, m, a)
        stage_gin_dense(nc, m, a)
        early.close()
        stage_norm(nc, m, a, 1)
        stage_gat_max(nc, m, a)
        stage_gat_shift(nc, m, a)
        stage_gat_pairs(nc, m, a)
        stage_gat_dense(nc, m, a)
        stage_norm(nc, m, a, 2)
        stage_signed_sums(nc, m, a)
        stage_below_sums(nc, m, a)
        stage_signed_scores(nc, m, a)
        stage_gru(nc, m, a, 0)
        stage_signed_max(nc, m, a, 1)
        stage_signed_max(nc, m, a, -1)

        def before(dve, ready):
            nc.vector.tensor_scalar(m.best2c[:], m.best2[:, 0:T, :].rearrange("p t k -> p (t k)"), -0.1 * BIG, None,
                                    ALU.max).then_inc(ready, 1)

        spread_rows(nc, m, a, "sh2", m.best2c[:], m.shift2[:, 0:T * HEADS * P], a["row_scratch"], T * HEADS, before,
                    clear=True)
        stage_signed_pairs(nc, m, a, 1)
        stage_signed_pairs(nc, m, a, -1)
        stage_gru(nc, m, a, 1)
        stage_norm(nc, m, a, 3)
        stage_select(nc, m, a)
        stage_repack(nc, m, a)
        stage_filter_pairs(nc, m, a)
        stage_output(nc, m, a)


_AS_THEY_ARE = ["x", "L0_gnn_x2", "L0_gnn_eps1", "L0_gnn_eps2", "L0_gnn_bm", "L1_gnn_W", "L1_gnn_a", "L2_gnn_gat_W",
                "L2_gnn_gat_a", "L3_gnn_W_proj", "L3_gnn_b_proj", "L3_gnn_W_gcn", "L3_gnn_b_gcn"]


def layout(inputs):
    import numpy as _np

    i = {k: _np.asarray(v) for k, v in inputs.items()}
    c = _np.ascontiguousarray
    arrays = {k: c(i[k]) for k in _AS_THEY_ARE}
    arrays["adj"] = c(i["adj"])
    arrays["adjT"] = c(i["adj"].T)
    arrays["adj_diagonal"] = c(_np.diagonal(i["adj"]).reshape(T, P).T)
    arrays["L0_WT"] = c(_np.stack([i["L0_gnn_W1"], i["L0_gnn_W2"]]).transpose(0, 1, 3, 2))
    arrays["L0_bT"] = c(_np.stack([i["L0_gnn_b1"], i["L0_gnn_b2"]]))
    arrays["L0_WmT"] = c(i["L0_gnn_Wm"].T)
    arrays["L1_WT"] = c(i["L1_gnn_W"].T)
    arrays["L2_WT"] = c(i["L2_gnn_gat_W"].transpose(0, 2, 1))
    arrays["L2_WihT"] = c(_np.stack([i["L2_gnn_edge_Wih"].T, i["L2_gnn_node_Wih"].T]))
    arrays["L2_WhhT"] = c(_np.stack([i["L2_gnn_edge_Whh"].T, i["L2_gnn_node_Whh"].T]))
    arrays["L2_bih"] = c(_np.stack([i["L2_gnn_edge_bih"], i["L2_gnn_node_bih"]]))
    arrays["L2_bhh"] = c(_np.stack([i["L2_gnn_edge_bhh"], i["L2_gnn_node_bhh"]]))
    return arrays


def kernel(**inputs):
    import concourse.bacc as _bacc
    from concourse import mybir as _mybir
    from concourse.bass_utils import run_bass_kernel_spmd as _run

    nc = _bacc.Bacc("TRN2", target_bir_lowering=False, num_devices=1)
    arrays = {f"in_{k}_dram": v for k, v in layout(inputs).items()}
    args = {k[3:-5]: nc.dram_tensor(k, v.shape, _mybir.dt.from_np(v.dtype), kind="ExternalInput").ap()
            for k, v in arrays.items()}
    args["out"] = nc.dram_tensor("out_0_dram", (N, D), F32, kind="ExternalOutput").ap()
    build(nc, args)
    r = _run(nc, [arrays], core_ids=[0])
    return r.results[0]["out_0_dram"]
```
